# Optimizing a Trainium2 kernel written in Bass

```python
import numpy as np
import jax
import jax.numpy as jnp

def _softmax(x, axis=-1):
    return jax.nn.softmax(x, axis=axis)

def _gelu(x):
    return jax.nn.gelu(x, approximate=True)

def _silu(x):
    return jax.nn.silu(x)

def _sigmoid(x):
    return jax.nn.sigmoid(x)

def _layernorm(x, axis=-1, eps=1e-05):
    m = jnp.mean(x, axis=axis, keepdims=True)
    v = jnp.var(x, axis=axis, keepdims=True)
    return (x - m) / jnp.sqrt(v + eps)

def _scatter_add(tgt, idx, src, axis=0):
    return tgt.at[idx].add(src)

def _segment_sum(src, seg, n):
    return jax.ops.segment_sum(src, seg, n)
kernel_name = 'mk_xattn_seq_d4_seqx_r8_1d9a0a'

def setup_inputs(seed: int=0):
    np.random.seed(seed)
    _w = jnp.asarray

    def _rec_inputs():
        import jax
        import jax.numpy as jnp
        _rk = jax.random.key(seed)
        x = -0.0002928 + 1 * jax.random.normal(jax.random.fold_in(_rk, 1), (16, 128, 256), jnp.float32)
        _lenS = 128 - jax.random.randint(jax.random.fold_in(_rk, 7), (16,), 0, max(1, 128 // 4) + 1, jnp.int32)
        _lenS2 = 128 - jax.random.randint(jax.random.fold_in(_rk, 8), (16,), 0, max(1, 128 // 4) + 1, jnp.int32)
        _ctx_2048P = jax.random.normal(jax.random.fold_in(_rk, 11), (16, 16, 256), jnp.float32)
        _ctx_2048c = jax.random.dirichlet(jax.random.fold_in(_rk, 511), 0.3 * jnp.ones((16,), jnp.float32), (16, 128))
        _ctx_2048t = jnp.einsum('bsk,bkd->bsd', _ctx_2048c, _ctx_2048P)
        _ctx_2048t = _ctx_2048t * jax.lax.rsqrt(jnp.mean(jnp.square(_ctx_2048t)) + 1e-12) * 0.953939
        ctx_2048 = -1.39393e-06 + 0.999914 * (_ctx_2048t + 0.3 * jax.random.normal(jax.random.fold_in(_rk, 611), (16, 128, 256), jnp.float32))
        _validS = jnp.arange(128)[None, :] < _lenS[:, None]
        _validS2 = jnp.arange(128)[None, :] < _lenS2[:, None]
        _causal = jnp.tril(jnp.ones((128, 128), dtype=bool))
        mask_1x1xSxS2_fc1 = jnp.where(jnp.broadcast_to(_validS2[0:1, None, None, :], (1, 1, 128, 128)), 1.0, 0.0).astype(jnp.float32)
        mask_Bx1xSxS2_ff1 = jnp.where(jnp.ones((16, 1, 128, 128), dtype=bool), 1.0, 0.0).astype(jnp.float32)
        return (x, ctx_2048, mask_1x1xSxS2_fc1, mask_Bx1xSxS2_ff1)
    x, ctx_2048, mask_1x1xSxS2_fc1, mask_Bx1xSxS2_ff1 = _rec_inputs()

    def _L0_xattn_setup():
        import jax, jax.numpy as jnp
        import numpy as np
        H = 256
        NH = 16
        HD = H // NH
        EPS = 1e-05

        def gelu(x):
            return 0.5 * x * (1.0 + jnp.tanh(0.7978845608028654 * x * (1.0 + 0.044715 * x * x)))

        def layernorm(x, scale, bias):
            m = jnp.mean(x, axis=-1, keepdims=True)
            v = jnp.mean(jnp.square(x - m), axis=-1, keepdims=True)
            return (x - m) * jax.lax.rsqrt(v + EPS) * scale + bias

        def split_heads(x):
            b, s, _ = x.shape
            return x.reshape(b, s, NH, HD).transpose(0, 2, 1, 3)

        def merge_heads(x):
            b, nh, s, hd = x.shape
            return x.transpose(0, 2, 1, 3).reshape(b, s, nh * hd)

        def attention(q, k, v, mask):
            scores = jnp.einsum('bhqd,bhkd->bhqk', q, k) / jnp.sqrt(jnp.float32(HD))
            scores = scores * mask - 10000.0 * (1.0 - mask)
            probs = jax.nn.softmax(scores, axis=-1)
            return jnp.einsum('bhqk,bhkd->bhqd', probs, v)
        key = jax.random.key(seed)
        ks = jax.random.split(key, 16)
        b, s, t = (2, 128, 128)
        w = lambda k, i, o: jax.random.normal(k, (i, o), jnp.float32) * 0.02
        inp = {'hidden_states': jax.random.normal(ks[0], (b, s, H), jnp.float32), 'encoder_states': jax.random.normal(ks[1], (b, t, H), jnp.float32), 'ltor_mask': jnp.tril(jnp.ones((1, 1, s, s), jnp.float32)), 'cross_mask': jnp.ones((b, 1, s, t), jnp.float32), 'ln1_s': jnp.ones((H,), jnp.float32), 'ln1_b': jnp.zeros((H,), jnp.float32), 'w_qkv': w(ks[2], H, 3 * H), 'b_qkv': jnp.zeros((3 * H,), jnp.float32), 'w_ao': w(ks[3], H, H), 'b_ao': jnp.zeros((H,), jnp.float32), 'ln2_s': jnp.ones((H,), jnp.float32), 'ln2_b': jnp.zeros((H,), jnp.float32), 'w_q': w(ks[4], H, H), 'b_q': jnp.zeros((H,), jnp.float32), 'w_kv': w(ks[5], H, 2 * H), 'b_kv': jnp.zeros((2 * H,), jnp.float32), 'w_co': w(ks[6], H, H), 'b_co': jnp.zeros((H,), jnp.float32), 'ln3_s': jnp.ones((H,), jnp.float32), 'ln3_b': jnp.zeros((H,), jnp.float32), 'w1': w(ks[7], H, 4 * H), 'b1': jnp.zeros((4 * H,), jnp.float32), 'w2': w(ks[8], 4 * H, H), 'b2': jnp.zeros((H,), jnp.float32)}
        return inp
    _L0_xattn_all = _L0_xattn_setup()
    _L0_xattn_in = {k: v for k, v in _L0_xattn_all.items() if k in ('ln1_s', 'ln1_b', 'w_qkv', 'b_qkv', 'w_ao', 'b_ao', 'ln2_s', 'ln2_b', 'w_q', 'b_q', 'w_kv', 'b_kv', 'w_co', 'b_co', 'ln3_s', 'ln3_b', 'w1', 'b1', 'w2', 'b2')}
    del _L0_xattn_all

    def _L1_xattn_setup():
        import jax, jax.numpy as jnp
        import numpy as np
        D_MODEL = 128
        N_HEAD = 16
        D_HEAD = 64
        IDX_LIST = [128, 256]
        SCALE = 1.0 / D_HEAD ** 0.5
        LN_EPS = 1e-05
        key = jax.random.key(seed)
        ks = jax.random.split(key, 9)
        s = 0.02
        B, L = (2, 256)
        return {'z1ss': jax.random.normal(ks[0], (B, D_MODEL, L), dtype=jnp.float32), 'u1ss': jax.random.normal(ks[1], (B, D_MODEL, L), dtype=jnp.float32), 'Wqkv0': jax.random.normal(ks[2], (3 * N_HEAD * D_HEAD, D_MODEL), dtype=jnp.float32) * s, 'Wqkv1': jax.random.normal(ks[3], (3 * N_HEAD * D_HEAD, D_MODEL), dtype=jnp.float32) * s, 'Winj0': jax.random.normal(ks[4], (3 * N_HEAD * D_HEAD, D_MODEL), dtype=jnp.float32) * s, 'Winj1': jax.random.normal(ks[5], (3 * N_HEAD * D_HEAD, D_MODEL), dtype=jnp.float32) * s, 'Wo': jax.random.normal(ks[6], (D_MODEL, N_HEAD * D_HEAD), dtype=jnp.float32) * s, 'bo': jax.random.normal(ks[7], (D_MODEL,), dtype=jnp.float32) * s, 'r_w_bias': jax.random.uniform(ks[8], (N_HEAD, D_HEAD), minval=-0.05, maxval=0.05, dtype=jnp.float32)}
    _L1_xattn_all = _L1_xattn_setup()
    _L1_xattn_in = {k: v for k, v in _L1_xattn_all.items() if k in ('Wqkv0', 'Wqkv1', 'Winj0', 'Winj1', 'Wo', 'bo', 'r_w_bias')}
    del _L1_xattn_all

    def _L2_xattn_setup():
        import jax, jax.numpy as jnp
        import numpy as np
        B, C1, C2, N = (8, 128, 128, 256)
        D = C2 // 8
        key = jax.random.key(seed)
        ks = jax.random.split(key, 8)
        s1 = 1.0 / np.sqrt(C1)
        s2 = 1.0 / np.sqrt(C2)
        return {'x1': jax.random.normal(ks[0], (B, C1, N), jnp.float32), 'x2': jax.random.normal(ks[1], (B, C2, N), jnp.float32), 'Wq': jax.random.uniform(ks[2], (D, C1), jnp.float32, -s1, s1), 'bq': jax.random.uniform(ks[3], (D,), jnp.float32, -s1, s1), 'Wk': jax.random.uniform(ks[4], (D, C2), jnp.float32, -s2, s2), 'bk': jax.random.uniform(ks[5], (D,), jnp.float32, -s2, s2), 'Wv': jax.random.uniform(ks[6], (C1, C2), jnp.float32, -s2, s2), 'bv': jax.random.uniform(ks[7], (C1,), jnp.float32, -s2, s2)}
    _L2_xattn_all = _L2_xattn_setup()
    _L2_xattn_in = {k: v for k, v in _L2_xattn_all.items() if k in ('Wq', 'bq', 'Wk', 'bk', 'Wv', 'bv')}
    del _L2_xattn_all

    def _L3_xattn_setup():
        import jax, jax.numpy as jnp
        import numpy as np
        B, C, CI, N = (16, 128, 64, 256)
        EPS = 1e-05

        def _conv1x1(w, b, x):
            return jnp.einsum('oc,bcn->bon', w, x) + b[None, :, None]
        key = jax.random.key(seed)
        ks = jax.random.split(key, 14)
        s = 0.02
        return {'x': jax.random.normal(ks[0], (B, C, N), jnp.float32), 'x_2': jax.random.normal(ks[1], (B, C, N), jnp.float32), 'theta_w': jax.random.normal(ks[2], (CI, C), jnp.float32) * s, 'theta_b': jax.random.normal(ks[3], (CI,), jnp.float32) * s, 'phi_w': jax.random.normal(ks[4], (CI, C), jnp.float32) * s, 'phi_b': jax.random.normal(ks[5], (CI,), jnp.float32) * s, 'g_w': jax.random.normal(ks[6], (CI, C), jnp.float32) * s, 'g_b': jax.random.normal(ks[7], (CI,), jnp.float32) * s, 'w_w': jax.random.normal(ks[8], (C, CI), jnp.float32) * s, 'w_b': jax.random.normal(ks[9], (C,), jnp.float32) * s, 'bn_gamma': jax.random.normal(ks[10], (C,), jnp.float32), 'bn_beta': jax.random.normal(ks[11], (C,), jnp.float32), 'bn_mean': jax.random.normal(ks[12], (C,), jnp.float32), 'bn_var': jax.random.uniform(ks[13], (C,), jnp.float32, 0.5, 1.5)}
    _L3_xattn_all = _L3_xattn_setup()
    _L3_xattn_in = {k: v for k, v in _L3_xattn_all.items() if k in ('theta_w', 'theta_b', 'phi_w', 'phi_b', 'g_w', 'g_b', 'w_w', 'w_b', 'bn_gamma', 'bn_beta', 'bn_mean', 'bn_var')}
    del _L3_xattn_all
    return {'x': x, 'ctx_2048': ctx_2048, 'mask_1x1xSxS2_fc1': mask_1x1xSxS2_fc1, 'mask_Bx1xSxS2_ff1': mask_Bx1xSxS2_ff1, 'L0_xattn_ln1_s': _L0_xattn_in['ln1_s'], 'L0_xattn_ln1_b': _L0_xattn_in['ln1_b'], 'L0_xattn_w_qkv': _L0_xattn_in['w_qkv'], 'L0_xattn_b_qkv': _L0_xattn_in['b_qkv'], 'L0_xattn_w_ao': _L0_xattn_in['w_ao'], 'L0_xattn_b_ao': _L0_xattn_in['b_ao'], 'L0_xattn_ln2_s': _L0_xattn_in['ln2_s'], 'L0_xattn_ln2_b': _L0_xattn_in['ln2_b'], 'L0_xattn_w_q': _L0_xattn_in['w_q'], 'L0_xattn_b_q': _L0_xattn_in['b_q'], 'L0_xattn_w_kv': _L0_xattn_in['w_kv'], 'L0_xattn_b_kv': _L0_xattn_in['b_kv'], 'L0_xattn_w_co': _L0_xattn_in['w_co'], 'L0_xattn_b_co': _L0_xattn_in['b_co'], 'L0_xattn_ln3_s': _L0_xattn_in['ln3_s'], 'L0_xattn_ln3_b': _L0_xattn_in['ln3_b'], 'L0_xattn_w1': _L0_xattn_in['w1'], 'L0_xattn_b1': _L0_xattn_in['b1'], 'L0_xattn_w2': _L0_xattn_in['w2'], 'L0_xattn_b2': _L0_xattn_in['b2'], 'L1_xattn_Wqkv0': _L1_xattn_in['Wqkv0'], 'L1_xattn_Wqkv1': _L1_xattn_in['Wqkv1'], 'L1_xattn_Winj0': _L1_xattn_in['Winj0'], 'L1_xattn_Winj1': _L1_xattn_in['Winj1'], 'L1_xattn_Wo': _L1_xattn_in['Wo'], 'L1_xattn_bo': _L1_xattn_in['bo'], 'L1_xattn_r_w_bias': _L1_xattn_in['r_w_bias'], 'L2_xattn_Wq': _L2_xattn_in['Wq'], 'L2_xattn_bq': _L2_xattn_in['bq'], 'L2_xattn_Wk': _L2_xattn_in['Wk'], 'L2_xattn_bk': _L2_xattn_in['bk'], 'L2_xattn_Wv': _L2_xattn_in['Wv'], 'L2_xattn_bv': _L2_xattn_in['bv'], 'L3_xattn_theta_w': _L3_xattn_in['theta_w'], 'L3_xattn_theta_b': _L3_xattn_in['theta_b'], 'L3_xattn_phi_w': _L3_xattn_in['phi_w'], 'L3_xattn_phi_b': _L3_xattn_in['phi_b'], 'L3_xattn_g_w': _L3_xattn_in['g_w'], 'L3_xattn_g_b': _L3_xattn_in['g_b'], 'L3_xattn_w_w': _L3_xattn_in['w_w'], 'L3_xattn_w_b': _L3_xattn_in['w_b'], 'L3_xattn_bn_gamma': _L3_xattn_in['bn_gamma'], 'L3_xattn_bn_beta': _L3_xattn_in['bn_beta'], 'L3_xattn_bn_mean': _L3_xattn_in['bn_mean'], 'L3_xattn_bn_var': _L3_xattn_in['bn_var']}

def reference(x, ctx_2048, mask_1x1xSxS2_fc1, mask_Bx1xSxS2_ff1, L0_xattn_ln1_s, L0_xattn_ln1_b, L0_xattn_w_qkv, L0_xattn_b_qkv, L0_xattn_w_ao, L0_xattn_b_ao, L0_xattn_ln2_s, L0_xattn_ln2_b, L0_xattn_w_q, L0_xattn_b_q, L0_xattn_w_kv, L0_xattn_b_kv, L0_xattn_w_co, L0_xattn_b_co, L0_xattn_ln3_s, L0_xattn_ln3_b, L0_xattn_w1, L0_xattn_b1, L0_xattn_w2, L0_xattn_b2, L1_xattn_Wqkv0, L1_xattn_Wqkv1, L1_xattn_Winj0, L1_xattn_Winj1, L1_xattn_Wo, L1_xattn_bo, L1_xattn_r_w_bias, L2_xattn_Wq, L2_xattn_bq, L2_xattn_Wk, L2_xattn_bk, L2_xattn_Wv, L2_xattn_bv, L3_xattn_theta_w, L3_xattn_theta_b, L3_xattn_phi_w, L3_xattn_phi_b, L3_xattn_g_w, L3_xattn_g_b, L3_xattn_w_w, L3_xattn_w_b, L3_xattn_bn_gamma, L3_xattn_bn_beta, L3_xattn_bn_mean, L3_xattn_bn_var):
    import jax
    import jax.numpy as jnp

    def _L0_xattn_ref(hidden_states, encoder_states, ltor_mask, cross_mask, ln1_s, ln1_b, w_qkv, b_qkv, w_ao, b_ao, ln2_s, ln2_b, w_q, b_q, w_kv, b_kv, w_co, b_co, ln3_s, ln3_b, w1, b1, w2, b2):
        import jax, jax.numpy as jnp
        import numpy as np
        H = 256
        NH = 16
        HD = H // NH
        EPS = 1e-05

        def gelu(x):
            return 0.5 * x * (1.0 + jnp.tanh(0.7978845608028654 * x * (1.0 + 0.044715 * x * x)))

        def layernorm(x, scale, bias):
            m = jnp.mean(x, axis=-1, keepdims=True)
            v = jnp.mean(jnp.square(x - m), axis=-1, keepdims=True)
            return (x - m) * jax.lax.rsqrt(v + EPS) * scale + bias

        def split_heads(x):
            b, s, _ = x.shape
            return x.reshape(b, s, NH, HD).transpose(0, 2, 1, 3)

        def merge_heads(x):
            b, nh, s, hd = x.shape
            return x.transpose(0, 2, 1, 3).reshape(b, s, nh * hd)

        def attention(q, k, v, mask):
            scores = jnp.einsum('bhqd,bhkd->bhqk', q, k) / jnp.sqrt(jnp.float32(HD))
            scores = scores * mask - 10000.0 * (1.0 - mask)
            probs = jax.nn.softmax(scores, axis=-1)
            return jnp.einsum('bhqk,bhkd->bhqd', probs, v)
        ln_out = layernorm(hidden_states, ln1_s, ln1_b)
        qkv = ln_out @ w_qkv + b_qkv
        q, k, v = jnp.split(qkv, 3, axis=-1)
        ctx = merge_heads(attention(split_heads(q), split_heads(k), split_heads(v), ltor_mask))
        attn_out = ctx @ w_ao + b_ao
        x = hidden_states + attn_out
        ln_out = layernorm(x, ln2_s, ln2_b)
        q = ln_out @ w_q + b_q
        kv = encoder_states @ w_kv + b_kv
        k, v = jnp.split(kv, 2, axis=-1)
        ctx = merge_heads(attention(split_heads(q), split_heads(k), split_heads(v), cross_mask))
        cross_out = ctx @ w_co + b_co
        x = x + cross_out
        ln_out = layernorm(x, ln3_s, ln3_b)
        mlp_out = gelu(ln_out @ w1 + b1) @ w2 + b2
        return x + mlp_out

    def _L1_xattn_ref(z1ss, u1ss, Wqkv0, Wqkv1, Winj0, Winj1, Wo, bo, r_w_bias):
        import jax, jax.numpy as jnp
        import numpy as np
        D_MODEL = 128
        N_HEAD = 16
        D_HEAD = 64
        IDX_LIST = [128, 256]
        SCALE = 1.0 / D_HEAD ** 0.5
        LN_EPS = 1e-05
        bsz, d_model, qlen = z1ss.shape
        bounds = [0] + IDX_LIST
        Wq_list, Wi_list = ([Wqkv0, Wqkv1], [Winj0, Winj1])
        chunks = []
        for i in range(len(IDX_LIST)):
            s, e = (bounds[i], bounds[i + 1])
            h = jnp.einsum('od,bdl->bol', Wq_list[i], z1ss[:, :, s:e])
            h = h + jnp.einsum('od,bdl->bol', Wi_list[i], u1ss[:, :, s:e])
            chunks.append(h)
        w_heads = jnp.concatenate(chunks, axis=2)
        q, k, v = jnp.split(w_heads, 3, axis=1)
        q = q[:, :, -qlen:]
        klen = k.shape[2]
        q = q.reshape(bsz, N_HEAD, D_HEAD, qlen)
        k = k.reshape(bsz, N_HEAD, D_HEAD, klen)
        v = v.reshape(bsz, N_HEAD, D_HEAD, klen)
        rq = q + r_w_bias[None, :, :, None]
        score = jnp.einsum('bndi,bndj->bnij', rq, k) * SCALE
        prob = jax.nn.softmax(score, axis=-1)
        attn_vec = jnp.einsum('bnij,bndj->bndi', prob, v)
        attn_vec = attn_vec.reshape(bsz, N_HEAD * D_HEAD, qlen)
        attn_out = jnp.einsum('od,bdl->bol', Wo, attn_vec) + bo[None, :, None]
        x = attn_out + z1ss
        m = jnp.mean(x, axis=1, keepdims=True)
        var = jnp.var(x, axis=1, keepdims=True)
        return (x - m) * jax.lax.rsqrt(var + LN_EPS)

    def _L2_xattn_ref(x1, x2, Wq, bq, Wk, bk, Wv, bv):
        import jax, jax.numpy as jnp
        import numpy as np
        B, C1, C2, N = (8, 128, 128, 256)
        D = C2 // 8
        q = jnp.einsum('bcn,dc->bnd', x1, Wq) + bq
        k = jnp.einsum('bcn,dc->bdn', x2, Wk) + bk[:, None]
        v = jnp.einsum('bcn,dc->bdn', x2, Wv) + bv[:, None]
        attn = jax.nn.softmax(jnp.einsum('bnd,bdm->bnm', q, k), axis=2)
        attn_out = jnp.einsum('bcm,bnm->bcn', v, attn)
        return attn_out + x1

    def _L3_xattn_ref(x, x_2, theta_w, theta_b, phi_w, phi_b, g_w, g_b, w_w, w_b, bn_gamma, bn_beta, bn_mean, bn_var):
        import jax, jax.numpy as jnp
        import numpy as np
        B, C, CI, N = (16, 128, 64, 256)
        EPS = 1e-05

        def _conv1x1(w, b, x):
            return jnp.einsum('oc,bcn->bon', w, x) + b[None, :, None]
        g_x = _conv1x1(g_w, g_b, x_2).transpose(0, 2, 1)
        theta_x = _conv1x1(theta_w, theta_b, x).transpose(0, 2, 1)
        phi_x = _conv1x1(phi_w, phi_b, x_2)
        W = jnp.einsum('bnc,bcm->bnm', theta_x, phi_x) / phi_x.shape[-1]
        y = jnp.einsum('bnm,bmc->bnc', W, g_x).transpose(0, 2, 1)
        wy = _conv1x1(w_w, w_b, y)
        inv_std = jax.lax.rsqrt(bn_var + EPS)
        wy = bn_gamma[None, :, None] * (wy - bn_mean[None, :, None]) * inv_std[None, :, None] + bn_beta[None, :, None]
        return wy + x
    x = _L0_xattn_ref(x, ctx_2048, mask_1x1xSxS2_fc1, mask_Bx1xSxS2_ff1, L0_xattn_ln1_s, L0_xattn_ln1_b, L0_xattn_w_qkv, L0_xattn_b_qkv, L0_xattn_w_ao, L0_xattn_b_ao, L0_xattn_ln2_s, L0_xattn_ln2_b, L0_xattn_w_q, L0_xattn_b_q, L0_xattn_w_kv, L0_xattn_b_kv, L0_xattn_w_co, L0_xattn_b_co, L0_xattn_ln3_s, L0_xattn_ln3_b, L0_xattn_w1, L0_xattn_b1, L0_xattn_w2, L0_xattn_b2)
    x = _L1_xattn_ref(x, ctx_2048, L1_xattn_Wqkv0, L1_xattn_Wqkv1, L1_xattn_Winj0, L1_xattn_Winj1, L1_xattn_Wo, L1_xattn_bo, L1_xattn_r_w_bias)
    x = _L2_xattn_ref(x, ctx_2048, L2_xattn_Wq, L2_xattn_bq, L2_xattn_Wk, L2_xattn_bk, L2_xattn_Wv, L2_xattn_bv)
    x = _L3_xattn_ref(x, ctx_2048, L3_xattn_theta_w, L3_xattn_theta_b, L3_xattn_phi_w, L3_xattn_phi_b, L3_xattn_g_w, L3_xattn_g_b, L3_xattn_w_w, L3_xattn_w_b, L3_xattn_bn_gamma, L3_xattn_bn_beta, L3_xattn_bn_mean, L3_xattn_bn_var)
    return x

_drawn_inputs = setup_inputs


def setup_inputs(seed=0):
    import zlib

    import numpy as np

    out = dict(_drawn_inputs(seed))
    spreads = {'L0_xattn_ln1_s': (1.0, 0.6),
     'L0_xattn_ln1_b': (0.0, 0.8),
     'L0_xattn_b_qkv': (0.0, 0.8),
     'L0_xattn_b_ao': (0.0, 0.8),
     'L0_xattn_ln2_s': (1.0, 0.6),
     'L0_xattn_ln2_b': (0.0, 0.8),
     'L0_xattn_b_q': (0.0, 0.8),
     'L0_xattn_b_kv': (0.0, 0.8),
     'L0_xattn_b_co': (0.0, 0.8),
     'L0_xattn_ln3_s': (1.0, 0.6),
     'L0_xattn_ln3_b': (0.0, 0.8),
     'L0_xattn_b1': (0.0, 0.8),
     'L0_xattn_b2': (0.0, 0.8)}
    factors = {'L0_xattn_w_qkv': 8.0,
     'L0_xattn_w_ao': 8.0,
     'L0_xattn_w_q': 8.0,
     'L0_xattn_w_kv': 8.0,
     'L0_xattn_w_co': 8.0,
     'L1_xattn_Wqkv0': 8.0,
     'L1_xattn_Wqkv1': 8.0,
     'L1_xattn_Winj0': 8.0,
     'L1_xattn_Winj1': 8.0,
     'L1_xattn_Wo': 7.454,
     'L1_xattn_bo': 39.648,
     'L1_xattn_r_w_bias': 8.0,
     'L2_xattn_bq': 4.969,
     'L2_xattn_bk': 64.0,
     'L3_xattn_theta_w': 8.0,
     'L3_xattn_theta_b': 8.0,
     'L3_xattn_phi_w': 8.0,
     'L3_xattn_phi_b': 22.152,
     'L3_xattn_g_w': 8.0,
     'L3_xattn_g_b': 8.0,
     'L3_xattn_w_w': 8.0,
     'L3_xattn_w_b': 29.704}
    for name, (base, spread) in spreads.items():
        noise = np.random.default_rng([zlib.crc32(name.encode()), seed]).standard_normal(out[name].shape)
        drawn = base * np.exp(spread * noise) if base else spread * noise
        out[name] = jnp.asarray(drawn.astype(out[name].dtype))
    for name, factor in factors.items():
        out[name] = (out[name] * factor).astype(out[name].dtype)
    return out
```

```python
from contextlib import ExitStack

import numpy as np
import concourse.bass as bass
from concourse import mybir

F32 = mybir.dt.float32
F32R = mybir.dt.float32r
ALU = mybir.AluOpType
ACT = mybir.ActivationFunctionType
AX = mybir.AxisListType

P = 128
B = 16
D = 256
G = 4
ROUNDS = B // G
TOK = G * P
EPS = 1e-5
H0, HD0 = 16, 16
QUAD = 4
UNITS0 = G * H0 // QUAD
F0 = 1024
H1, HD1 = 16, 64
PAIRS = H1 // 2
BANK = 512
RING = 3
LAG_T, LAG_V = 2, 3


class Event:

    def __init__(self, ctx, nc, name, per, unit=1):
        self.sem = ctx.enter_context(nc.semaphore(name))
        self.per, self.unit = per * unit, unit

    def at(self, i, k=0):
        return self.sem, (i + 1) * self.per + (k + 1) * self.unit


class Banks:

    def __init__(self, ctx, nc, tag, names):
        assert len(names) % 2 == 0
        self.place = {n: (k % 2, k // 2) for k, n in enumerate(names)}
        per = len(names) // 2
        self.full_ev = [Event(ctx, nc, f"{tag}_bank{j}_full", per) for j in range(2)]
        self.out_ev = [Event(ctx, nc, f"{tag}_bank{j}_read_out", per) for j in range(2)]

    def bank(self, name):
        return self.place[name][0]

    def free(self, name, i):
        j, k = self.place[name]
        return self.out_ev[j].at(i, k - 1)

    def full(self, name, i):
        j, k = self.place[name]
        return self.full_ev[j].at(i, k)

    def out(self, name, i):
        j, k = self.place[name]
        return self.out_ev[j].at(i, k)

    def fills(self, name):
        return self.full_ev[self.bank(name)].sem

    def reads(self, name):
        return self.out_ev[self.bank(name)].sem


COLS = {}
for _name, _n in (("ln_s", 6), ("ln_b", 6), ("bq0", 2), ("bk0", 2), ("bcq", 2), ("bck", 2), ("b1", 8),
                  ("bo", 1), ("rwb", 8), ("bq2", 1), ("bk2", 1), ("theta_b", 1), ("w_b", 1), ("gamma", 1),
                  ("beta", 1), ("bn_mean", 1), ("bn_var", 1)):
    _at = sum(n for _, n in COLS.values())
    COLS[_name] = (_at, _n)
NCOLS = sum(n for _, n in COLS.values())
ROWS = {n: k * D for k, n in enumerate(("bv0", "bao", "bcv", "bco", "b2", "bvpg"))}


def program(nc, x, ctx_in, ctxT, smask, cmask, cols_in, rows_in, wqkv_in, wao_in, wq_in, wkv_in, wco_in,
            w1_in, w2_in, wz_in, wi_in, wo_in, wqk2_in, wvpg_in, theta_in, ww_in, out, dbg=None, phases="ABC"):
    with ExitStack() as ctx:
        def sb(name, shape, c=ctx):
            return c.enter_context(nc.sbuf_tensor(name, shape, F32))

        psum = ctx.enter_context(nc.psum_tensor("psum", [P, 8, BANK], F32))
        score_bank = [psum[:, j, :] for j in range(3)]
        turn_bank = [psum[:, 3 + j, :] for j in range(2)]
        pv_bank = psum[:, 5, :]
        work_bank = [psum[:, 6 + j, :] for j in range(2)]

        xs = sb("xs", [P, B, D])
        ident = sb("ident", [P, P])
        mean_w = sb("mean_w", [P, P])
        cols = sb("cols", [P, NCOLS])
        half_neg = sb("half_neg", [P, 4])

        def col(name, k=0, n=1, p=P):
            at = COLS[name][0] + k
            return cols[0:p, at:at + n]

        if "A" in phases:
            layer0(nc, locals())
        if "B" in phases:
            layer1(nc, locals())
        if "C" in phases:
            layers23(nc, locals())
        if dbg is not None:
            s_dbg = ctx.enter_context(nc.semaphore("s_dbg"))
            block = nc.Block()
            with block:
                @block.sync
                def _(sp):
                    sp.dma_start(dbg.rearrange("b p d -> p b d"), xs[:, :, :]).then_inc(s_dbg, 16)
                    sp.wait_ge(s_dbg, 16)


def layer0(nc, v):
    (sb_, psum, score_bank, turn_bank, pv_bank, work_bank, xs, ident, mean_w, cols, half_neg, col) = (
        v[n] for n in ("sb", "psum", "score_bank", "turn_bank", "pv_bank", "work_bank", "xs", "ident", "mean_w",
                       "cols", "half_neg", "col"))
    with ExitStack() as ctx:
        def sb(name, shape):
            return sb_(name, shape, ctx)

        def sem(name):
            return ctx.enter_context(nc.semaphore(name))

        def event(name, per, unit=1):
            e = Event(ctx, nc, name, per, unit)
            events.append(e)
            return e

        rows = sb("rows", [P, len(ROWS) * D])
        ring_e = sb("ring_e", [P, RING, BANK])
        ring_t = sb("ring_t", [P, RING, BANK])
        neg_max = sb("neg_max", [P, RING, QUAD])
        z_sum = sb("z_sum", [P, RING, QUAD])
        z_inv = sb("z_inv", [P, RING, QUAD])

        def row(name):
            return rows[:, ROWS[name]:ROWS[name] + D]

        VSTEP = P + HD0
        wqkv = sb("wqkv", [P, 2, 3 * D])
        wao = sb("wao", [P, 2, D])
        wq = sb("wq", [P, 2, D])
        wkv = sb("wkv", [P, 2, 2 * D])
        wco = sb("wco", [P, 2, D])
        w1 = sb("w1", [P, 2, F0])
        w2 = sb("w2", [P, F0 // P, D])
        xg = sb("xg", [P, G, D])
        xr = sb("xr", [P, G, D])
        ln = sb("ln", [P, G, D])
        lnT = sb("lnT", [P, 2, TOK])
        shared = sb("shared", [P, 4, 2 * TOK])
        qT, kT, oT, cT = (shared[:, j, :].rearrange("p (c t) -> p c t", c=2) for j in range(4))
        hid = shared[:, :, :].rearrange("p a (c t) -> p (a c) t", c=2)
        km = sb("km", [P, RING, BANK])
        vm = sb("vm", [P, G, 2, 8 * VSTEP])
        self_mul = sb("self_mul", [P, P])
        self_add = sb("self_add", [P, P])
        cross_mul = sb("cross_mul", [P, G, P])
        cross_add = sb("cross_add", [P, G, P])
        stats = sb("stats", [P, G, 6])
        mean_var = sb("mean_var", [P, G, 2])
        var_eps = sb("var_eps", [P, G])
        eps = sb("eps", [P, G])
        first_stat = sb("first_stat", [P, 1])
        rstd = sb("rstd", [P, G])
        head_rows = sb("head_rows", [P, 8])
        bq_scaled = sb("bq_scaled", [P, 4])

        events = []
        names = (["T0h0", "T0h1", "q0", "q1", "k0", "k1"] + [f"v{b}" for b in range(G)] + [f"o{b}" for b in range(G)]
                 + ["ck0", "ck1"] + [f"cv{b}" for b in range(G)] + ["T1h0", "T1h1", "cq0", "cq1"]
                 + [f"co{b}" for b in range(G)] + ["T2h0", "T2h1"] + [f"f{f}" for f in range(8)]
                 + [f"y{b}" for b in range(G)])
        work = Banks(ctx, nc, "work", names)
        events += work.full_ev + work.out_ev
        N_U = 2 * UNITS0
        input_in = event("input_in", 1, 16)
        cross_mask_in = event("cross_mask_in", 1, 16)
        ctxT_in = event("ctxT_in", 1, 16)
        stats_done = event("stats_done", 3)
        mean_var_done = event("mean_var_done", 3)
        var_eps_done = event("var_eps_done", 3)
        rstd_done = event("rstd_done", 3)
        ln_done = event("ln_done", 3)
        residual_biased = event("residual_biased", 3)
        keys_masked = event("keys_masked", N_U)
        scores_done = event("scores_done", N_U)
        scores_mul = event("scores_mul", N_U)
        scores_add = event("scores_add", N_U)
        max_done = event("max_done", N_U)
        exp_done = event("exp_done", N_U)
        z_inv_done = event("z_inv_done", N_U)
        probs_done = event("probs_done", N_U)
        turned = event("turned", N_U)
        probsT_done = event("probsT_done", N_U)
        pv_done = event("pv_done", N_U)
        heads_out = event("heads_out", N_U // 2)
        cross_add_made = event("cross_add_made", 1)
        h_lin = event("h_lin", 8)
        h_poly = event("h_poly", 8)
        h_arg = event("h_arg", 8)
        h_tanh = event("h_tanh", 8)
        h_gate = event("h_gate", 8)

        weights_in = [sem(f"weights_in_{n}") for n in ("consts", "qkv", "ao", "kv", "q", "co", "1", "2", "mask")]
        w_consts, w_qkv, w_ao, w_kv, w_q, w_co, w_1, w_2, w_mask = weights_in
        consts_made = sem("consts_made")
        head_rows_made = sem("head_rows_made")
        dve_consts = sem("dve_consts")
        ident_step = sem("ident_step")

        block = ctx.enter_context(nc.Block())

        @block.sync
        def _(sp):
            for e in events:
                sp.nop().then_inc(e.sem, e.per)

            def load_round(i):
                sp.dma_start(xg[:, :, :], v["x"].rearrange("b s d -> s b d")[:, bass.ds(i * G, G), :])\
                    .then_inc(input_in.sem, 16)

            def load_cross(i):
                sp.dma_start(cT, v["ctxT"].rearrange("(c p) t -> p c t", c=2)[:, :, bass.ds(i * TOK, TOK)])\
                    .then_inc(ctxT_in.sem, 16)
                sp.dma_start(cross_mul[:, :, :], v["cmask"].rearrange("b q k -> q b k")[:, bass.ds(i * G, G), :])\
                    .then_inc(cross_mask_in.sem, 16)

            load_round(0)
            sp.dma_start(cols[:, :], v["cols_in"]).then_inc(w_consts, 16)
            sp.dma_start(rows[:, :], v["rows_in"].partition_broadcast(P)).then_inc(w_consts, 16)
            sp.dma_start(wqkv[:, :, :], v["wqkv_in"].rearrange("(c p) n -> p c n", p=P)).then_inc(w_qkv, 16)
            sp.dma_start(self_mul[:, :], v["smask"]).then_inc(w_mask, 16)
            sp.dma_start(wao[:, :, :], v["wao_in"].rearrange("(c p) n -> p c n", p=P)).then_inc(w_ao, 16)
            load_cross(0)
            for w, src, s in ((wkv, "wkv_in", w_kv), (wq, "wq_in", w_q), (wco, "wco_in", w_co), (w1, "w1_in", w_1),
                              (w2, "w2_in", w_2)):
                sp.dma_start(w[:, :, :], v[src].rearrange("(c p) n -> p c n", p=P)).then_inc(s, 16)
            with sp.Fori(1, ROUNDS) as i:
                sp.wait_ge(*ln_done.at(i - 1, 0))
                sp.wait_ge(*residual_biased.at(i - 1, 0))
                load_round(i)
                sp.wait_ge(*work.out("y3", i - 1))
                sp.wait_ge(*scores_mul.at(i - 1, N_U - 1))
                load_cross(i)
            sp.wait_ge(w_mask, 16)

        @block.gpsimd
        def _(pool):
            pool.memset(ident[:, :], 0.0).then_inc(ident_step, 1)
            pool.memset(head_rows[:, :], 1.0).then_inc(ident_step, 1)
            pool.wait_ge(ident_step, 2)
            pool.affine_select(out=ident[:, :], in_=ident[:, :], compare_op=ALU.not_equal, fill=1.0, base=0,
                               pattern=[[-1, P]], channel_multiplier=1).then_inc(consts_made, 1)
            pool.affine_select(out=head_rows[:, :], in_=head_rows[:, :], compare_op=ALU.is_ge, fill=0.0, base=0,
                               pattern=[[-HD0, 8]], channel_multiplier=1).then_inc(ident_step, 1)
            pool.wait_ge(ident_step, 3)
            pool.affine_select(out=head_rows[:, :], in_=head_rows[:, :], compare_op=ALU.is_ge, fill=0.0,
                               base=HD0 - 1, pattern=[[HD0, 8]], channel_multiplier=-1).then_inc(head_rows_made, 1)
            pool.memset(half_neg[:, :], -0.5).then_inc(head_rows_made, 1)
            pool.memset(mean_w[:, :], 1.0 / P)
            pool.memset(eps[:, :], EPS).then_inc(head_rows_made, 1)
            pool.wait_ge(head_rows_made, 3)
            pool.wait_ge(w_consts, 32)

            def inverse_std(i, k):
                pool.wait_ge(*mean_var_done.at(i, k))
                pool.wait_ge(*rstd_done.at(i, k - 1))
                pool.tensor_tensor(var_eps[:, :], mean_var[:, :, 1], eps[:, :], ALU.add).then_inc(var_eps_done.sem, 1)
                pool.wait_ge(*var_eps_done.at(i, k))
                pool.tensor_tensor(rstd[:, :], var_eps[:, :], half_neg[:, 0:G], ALU.pow).then_inc(rstd_done.sem, 1)

            def add_bias(i, k, src, bias):
                pool.wait_ge(*ln_done.at(i, k))
                pool.tensor_tensor(xr[:, :, :], src[:, :, :], row(bias).unsqueeze(1).broadcast_to([P, G, D]),
                                   ALU.add).then_inc(residual_biased.sem, 1)

            def mask_keys(i, a):
                for u in range(UNITS0):
                    b, quad = divmod(u, QUAD)
                    half, q = divmod(quad, 2)
                    n = a * UNITS0 + u
                    if u == 0 or quad == 2:
                        pool.wait_ge(*work.out(("k", "ck")[a] + str(half), i))
                    pool.wait_ge(*scores_done.at(i, n - RING))
                    pool.tensor_tensor(
                        km[:, n % RING, :].rearrange("p (h k) -> p h k", h=QUAD),
                        kT[:, half, b * P:(b + 1) * P].unsqueeze(1).broadcast_to([P, QUAD, P]),
                        head_rows[:, QUAD * q:QUAD * q + QUAD].unsqueeze(2).broadcast_to([P, QUAD, P]),
                        ALU.mult).then_inc(keys_masked.sem, 1)

            with pool.Fori(0, ROUNDS) as i:
                inverse_std(i, 0)
                pool.wait_ge(*work.out("y3", i - 1))
                add_bias(i, 0, xg, "bao")
                mask_keys(i, 0)
                inverse_std(i, 1)
                add_bias(i, 1, xr, "bco")
                mask_keys(i, 1)
                inverse_std(i, 2)
                add_bias(i, 2, xr, "b2")

        @block.tensor
        def _(pe):
            def norm_turn(i, k):
                pe.wait_ge(*ln_done.at(i, k))
                for c in range(2):
                    name = f"T{k}h{c}"
                    pe.wait_ge(*work.free(name, i))
                    ps = work_bank[work.bank(name)]
                    for b in range(G):
                        last = nc.tensor.transpose(ps[:, b * P:(b + 1) * P], ln[:, b, c * P:(c + 1) * P], ident[:, :])
                    last.then_inc(work.fills(name), 1)

            def features_out(i, prefix, w, at, src):
                for m in range(2):
                    name = f"{prefix}{m}"
                    pe.wait_ge(*work.free(name, i))
                    for c in range(2):
                        last = nc.tensor.matmul(work_bank[work.bank(name)], w[:, c, at + m * P:at + (m + 1) * P],
                                                src[:, c, :], start=c == 0, stop=c == 1)
                    last.then_inc(work.fills(name), 1)

            def tokens_out(i, prefix, w, at, src, chunks):
                for b in range(G):
                    name = f"{prefix}{b}"
                    pe.wait_ge(*work.free(name, i))
                    for c in range(chunks):
                        last = nc.tensor.matmul(work_bank[work.bank(name)][:, 0:D], src[:, c, b * P:(b + 1) * P],
                                                w[:, c, at:at + D], start=c == 0, stop=c == chunks - 1)
                    last.then_inc(work.fills(name), 1)

            def attend(i, a):
                for t in range(UNITS0 + LAG_V):
                    if t < UNITS0:
                        b, quad = divmod(t, QUAD)
                        n = a * UNITS0 + t
                        pe.wait_ge(*keys_masked.at(i, n))
                        pe.wait_ge(*scores_mul.at(i, n - RING))
                        nc.tensor.matmul(score_bank[n % RING], qT[:, quad // 2, b * P:(b + 1) * P],
                                         km[:, n % RING, :], start=True, stop=True).then_inc(scores_done.sem, 1)
                    if LAG_T <= t < UNITS0 + LAG_T:
                        n = a * UNITS0 + t - LAG_T
                        pe.wait_ge(*probs_done.at(i, n))
                        pe.wait_ge(*probsT_done.at(i, n - 2))
                        for h in range(QUAD):
                            last = nc.tensor.transpose(turn_bank[n % 2][:, h * P:(h + 1) * P],
                                                       ring_e[:, n % RING, h * P:(h + 1) * P], ident[:, :])
                        last.then_inc(turned.sem, 1)
                    if t >= LAG_V:
                        u = t - LAG_V
                        b, quad = divmod(u, QUAD)
                        half, q = divmod(quad, 2)
                        n = a * UNITS0 + u
                        pe.wait_ge(*probsT_done.at(i, n))
                        if q == 0:
                            pe.wait_ge(*work.out(("v", "cv")[a] + str(b), i))
                            pe.wait_ge(*heads_out.at(i, n // 2 - 1))
                        for h in range(QUAD):
                            j = QUAD * q + h
                            last = nc.tensor.matmul(pv_bank[:, 0:P], vm[:, b, half, j * P:(j + 1) * P],
                                                    ring_t[:, n % RING, h * P:(h + 1) * P],
                                                    start=j == 0, stop=j == 7)
                        last.then_inc(pv_done.sem, 1)

            pe.wait_ge(consts_made, 1)
            pe.wait_ge(w_qkv, 16)
            pe.wait_ge(w_ao, 16)
            pe.wait_ge(w_kv, 16)
            pe.wait_ge(w_q, 16)
            pe.wait_ge(w_co, 16)
            pe.wait_ge(w_1, 16)
            pe.wait_ge(w_2, 16)
            with pe.Fori(0, ROUNDS) as i:
                norm_turn(i, 0)
                pe.wait_ge(*work.out("T0h0", i))
                pe.wait_ge(*work.out("T0h1", i))
                features_out(i, "q", wqkv, 0, lnT)
                features_out(i, "k", wqkv, D, lnT)
                tokens_out(i, "v", wqkv, 2 * D, lnT, 2)
                pe.wait_ge(*work.out("q0", i))
                pe.wait_ge(*work.out("q1", i))
                attend(i, 0)
                pe.wait_ge(*heads_out.at(i, UNITS0 // 2 - 1))
                tokens_out(i, "o", wao, 0, oT, 2)
                pe.wait_ge(*ctxT_in.at(i))
                features_out(i, "ck", wkv, 0, cT)
                tokens_out(i, "cv", wkv, D, cT, 2)
                norm_turn(i, 1)
                pe.wait_ge(*work.out("T1h0", i))
                pe.wait_ge(*work.out("T1h1", i))
                features_out(i, "cq", wq, 0, lnT)
                pe.wait_ge(*work.out("cq0", i))
                pe.wait_ge(*work.out("cq1", i))
                attend(i, 1)
                pe.wait_ge(*heads_out.at(i, UNITS0 - 1))
                tokens_out(i, "co", wco, 0, oT, 2)
                norm_turn(i, 2)
                pe.wait_ge(*work.out("T2h0", i))
                pe.wait_ge(*work.out("T2h1", i))
                for f in range(8):
                    name = f"f{f}"
                    pe.wait_ge(*work.free(name, i))
                    for c in range(2):
                        last = nc.tensor.matmul(work_bank[work.bank(name)], w1[:, c, f * P:(f + 1) * P],
                                                lnT[:, c, :], start=c == 0, stop=c == 1)
                    last.then_inc(work.fills(name), 1)
                pe.wait_ge(*h_gate.at(i, 7))
                tokens_out(i, "y", w2, 0, hid, 8)

        @block.scalar
        def _(act):
            def norm_affine(i, k):
                for c in range(2):
                    name = f"T{k}h{c}"
                    act.wait_ge(*work.full(name, i))
                    nc.scalar.activation(lnT[:, c, :], work_bank[work.bank(name)], ACT.Identity,
                                         bias=col("ln_b", 2 * k + c), scale=col("ln_s", 2 * k + c))\
                        .then_inc(work.reads(name), 1)

            def biased(i, prefix, dst, bias, scale=1.0):
                for m in range(2):
                    name = f"{prefix}{m}"
                    act.wait_ge(*work.full(name, i))
                    nc.scalar.activation(dst[:, m, :], work_bank[work.bank(name)], ACT.Identity,
                                         bias=bias(m), scale=scale).then_inc(work.reads(name), 1)

            def attend(i, a):
                for t in range(UNITS0 + LAG_V):
                    if t < UNITS0:
                        n = a * UNITS0 + t
                        act.wait_ge(*max_done.at(i, n))
                        act.wait_ge(*z_inv_done.at(i, n - RING))
                        for h in range(QUAD):
                            e = ring_e[:, n % RING, h * P:(h + 1) * P]
                            last = nc.scalar.activation(e, e, ACT.Exp, bias=neg_max[:, n % RING, h:h + 1],
                                                        accum_out=z_sum[:, n % RING, h:h + 1])
                        last.then_inc(exp_done.sem, 1)
                    if LAG_T <= t < UNITS0 + LAG_T:
                        n = a * UNITS0 + t - LAG_T
                        act.wait_ge(*turned.at(i, n))
                        act.wait_ge(*pv_done.at(i, n - RING))
                        nc.scalar.copy(ring_t[:, n % RING, :], turn_bank[n % 2]).then_inc(probsT_done.sem, 1)
                    if t >= LAG_V and (t - LAG_V) % 2 == 1:
                        u = t - LAG_V
                        b, quad = divmod(u, QUAD)
                        act.wait_ge(*pv_done.at(i, a * UNITS0 + u))
                        nc.scalar.copy(oT[:, quad // 2, b * P:(b + 1) * P], pv_bank[:, 0:P])\
                            .then_inc(heads_out.sem, 1)

            act.wait_ge(w_consts, 32)
            act.wait_ge(dve_consts, 1)
            with act.Fori(0, ROUNDS) as i:
                norm_affine(i, 0)
                biased(i, "q", qT, lambda m: bq_scaled[:, m:m + 1], HD0 ** -0.5)
                biased(i, "k", kT, lambda m: col("bk0", m))
                attend(i, 0)
                biased(i, "ck", kT, lambda m: col("bck", m))
                norm_affine(i, 1)
                biased(i, "cq", qT, lambda m: bq_scaled[:, 2 + m:3 + m], HD0 ** -0.5)
                attend(i, 1)
                norm_affine(i, 2)
                for f in range(9):
                    if f < 8:
                        name = f"f{f}"
                        ps = work_bank[work.bank(name)]
                        act.wait_ge(*work.full(name, i))
                        act.wait_ge(*h_gate.at(i, f - 2))
                        nc.scalar.activation(ring_e[:, f % 2, :], ps, ACT.Identity, bias=col("b1", f))\
                            .then_inc(h_lin.sem, 1)
                        nc.scalar.activation(ring_t[:, f % 2, :], ps, ACT.Square, bias=col("b1", f))\
                            .then_inc(work.reads(name), 1)
                    if f >= 1:
                        act.wait_ge(*h_arg.at(i, f - 1))
                        t = ring_t[:, (f - 1) % 2, :]
                        nc.scalar.activation(t, t, ACT.Tanh, scale=0.7978845608028654).then_inc(h_tanh.sem, 1)

        @block.vector
        def _(dve):
            def normalise(i, k, src):
                for b in range(G):
                    last = nc.vector.bn_stats(stats[:, b, :], src[:, b, :])
                last.then_inc(stats_done.sem, 1)
                dve.wait_ge(*stats_done.at(i, k))
                nc.vector.tensor_copy(first_stat[:, :], stats[:, 0, 0:1])
                for b in range(G):
                    last = nc.vector.bn_aggr(mean_var[:, b, :], stats[:, b, :])
                last.then_inc(mean_var_done.sem, 1)
                dve.wait_ge(*rstd_done.at(i, k))
                for b in range(G):
                    last = nc.vector.tensor_scalar(ln[:, b, :], src[:, b, :], mean_var[:, b, 0:1], rstd[:, b:b + 1],
                                                   ALU.subtract, ALU.mult)
                last.then_inc(ln_done.sem, 1)

            def spread_values(i, prefix, bias):
                for b in range(G):
                    name = f"{prefix}{b}"
                    dve.wait_ge(*work.full(name, i))
                    dst = vm[:, b, :, :].rearrange("p c (j w) -> p c j w", w=VSTEP)[:, :, :, 0:HD0]
                    nc.vector.tensor_tensor(
                        dst, work_bank[work.bank(name)][:, 0:D].rearrange("p (c j w) -> p c j w", c=2, w=HD0),
                        row(bias).rearrange("p (c j w) -> p c j w", c=2, w=HD0), ALU.add)\
                        .then_inc(work.reads(name), 1)

            def attend(i, a):
                mul = (self_mul[:, :].unsqueeze(1).broadcast_to([P, QUAD, P]),)
                add = (self_add[:, :].unsqueeze(1).broadcast_to([P, QUAD, P]),)
                if a == 1:
                    mul = [cross_mul[:, b, :].unsqueeze(1).broadcast_to([P, QUAD, P]) for b in range(G)]
                    add = [cross_add[:, b, :].unsqueeze(1).broadcast_to([P, QUAD, P]) for b in range(G)]
                for t in range(UNITS0 + 1):
                    if t < UNITS0:
                        n = a * UNITS0 + t
                        b = t // QUAD
                        e = ring_e[:, n % RING, :].rearrange("p (h k) -> p h k", h=QUAD)
                        dve.wait_ge(*scores_done.at(i, n))
                        dve.wait_ge(*turned.at(i, n - RING))
                        nc.vector.tensor_tensor(e, score_bank[n % RING].rearrange("p (h k) -> p h k", h=QUAD),
                                                mul[b % len(mul)], ALU.mult).then_inc(scores_mul.sem, 1)
                    if t >= 1:
                        m = a * UNITS0 + t - 1
                        dve.wait_ge(*exp_done.at(i, m))
                        nc.vector.reciprocal(z_inv[:, m % RING, :], z_sum[:, m % RING, :]).then_inc(z_inv_done.sem, 1)
                    if t < UNITS0:
                        dve.wait_ge(*scores_mul.at(i, n))
                        nc.vector.tensor_tensor(e, e, add[b % len(add)], ALU.add).then_inc(scores_add.sem, 1)
                    if t >= 1:
                        dve.wait_ge(*z_inv_done.at(i, m))
                        p = ring_e[:, m % RING, :].rearrange("p (h k) -> p h k", h=QUAD)
                        nc.vector.tensor_tensor(p, p, z_inv[:, m % RING, :].unsqueeze(2).broadcast_to([P, QUAD, P]),
                                                ALU.mult).then_inc(probs_done.sem, 1)
                    if t < UNITS0:
                        dve.wait_ge(*scores_add.at(i, n))
                        nc.vector.tensor_reduce(neg_max[:, n % RING, :], e, AX.X, ALU.max, negate=True)\
                            .then_inc(max_done.sem, 1)

            def add_product(i, prefix):
                for b in range(G):
                    name = f"{prefix}{b}"
                    dve.wait_ge(*work.full(name, i))
                    nc.vector.tensor_tensor(xr[:, b, :], work_bank[work.bank(name)][:, 0:D], xr[:, b, :], ALU.add)\
                        .then_inc(work.reads(name), 1)

            dve.memset(vm[:, :, :, :], 0.0)
            dve.wait_ge(w_mask, 16)
            nc.vector.tensor_scalar(self_add[:, :], self_mul[:, :], -1.0, 10000.0, ALU.add, ALU.mult)
            dve.wait_ge(w_consts, 32)
            nc.vector.tensor_scalar(bq_scaled[:, 0:2], col("bq0", 0, 2), HD0 ** -0.5, None, ALU.mult)
            nc.vector.tensor_scalar(bq_scaled[:, 2:4], col("bcq", 0, 2), HD0 ** -0.5, None, ALU.mult)\
                .then_inc(dve_consts, 1)
            dve.wait_ge(dve_consts, 1)
            with dve.Fori(0, ROUNDS) as i:
                dve.wait_ge(*input_in.at(i))
                normalise(i, 0, xg)
                spread_values(i, "v", "bv0")
                attend(i, 0)
                dve.wait_ge(*cross_mask_in.at(i))
                nc.vector.tensor_scalar(cross_add[:, :, :], cross_mul[:, :, :], -1.0, 10000.0, ALU.add, ALU.mult)\
                    .then_inc(cross_add_made.sem, 1)
                dve.wait_ge(*residual_biased.at(i, 0))
                add_product(i, "o")
                dve.wait_ge(*work.out("o2", i))
                dve.wait_ge(*work.out("o3", i))
                normalise(i, 1, xr)
                spread_values(i, "cv", "bcv")
                dve.wait_ge(*cross_add_made.at(i))
                attend(i, 1)
                dve.wait_ge(*residual_biased.at(i, 1))
                add_product(i, "co")
                dve.wait_ge(*work.out("co2", i))
                dve.wait_ge(*work.out("co3", i))
                normalise(i, 2, xr)
                for f in range(9):
                    if f < 8:
                        t, h = ring_t[:, f % 2, :], ring_e[:, f % 2, :]
                        dve.wait_ge(*work.out(f"f{f}", i))
                        nc.vector.tensor_scalar(t, t, 0.044715, 1.0, ALU.mult, ALU.add).then_inc(h_poly.sem, 1)
                        dve.wait_ge(*h_poly.at(i, f))
                        nc.vector.tensor_tensor(t, t, h, ALU.mult).then_inc(h_arg.sem, 1)
                    if f >= 1:
                        g = f - 1
                        dve.wait_ge(*h_tanh.at(i, g))
                        nc.vector.scalar_tensor_tensor(out=hid[:, g, :], in0=ring_t[:, g % 2, :], scalar=1.0,
                                                       in1=ring_e[:, g % 2, :], op0=ALU.add, op1=ALU.mult)\
                            .then_inc(h_gate.sem, 1)
                dve.wait_ge(*residual_biased.at(i, 2))
                for b in range(G):
                    name = f"y{b}"
                    dve.wait_ge(*work.full(name, i))
                    nc.vector.scalar_tensor_tensor(out=xs[:, bass.ds(i * G + b, 1), :].rearrange("p a d -> p (a d)"),
                                                   in0=work_bank[work.bank(name)][:, 0:D], scalar=0.5,
                                                   in1=xr[:, b, :], op0=ALU.mult, op1=ALU.add)\
                        .then_inc(work.reads(name), 1)


def layer1(nc, v):
    (sb_, psum, xs, ident, mean_w, half_neg, col) = (v[n] for n in (
        "sb", "psum", "xs", "ident", "mean_w", "half_neg", "col"))
    NB = 2
    R1 = B // NB
    UNITS = H1 * NB
    NQ = H1 * HD1
    RE, RT = 4, 2
    L_T, L_V, L_O = 2, 3, 4
    SCALE = HD1 ** -0.5
    with ExitStack() as ctx:
        def sb(name, shape, dt=F32):
            return ctx.enter_context(nc.sbuf_tensor(name, shape, dt))

        def sem(name):
            return ctx.enter_context(nc.semaphore(name))

        events = []

        def event(name, per, unit=1):
            e = Event(ctx, nc, "l1_" + name, per, unit)
            events.append(e)
            return e

        wz = [sb(f"wz{p}", [P, 2, 3 * NQ], F32R) for p in ("h", "l")]
        wi = [sb(f"wi{p}", [P, 2, 3 * NQ], F32R) for p in ("h", "l")]
        wo = [sb(f"wo{p}", [P, H1, P], F32R) for p in ("h", "l")]
        zu = [sb(f"zu{p}", [P, 2, 2, NB, P], F32R) for p in ("h", "l")]
        q = [sb(f"q{p}", [P, 2, 2, 2, NB, P], F32R) for p in ("h", "l")]
        k = [sb(f"k{p}", [P, 2, 2, NB, P], F32R) for p in ("h", "l")]
        vs = sb("vs", [P, 2, NB, 2, 4, 2, HD1], F32R)
        STAGE = 3 * NQ // 2
        plain = sb("plain", [P, RE * BANK + 3 * NB * D])
        stage = plain[:, 0:2 * STAGE].rearrange("p (s n) -> p s n", s=2)
        prob = plain[:, 0:RE * BANK].rearrange("p (s n) -> p s n", s=RE)
        ub, y, ysq = (plain[:, RE * BANK + j * NB * D:RE * BANK + (j + 1) * NB * D].rearrange(
            "p (b d) -> p b d", b=NB) for j in range(3))
        pT = [sb(f"pT{p}", [P, RT, BANK], F32R) for p in ("h", "l")]
        aT = [sb(f"aT{p}", [P, RT, D], F32R) for p in ("h", "l")]
        neg_max = sb("l1_neg_max", [P, RE, 2])
        z_sum = sb("l1_z_sum", [P, RE, 2])
        z_inv = sb("l1_z_inv", [P, RE, 2])
        var_eps = sb("l1_var_eps", [P, 4])
        rstd = sb("l1_rstd", [P, 4])
        diag = ysq.rearrange("p b (h c) -> p (b h) c", h=2)

        score_bank = [psum[:, j, :] for j in range(2)]
        turn_bank = psum[:, 2, :]
        pv_bank = psum[:, 3, :]
        work_bank = [psum[:, 4 + j, :] for j in range(2)]
        wo_bank = [psum[:, 6 + j, :] for j in range(NB)]

        with ExitStack() as c2:
            staged = c2.enter_context(nc.semaphore("weights_staged"))
            staged1 = c2.enter_context(nc.semaphore("weights_staged_odd"))
            hi_made = c2.enter_context(nc.semaphore("weights_hi_made"))
            lo_made = c2.enter_context(nc.semaphore("weights_lo_made"))
            chunks = [(src, pair, c, h) for src, pair in (("wz_in", wz), ("wi_in", wi)) for c in range(2)
                      for h in range(2)]
            landed = [staged, staged1]

            def views(n):
                src, pair, c, h = chunks[n]
                return [w[:, c, h * STAGE:(h + 1) * STAGE] for w in pair]

            block = c2.enter_context(nc.Block())

            @block.sync
            def _(sp):
                for n, (src, pair, c, h) in enumerate(chunks):
                    if n >= 2:
                        sp.wait_ge(lo_made, n - 1)
                    sp.dma_start(stage[:, n % 2, :], v[src].rearrange("(c p) n -> p c n", p=P)[
                        :, c, h * STAGE:(h + 1) * STAGE]).then_inc(landed[n % 2], 16)
                for g in range(2):
                    n = len(chunks) + g
                    sp.wait_ge(lo_made, n - 1)
                    src = v["wo_in"].rearrange("(h r) o -> r h o", r=HD1)[:, g * 8:(g + 1) * 8, :]
                    for half in range(2):
                        sp.dma_start(stage[half * HD1:(half + 1) * HD1, n % 2, 0:8 * P].rearrange(
                            "p (h o) -> p h o", h=8), src).then_inc(landed[n % 2], 16)

            def arrived(n):
                done = n // 2 + 1
                return landed[n % 2], 16 * (done if n < len(chunks) else done + 1)

            def parts(n):
                if n < len(chunks):
                    return stage[:, n % 2, :], *views(n)
                g = n - len(chunks)
                return (stage[:, n % 2, 0:8 * P], *(w[:, g * 8:(g + 1) * 8, :].rearrange("p h o -> p (h o)")
                                                    for w in wo))

            @block.scalar
            def _(act):
                for n in range(len(chunks) + 2):
                    src, hi, lo = parts(n)
                    act.wait_ge(*arrived(n))
                    nc.scalar.copy(hi, src).then_inc(hi_made, 1)

            @block.vector
            def _(dve):
                for n in range(len(chunks) + 2):
                    src, hi, lo = parts(n)
                    dve.wait_ge(hi_made, n + 1)
                    nc.vector.tensor_tensor(lo, src, hi.bitcast(F32), ALU.subtract).then_inc(lo_made, 1)

        names = ["q0", "k0", "v0b0", "v0b1", "q1", "k1", "q2", "k2", "v1b0", "v1b1", "q3", "k3", "mean", "var",
                 "q4", "k4", "v2b0", "v2b1", "q5", "k5", "inv0", "inv1", "q6", "k6", "v3b0", "v3b1",
                 "q7", "k7"]
        made = [n for n in names if n[0] in "qkv" and n != "var"]
        work = Banks(ctx, nc, "l1_work", names)
        events += work.full_ev + work.out_ev
        work_hi = event("work_hi", len(made))
        u_in = event("u_in", 1, 16)
        zu_hi = event("zu_hi", 2)
        zu_lo = event("zu_lo", 2)
        scores_done = event("scores_done", UNITS)
        max_done = event("max_done", UNITS)
        exp_done = event("exp_done", UNITS)
        z_inv_done = event("z_inv_done", UNITS)
        probs_done = event("probs_done", UNITS)
        turned = event("turned", UNITS)
        pT_hi = event("pT_hi", UNITS)
        pT_lo = event("pT_lo", UNITS)
        pv_done = event("pv_done", UNITS)
        aT_hi = event("aT_hi", UNITS)
        aT_lo = event("aT_lo", UNITS)
        wo_done = event("wo_done", UNITS)
        y_done = event("y_done", 1)
        centred = event("centred", 1)
        squared = event("squared", 1)
        rstd_done = event("rstd_done", 1)
        diagonal = event("diagonal", 1)
        zeroed = sem("l1_zeroed")

        def unit(n):
            n %= UNITS
            return n // 4, n % 4 // 2, n % 2

        def work_at(t):
            s, r = divmod(t, 4)
            nxt = (s + 1) % 8
            if r < 2:
                return "qk"[r] + str(nxt), int(s == 7)
            return (f"v{nxt // 2}b{r - 2}", int(s == 7)) if s % 2 == 1 else (None, 0)

        T_Y, T_MEAN, T_VAR, T_INV, T_ZU = 4, 10, 11, 18, 25

        def tile_of(name):
            slot = int(name[1]) % 2
            if name[0] == "q":
                return [[(w[h * HD1:(h + 1) * HD1, slot, h, :, :, :].rearrange("p c b l -> p (c b l)"))
                         for w in q] for h in range(2)]
            if name[0] == "k":
                return [w[:, slot, :, :, :].rearrange("p c b l -> p (c b l)") for w in k]
            d = vs[:, slot, int(name[3]), :, :, :, :].rearrange("p c h s f -> p (c h) s f")
            return [d[:, :, s, :] for s in range(2)]

        def work_psum(name):
            ps = work_bank[work.bank(name)]
            return ps if name[0] != "v" else ps.rearrange("p (c f) -> p c f", f=HD1)

        def rounds(eng, body, tail):
            body(0, first=True, last=False)
            with eng.Fori(1, R1 - 1) as i:
                body(i, first=False, last=False)
            body(R1 - 1, first=False, last=True)
            tail(R1)

        block = ctx.enter_context(nc.Block())

        @block.sync
        def _(sp):
            for e in events:
                sp.nop().then_inc(e.sem, e.per)

            def load_u(i):
                sp.dma_start(ub[:, :, :], v["ctx_in"].rearrange("b p d -> p b d")[:, bass.ds(i * NB, NB), :])\
                    .then_inc(u_in.sem, 16)

            load_u(0)
            with sp.Fori(1, R1) as i:
                sp.wait_ge(*zu_lo.at(i - 1, 1))
                load_u(i)

        @block.gpsimd
        def _(pool):
            def norm(i, n):
                pool.wait_ge(*z_inv_done.at(i, n))
                e = prob[:, n % RE, :].rearrange("p (t c) -> p t c", t=2)
                pool.tensor_tensor(e, e, z_inv[:, n % RE, :].unsqueeze(2).broadcast_to([P, 2, D]), ALU.mult)\
                    .then_inc(probs_done.sem, 1)

            def inverse_std(i, name):
                pool.wait_ge(*work.out(name, i))
                pool.tensor_tensor(rstd[:, :], var_eps[:, :], half_neg[:, 0:4], ALU.pow).then_inc(rstd_done.sem, 1)

            def body(i, first, last):
                for t in range(UNITS):
                    if t >= 1 or not first:
                        norm(i, t - 1)
                    if t == T_VAR + 1:
                        inverse_std(i, "var")

            def tail(i):
                norm(i, -1)
                inverse_std(i, "k0")

            pool.memset(q[0][:, :, :, :, :, :].bitcast(F32), 0.0).then_inc(zeroed, 1)
            pool.memset(q[1][:, :, :, :, :, :].bitcast(F32), 0.0).then_inc(zeroed, 1)
            rounds(pool, body, tail)

        @block.tensor
        def _(pe):
            mm = nc.tensor.matmul

            def project(i, name):
                ps = work_bank[work.bank(name)]
                pe.wait_ge(*work.free(name, i))
                pe.wait_ge(*zu_lo.at(i, 1))
                for c in range(2):
                    o = ps[:, c * D:(c + 1) * D]
                    for s, w in enumerate((wz, wi)):
                        for wp, xp in ((0, 0), (0, 1), (1, 0)):
                            flags = {"start": (s, wp, xp) == (0, 0, 0), "stop": (s, wp, xp) == (1, 1, 0)}
                            if name[0] in "qk":
                                at = "qk".index(name[0]) * NQ + int(name[1]) * P
                                last = mm(o, w[wp][:, c, at:at + P],
                                          zu[xp][:, s, c, :, :].rearrange("p b l -> p (b l)"), **flags)
                            else:
                                at = 2 * NQ + int(name[1]) * D
                                last = mm(o, zu[xp][:, s, c, int(name[3]), :], w[wp][:, c, at:at + D], **flags)
                last.then_inc(work.fills(name), 1)

            def scores(i, n):
                pair, h, b = unit(n)
                if n % 4 == 0:
                    pe.wait_ge(*work.out(f"q{pair}", i))
                    pe.wait_ge(*work.out(f"k{pair}", i))
                pe.wait_ge(*exp_done.at(i, n - 2))
                for qt in range(2):
                    for qp, kp in ((0, 0), (0, 1), (1, 0)):
                        last = mm(score_bank[n % 2][:, qt * D:(qt + 1) * D], q[qp][:, pair % 2, h, qt, b, :],
                                  k[kp][:, pair % 2, :, b, :], start=(qp, kp) == (0, 0), stop=(qp, kp) == (1, 0))
                last.then_inc(scores_done.sem, 1)

            def turn(i, n):
                pe.wait_ge(*probs_done.at(i, n))
                pe.wait_ge(*pT_lo.at(i, n - 1))
                for qt in range(2):
                    for kt in range(2):
                        last = nc.tensor.transpose(turn_bank[:, kt * D + qt * P:kt * D + (qt + 1) * P],
                                                   prob[:, n % RE, qt * D + kt * P:qt * D + (kt + 1) * P],
                                                   ident[:, :])
                last.then_inc(turned.sem, 1)

            def times_v(i, n):
                pair, h, b = unit(n)
                if n % 8 == 0:
                    pe.wait_ge(*work.out(f"v{pair // 2}b0", i))
                    pe.wait_ge(*work.out(f"v{pair // 2}b1", i))
                pe.wait_ge(*pT_lo.at(i, n))
                pe.wait_ge(*aT_lo.at(i, n - 1))
                for kt in range(2):
                    w = vs[:, pair // 2 % 2, b, kt, 2 * (pair % 2) + h, :, :].rearrange("p s f -> p (s f)")
                    for pp in range(2):
                        last = mm(pv_bank[:, 0:D], w, pT[pp][:, n % RT, kt * D:(kt + 1) * D],
                                  start=(kt, pp) == (0, 0), stop=(kt, pp) == (1, 1))
                last.then_inc(pv_done.sem, 1)

            def times_wo(i, n):
                pair, h, b = unit(n)
                head = 2 * pair + h
                pe.wait_ge(*aT_lo.at(i, n))
                if head == 0:
                    pe.wait_ge(*y_done.at(i))
                for wp, ap in ((0, 0), (0, 1), (1, 0)):
                    last = mm(wo_bank[b][:, 0:D], wo[wp][:, head, :], aT[ap][:, n % RT, :],
                              start=head == 0 and (wp, ap) == (0, 0), stop=head == H1 - 1 and (wp, ap) == (1, 0))
                last.then_inc(wo_done.sem, 1)

            def mean(i, name):
                pe.wait_ge(*work.free(name, i))
                pe.wait_ge(*y_done.at(i))
                mm(work_bank[work.bank(name)], mean_w[:, :], y[:, :, :].rearrange("p b d -> p (b d)"),
                   start=True, stop=True).then_inc(work.fills(name), 1)

            def variance(i, name):
                pe.wait_ge(*work.free(name, i))
                pe.wait_ge(*squared.at(i))
                for j in range(4):
                    last = mm(work_bank[work.bank(name)][:, j:j + 1], ysq[:, j // 2, j % 2 * P:(j % 2 + 1) * P],
                              mean_w[:, 0:1], start=True, stop=True)
                last.then_inc(work.fills(name), 1)

            def spread(i, name, b):
                pe.wait_ge(*work.free(name, i))
                pe.wait_ge(*diagonal.at(i))
                for j in range(2):
                    last = mm(work_bank[work.bank(name)][:, j * P:(j + 1) * P], mean_w[:, :],
                              diag[:, 2 * b + j, :], start=True, stop=True)
                last.then_inc(work.fills(name), 1)

            def body(i, first, last):
                for t in range(UNITS):
                    scores(i, t)
                    if t >= L_T or not first:
                        turn(i, t - L_T)
                    name, ahead = work_at(t)
                    if name and not (last and ahead):
                        project(i + ahead, name)
                    if t == T_MEAN:
                        mean(i, "mean")
                    if t == T_VAR:
                        variance(i, "var")
                    if t in (T_INV, T_INV + 1):
                        spread(i, f"inv{t - T_INV}", t - T_INV)
                    if t >= L_V or not first:
                        times_v(i, t - L_V)
                    if t >= L_O or not first:
                        times_wo(i, t - L_O)

            def tail(i):
                for t in range(L_O):
                    if t < L_T:
                        turn(i, t - L_T)
                    if t < L_V:
                        times_v(i, t - L_V)
                    times_wo(i, t - L_O)
                mean(i, "q0")
                variance(i, "k0")
                spread(i, "v0b0", 0)
                spread(i, "v0b1", 1)

            pe.wait_ge(zeroed, 2)
            for name in names[:4]:
                project(0, name)
            rounds(pe, body, tail)

        @block.scalar
        def _(act):
            def exponentials(i, n):
                act.wait_ge(*max_done.at(i, n))
                act.wait_ge(*turned.at(i, n - RE))
                for qt in range(2):
                    last = nc.scalar.activation(prob[:, n % RE, qt * D:(qt + 1) * D],
                                                score_bank[n % 2][:, qt * D:(qt + 1) * D], ACT.Exp,
                                                bias=neg_max[:, n % RE, qt:qt + 1],
                                                accum_out=z_sum[:, n % RE, qt:qt + 1])
                last.then_inc(exp_done.sem, 1)

            def round_probs(i, n):
                act.wait_ge(*turned.at(i, n))
                act.wait_ge(*pv_done.at(i, n - RT))
                nc.scalar.copy(pT[0][:, n % RT, :], turn_bank).then_inc(pT_hi.sem, 1)

            def round_heads(i, n):
                act.wait_ge(*pv_done.at(i, n))
                act.wait_ge(*wo_done.at(i, n - RT))
                nc.scalar.copy(aT[0][:, n % RT, :], pv_bank[:, 0:D]).then_inc(aT_hi.sem, 1)

            def round_work(i, name):
                act.wait_ge(*work.full(name, i))
                tile, ps = tile_of(name), work_psum(name)
                if name[0] == "q":
                    for h in range(2):
                        at = slice(h * HD1, (h + 1) * HD1)
                        last = nc.scalar.activation(tile[h][0], ps[at, :], ACT.Identity,
                                                    bias=col("rwb", int(name[1]))[at, :])
                elif name[0] == "k":
                    last = nc.scalar.activation(tile[0], ps, ACT.Identity, scale=SCALE)
                else:
                    last = nc.scalar.copy(tile[0], ps)
                last.then_inc(work_hi.sem, 1)

            def round_inputs(i):
                if not isinstance(i, int) or i > 0:
                    act.wait_ge(*work.full("k7", i - 1))
                nc.scalar.copy(zu[0][:, 0, :, :, :], xs[:, bass.ds(i * NB, NB), :].rearrange(
                    "p b (c l) -> p c b l", c=2)).then_inc(zu_hi.sem, 1)
                act.wait_ge(*u_in.at(i))
                nc.scalar.copy(zu[0][:, 1, :, :, :], ub[:, :, :].rearrange("p b (c l) -> p c b l", c=2))\
                    .then_inc(zu_hi.sem, 1)

            def body(i, first, last):
                for t in range(UNITS):
                    exponentials(i, t)
                    if t >= L_T or not first:
                        round_probs(i, t - L_T)
                    name, ahead = work_at(t)
                    if name and not (last and ahead):
                        round_work(i + ahead, name)
                    if t >= L_V or not first:
                        round_heads(i, t - L_V)
                    if t == T_ZU and not last:
                        round_inputs(i + 1)

            def tail(i):
                for t in range(L_V):
                    if t < L_T:
                        round_probs(i, t - L_T)
                    round_heads(i, t - L_V)

            round_inputs(0)
            act.wait_ge(zeroed, 2)
            for name in names[:4]:
                round_work(0, name)
            rounds(act, body, tail)

        @block.vector
        def _(dve):
            def maxima(i, n):
                dve.wait_ge(*scores_done.at(i, n))
                dve.wait_ge(*exp_done.at(i, n - RE))
                nc.vector.tensor_reduce(neg_max[:, n % RE, :], score_bank[n % 2].rearrange("p (t c) -> p t c", t=2),
                                        AX.X, ALU.max, negate=True).then_inc(max_done.sem, 1)

            def inverse_sums(i, n):
                dve.wait_ge(*exp_done.at(i, n))
                dve.wait_ge(*probs_done.at(i, n - RE))
                nc.vector.reciprocal(z_inv[:, n % RE, :], z_sum[:, n % RE, :]).then_inc(z_inv_done.sem, 1)

            def rest_probs(i, n):
                dve.wait_ge(*pT_hi.at(i, n))
                nc.vector.tensor_tensor(pT[1][:, n % RT, :], turn_bank, pT[0][:, n % RT, :].bitcast(F32),
                                        ALU.subtract).then_inc(pT_lo.sem, 1)

            def rest_heads(i, n):
                dve.wait_ge(*aT_hi.at(i, n))
                nc.vector.tensor_tensor(aT[1][:, n % RT, :], pv_bank[:, 0:D], aT[0][:, n % RT, :].bitcast(F32),
                                        ALU.subtract).then_inc(aT_lo.sem, 1)

            def rest_work(i, name):
                dve.wait_ge(*work_hi.at(i, made.index(name)))
                tile, ps = tile_of(name), work_psum(name)
                if name[0] == "q":
                    for h in range(2):
                        at = slice(h * HD1, (h + 1) * HD1)
                        hi, lo = tile[h]
                        last = nc.vector.scalar_tensor_tensor(
                            out=lo, in0=ps[at, :], scalar=col("rwb", int(name[1]))[at, :], in1=hi.bitcast(F32),
                            op0=ALU.add, op1=ALU.subtract)
                elif name[0] == "k":
                    last = nc.vector.scalar_tensor_tensor(out=tile[1], in0=ps, scalar=SCALE,
                                                          in1=tile[0].bitcast(F32), op0=ALU.mult, op1=ALU.subtract)
                else:
                    last = nc.vector.tensor_tensor(tile[1], ps, tile[0].bitcast(F32), ALU.subtract)
                last.then_inc(work.reads(name), 1)

            def rest_inputs(i):
                dve.wait_ge(*zu_hi.at(i, 0))
                z = xs[:, bass.ds(i * NB, NB), :].rearrange("p b (c l) -> p c b l", c=2)
                nc.vector.tensor_tensor(zu[1][:, 0, :, :, :], z, zu[0][:, 0, :, :, :].bitcast(F32), ALU.subtract)\
                    .then_inc(zu_lo.sem, 1)
                dve.wait_ge(*zu_hi.at(i, 1))
                nc.vector.tensor_tensor(zu[1][:, 1, :, :, :], ub[:, :, :].rearrange("p b (c l) -> p c b l", c=2),
                                        zu[0][:, 1, :, :, :].bitcast(F32), ALU.subtract).then_inc(zu_lo.sem, 1)

            def residual(i):
                dve.wait_ge(*wo_done.at(i, -1))
                for b in range(NB):
                    last = nc.vector.scalar_tensor_tensor(
                        out=y[:, b, :], in0=wo_bank[b][:, 0:D], scalar=col("bo"),
                        in1=xs[:, bass.ds((i - 1) * NB + b, 1), :].rearrange("p a d -> p (a d)"),
                        op0=ALU.add, op1=ALU.add)
                last.then_inc(y_done.sem, 1)

            def centre(i, name):
                dve.wait_ge(*work.full(name, i))
                yy = y[:, :, :].rearrange("p b d -> p (b d)")
                nc.vector.tensor_tensor(yy, yy, work_bank[work.bank(name)], ALU.subtract)\
                    .then_inc(work.reads(name), 1)
                dve.wait_ge(*work.out(name, i))
                nc.vector.tensor_tensor(ysq[:, :, :], y[:, :, :], y[:, :, :], ALU.mult).then_inc(squared.sem, 1)

            def read_variance(i, name):
                dve.wait_ge(*work.full(name, i))
                nc.vector.tensor_scalar(var_eps[:, :], work_bank[work.bank(name)][:, 0:4], EPS, None, ALU.add)\
                    .then_inc(work.reads(name), 1)

            def make_diagonal(i):
                dve.wait_ge(*rstd_done.at(i))
                for j in range(4):
                    last = nc.vector.tensor_scalar(diag[:, j, :], ident[:, :], rstd[:, j:j + 1], float(P),
                                                   ALU.mult, ALU.mult)
                last.then_inc(diagonal.sem, 1)

            def output(i, name, b, first=False):
                dve.wait_ge(*work.full(name, i))
                ps = work_bank[work.bank(name)][:, 0:D]
                to = y[:, b, :] if first else xs[:, bass.ds((i - 1) * NB + b, 1), :].rearrange("p a d -> p (a d)")
                nc.vector.tensor_tensor(to, y[:, b, :], ps, ALU.mult).then_inc(work.reads(name), 1)

            def body(i, first, last):
                for t in range(UNITS):
                    if t >= 1 or not first:
                        inverse_sums(i, t - 1)
                    maxima(i, t)
                    if t >= L_T or not first:
                        rest_probs(i, t - L_T)
                    name, ahead = work_at(t)
                    if name and not (last and ahead):
                        rest_work(i + ahead, name)
                    if t >= L_V or not first:
                        rest_heads(i, t - L_V)
                    if t == T_Y:
                        if first:
                            nc.vector.memset(y[:, :, :], 0.0).then_inc(y_done.sem, 1)
                        else:
                            residual(i)
                    if t == T_MEAN:
                        centre(i, "mean")
                    if t == T_VAR:
                        read_variance(i, "var")
                    if t == T_VAR + 2:
                        make_diagonal(i)
                    if t in (T_INV, T_INV + 1):
                        output(i, f"inv{t - T_INV}", t - T_INV, first)
                    if t == T_ZU and not last:
                        rest_inputs(i + 1)

            def tail(i):
                inverse_sums(i, -1)
                for t in range(L_V):
                    if t < L_T:
                        rest_probs(i, t - L_T)
                    rest_heads(i, t - L_V)
                residual(i)
                centre(i, "q0")
                read_variance(i, "k0")
                make_diagonal(i)
                output(i, "v0b0", 0)
                output(i, "v0b1", 1)

            rest_inputs(0)
            dve.wait_ge(zeroed, 2)
            for name in names[:4]:
                rest_work(0, name)
            rounds(dve, body, tail)


def layers23(nc, v):
    (psum, xs, ident, half_neg, col) = (v[n] for n in ("psum", "xs", "ident", "half_neg", "col"))
    DK = 16
    CI = 64
    RE, RT = 4, 2
    with ExitStack() as ctx:
        def sb(name, shape, dt=F32):
            return ctx.enter_context(nc.sbuf_tensor(name, shape, dt))

        def sem(name):
            return ctx.enter_context(nc.semaphore(name))

        events = []

        def event(name, per, unit=1):
            e = Event(ctx, nc, "l2_" + name, per, unit)
            events.append(e)
            return e

        wqk = sb("wqk2", [P, 2 * DK])
        wvpg = sb("wvpg", [P, D])
        wtheta = sb("wtheta", [P, CI])
        ww = sb("ww", [CI, P])
        bvpg = sb("bvpg", [P, D])
        bn = sb("bn", [P, 4])
        cg = sb("cg", [P, G, D])
        xg = sb("l2_xg", [P, G, D])
        q2 = sb("q2", [P, G, D])
        k2 = sb("k2", [P, G, D])
        vpg = sb("vpg", [P, G, 2, D])
        gT = sb("gT", [CI, G, P])
        hw = sb("hw", [CI, G, P])
        theta = sb("theta", [CI, G, D])
        prob = sb("l2_prob", [P, RE, BANK])
        pT = sb("l2_pT", [P, RT, BANK])
        x2 = sb("x2", [P, G, D])
        fin = sb("fin", [P, G, D])
        neg_max = sb("l2_neg_max", [P, RE, 2])
        z_sum = sb("l2_z_sum", [P, RE, 2])
        z_inv = sb("l2_z_inv", [P, RE, 2])

        score_bank = [psum[:, j, :] for j in range(2)]
        turn_bank = [psum[:, 2 + j, :] for j in range(2)]
        pv_bank = [psum[:, 4 + j, 0:D] for j in range(2)]
        work_bank = [psum[:, 6 + j, :] for j in range(2)]

        names = ["q0", "q1", "k0", "k1"] + [f"w{b}" for b in range(G)] + ["g", "h", "t0", "t1", "y0", "y1"]
        work = Banks(ctx, nc, "l2_work", names)
        events += work.full_ev + work.out_ev
        ctx_in = event("ctx_in", 1, 16)
        x_copied = event("x_copied", 1)
        scores_done = event("scores_done", G)
        max_done = event("max_done", G)
        exp_done = event("exp_done", G)
        z_inv_done = event("z_inv_done", G)
        probs_done = event("probs_done", G)
        turned = event("turned", G)
        probsT_done = event("probsT_done", G)
        pv_done = event("pv_done", G)
        x2_done = event("x2_done", G)
        final_done = event("final_done", 2)
        out_written = event("out_written", 1, 16)
        weights_in = sem("l2_weights_in")
        zeroed = sem("l2_zeroed")
        bn_step = sem("bn_step")

        def two(t, m):
            return t[:, 2 * m:2 * m + 2, :].rearrange("p b d -> p (b d)")

        block = ctx.enter_context(nc.Block())

        @block.sync
        def _(sp):
            for e in events:
                sp.nop().then_inc(e.sem, e.per)
            sp.dma_start(wqk[:, :], v["wqk2_in"]).then_inc(weights_in, 16)
            sp.dma_start(wvpg[:, :], v["wvpg_in"]).then_inc(weights_in, 16)
            sp.dma_start(wtheta[:, :], v["theta_in"]).then_inc(weights_in, 16)
            sp.dma_start(ww[:, :], v["ww_in"]).then_inc(weights_in, 16)
            sp.dma_start(bvpg[:, :], v["rows_in"][ROWS["bvpg"]:ROWS["bvpg"] + D].partition_broadcast(P))\
                .then_inc(weights_in, 16)

            def load(i):
                sp.dma_start(cg[:, :, :], v["ctx_in"].rearrange("b p d -> p b d")[:, bass.ds(i * G, G), :])\
                    .then_inc(ctx_in.sem, 16)

            def store(i):
                sp.wait_ge(*final_done.at(i, 1))
                sp.dma_start(v["out"].rearrange("b p d -> p b d")[:, bass.ds(i * G, G), :], fin[:, :, :])\
                    .then_inc(out_written.sem, 16)

            load(0)
            with sp.Fori(1, ROUNDS) as i:
                sp.wait_ge(*work.full("w3", i - 1))
                load(i)
                store(i - 1)
            store(ROUNDS - 1)
            sp.wait_ge(*out_written.at(ROUNDS - 1))

        @block.gpsimd
        def _(pool):
            pool.memset(q2[:, :, :], 0.0).then_inc(zeroed, 1)
            pool.memset(k2[:, :, :], 0.0).then_inc(zeroed, 1)
            pool.memset(gT[:, :, :], 0.0).then_inc(zeroed, 1)
            pool.tensor_scalar(bn[:, 0:1], col("bn_var"), EPS, None, ALU.add).then_inc(bn_step, 1)
            pool.tensor_tensor(bn[:, 3:4], col("w_b"), col("bn_mean"), ALU.subtract).then_inc(bn_step, 1)
            pool.wait_ge(bn_step, 2)
            pool.tensor_tensor(bn[:, 1:2], bn[:, 0:1], half_neg[:, 0:1], ALU.pow).then_inc(bn_step, 1)
            pool.wait_ge(bn_step, 3)
            pool.tensor_tensor(bn[:, 2:3], bn[:, 1:2], col("gamma"), ALU.mult).then_inc(bn_step, 1)
            pool.wait_ge(bn_step, 4)
            pool.tensor_tensor(bn[:, 3:4], bn[:, 3:4], bn[:, 2:3], ALU.mult).then_inc(bn_step, 1)
            pool.wait_ge(bn_step, 5)
            pool.tensor_tensor(bn[:, 3:4], bn[:, 3:4], col("beta"), ALU.add).then_inc(bn_step, 1)

        @block.tensor
        def _(pe):
            mm = nc.tensor.matmul

            def bank(name, i):
                pe.wait_ge(*work.free(name, i))
                return work_bank[work.bank(name)]

            pe.wait_ge(weights_in, 80)
            pe.wait_ge(zeroed, 3)
            with pe.Fori(0, ROUNDS) as i:
                pe.wait_ge(*x_copied.at(i))
                for m in range(2):
                    mm(bank(f"q{m}", i)[0:DK, :], wqk[:, 0:DK], two(xg, m), start=True, stop=True)\
                        .then_inc(work.fills(f"q{m}"), 1)
                pe.wait_ge(*ctx_in.at(i))
                for m in range(2):
                    mm(bank(f"k{m}", i)[0:DK, :], wqk[:, DK:2 * DK], two(cg, m), start=True, stop=True)\
                        .then_inc(work.fills(f"k{m}"), 1)
                for b in range(G):
                    ps = bank(f"w{b}", i)
                    for j in range(2):
                        last = mm(ps[:, j * D:(j + 1) * D], cg[:, b, j * P:(j + 1) * P], wvpg[:, :],
                                  start=True, stop=True)
                    last.then_inc(work.fills(f"w{b}"), 1)
                pe.wait_ge(*work.out("k0", i))
                pe.wait_ge(*work.out("k1", i))

                def scores(b):
                    pe.wait_ge(*exp_done.at(i, b - 2))
                    for qt in range(2):
                        last = mm(score_bank[b % 2][:, qt * D:(qt + 1) * D], q2[:, b, qt * P:(qt + 1) * P],
                                  k2[:, b, :], start=True, stop=True)
                    last.then_inc(scores_done.sem, 1)

                def turn(b):
                    pe.wait_ge(*probs_done.at(i, b))
                    pe.wait_ge(*probsT_done.at(i, b - 2))
                    for qt in range(2):
                        for kt in range(2):
                            last = nc.tensor.transpose(turn_bank[b % 2][:, kt * D + qt * P:kt * D + (qt + 1) * P],
                                                       prob[:, b % RE, qt * D + kt * P:qt * D + (kt + 1) * P],
                                                       ident[:, :])
                    last.then_inc(turned.sem, 1)

                def times_v(b):
                    pe.wait_ge(*probsT_done.at(i, b))
                    pe.wait_ge(*x2_done.at(i, b - 2))
                    for kt in range(2):
                        last = mm(pv_bank[b % 2], vpg[:, b, kt, 0:P], pT[:, b % RT, kt * D:(kt + 1) * D],
                                  start=kt == 0, stop=kt == 1)
                    last.then_inc(pv_done.sem, 1)

                for b in range(3):
                    scores(b)
                pe.wait_ge(*work.out("w2", i))
                pe.wait_ge(*work.out("w3", i))
                ps = bank("g", i)
                for b in range(G):
                    for j in range(2):
                        last = mm(ps[0:CI, b * CI:(b + 1) * CI], vpg[:, b, j, P + CI:D], vpg[:, b, j, P:P + CI],
                                  start=j == 0, stop=j == 1)
                last.then_inc(work.fills("g"), 1)
                turn(0)
                scores(3)
                turn(1)
                times_v(0)
                pe.wait_ge(*work.out("g", i))
                ps = bank("h", i)
                for b in range(G):
                    last = mm(ps[:, b * P:(b + 1) * P], gT[:, b, :], ww[:, :], start=True, stop=True)
                last.then_inc(work.fills("h"), 1)
                turn(2)
                times_v(1)
                turn(3)
                times_v(2)
                pe.wait_ge(*x2_done.at(i, 1))
                mm(bank("t0", i)[0:CI, :], wtheta[:, :], two(x2, 0), start=True, stop=True)\
                    .then_inc(work.fills("t0"), 1)
                times_v(3)
                pe.wait_ge(*x2_done.at(i, 3))
                mm(bank("t1", i)[0:CI, :], wtheta[:, :], two(x2, 1), start=True, stop=True)\
                    .then_inc(work.fills("t1"), 1)
                pe.wait_ge(*work.out("h", i))
                for m in range(2):
                    pe.wait_ge(*work.out(f"t{m}", i))
                    ps = bank(f"y{m}", i)
                    for b in (2 * m, 2 * m + 1):
                        last = mm(ps[:, b % 2 * D:(b % 2 + 1) * D], hw[:, b, :], theta[:, b, :],
                                  start=True, stop=True)
                    last.then_inc(work.fills(f"y{m}"), 1)

        @block.scalar
        def _(act):
            act.wait_ge(zeroed, 3)
            with act.Fori(0, ROUNDS) as i:
                act.wait_ge(*x2_done.at(i - 1, G - 1))
                nc.scalar.copy(xg[:, :, :], xs[:, bass.ds(i * G, G), :]).then_inc(x_copied.sem, 1)
                for name, t, bias in (("q", q2, "bq2"), ("k", k2, "bk2")):
                    for m in range(2):
                        act.wait_ge(*work.full(f"{name}{m}", i))
                        nc.scalar.activation(two(t, m)[0:DK, :], work_bank[work.bank(f"{name}{m}")][0:DK, :],
                                             ACT.Identity, bias=col(bias, p=DK)).then_inc(work.reads(f"{name}{m}"), 1)

                def exponentials(b):
                    act.wait_ge(*max_done.at(i, b))
                    act.wait_ge(*turned.at(i, b - RE))
                    for qt in range(2):
                        last = nc.scalar.activation(prob[:, b % RE, qt * D:(qt + 1) * D],
                                                    score_bank[b % 2][:, qt * D:(qt + 1) * D], ACT.Exp,
                                                    bias=neg_max[:, b % RE, qt:qt + 1],
                                                    accum_out=z_sum[:, b % RE, qt:qt + 1])
                    last.then_inc(exp_done.sem, 1)

                def turned_out(b):
                    act.wait_ge(*turned.at(i, b))
                    act.wait_ge(*pv_done.at(i, b - RT))
                    nc.scalar.copy(pT[:, b % RT, :], turn_bank[b % 2]).then_inc(probsT_done.sem, 1)

                exponentials(0)
                exponentials(1)
                exponentials(2)
                act.wait_ge(*work.full("g", i))
                nc.scalar.activation(gT[:, :, 0:CI], work_bank[work.bank("g")][0:CI, 0:G * CI].rearrange(
                    "p (b c) -> p b c", b=G), ACT.Identity, scale=1.0 / D).then_inc(work.reads("g"), 1)
                turned_out(0)
                exponentials(3)
                turned_out(1)
                act.wait_ge(*work.full("h", i))
                nc.scalar.copy(hw[:, :, :].rearrange("p b c -> p (b c)"), work_bank[work.bank("h")][0:CI, :])\
                    .then_inc(work.reads("h"), 1)
                turned_out(2)
                turned_out(3)
                for m in range(2):
                    act.wait_ge(*work.full(f"t{m}", i))
                    nc.scalar.activation(two(theta, m), work_bank[work.bank(f"t{m}")][0:CI, :], ACT.Identity,
                                         bias=col("theta_b", p=CI)).then_inc(work.reads(f"t{m}"), 1)

        @block.vector
        def _(dve):
            dve.wait_ge(weights_in, 80)
            dve.wait_ge(bn_step, 6)
            with dve.Fori(0, ROUNDS) as i:
                def maxima(b):
                    dve.wait_ge(*scores_done.at(i, b))
                    dve.wait_ge(*exp_done.at(i, b - RE))
                    nc.vector.tensor_reduce(neg_max[:, b % RE, :], score_bank[b % 2].rearrange(
                        "p (t c) -> p t c", t=2), AX.X, ALU.max, negate=True).then_inc(max_done.sem, 1)

                def values(b):
                    dve.wait_ge(*work.full(f"w{b}", i))
                    nc.vector.tensor_tensor(vpg[:, b, :, :], work_bank[work.bank(f"w{b}")].rearrange(
                        "p (j n) -> p j n", j=2), bvpg[:, :].unsqueeze(1).broadcast_to([P, 2, D]), ALU.add)\
                        .then_inc(work.reads(f"w{b}"), 1)

                def norm(b):
                    dve.wait_ge(*exp_done.at(i, b))
                    nc.vector.reciprocal(z_inv[:, b % RE, :], z_sum[:, b % RE, :]).then_inc(z_inv_done.sem, 1)
                    dve.wait_ge(*z_inv_done.at(i, b))
                    e = prob[:, b % RE, :].rearrange("p (t c) -> p t c", t=2)
                    nc.vector.tensor_tensor(e, e, z_inv[:, b % RE, :].unsqueeze(2).broadcast_to([P, 2, D]),
                                            ALU.mult).then_inc(probs_done.sem, 1)

                def add_x(b):
                    dve.wait_ge(*pv_done.at(i, b))
                    nc.vector.tensor_tensor(x2[:, b, :], pv_bank[b % 2], xg[:, b, :], ALU.add)\
                        .then_inc(x2_done.sem, 1)

                for b in range(G):
                    values(b)
                maxima(0)
                maxima(1)
                norm(0)
                maxima(2)
                norm(1)
                norm(2)
                maxima(3)
                norm(3)
                for b in range(G):
                    add_x(b)
                for m in range(2):
                    dve.wait_ge(*work.full(f"y{m}", i))
                    if m == 0:
                        dve.wait_ge(*out_written.at(i - 1))
                    nc.vector.tensor_scalar(two(fin, m), work_bank[work.bank(f"y{m}")], bn[:, 2:3], bn[:, 3:4],
                                            ALU.mult, ALU.add).then_inc(work.reads(f"y{m}"), 1)
                    dve.wait_ge(*work.out(f"y{m}", i))
                    nc.vector.tensor_tensor(two(fin, m), two(fin, m), two(x2, m), ALU.add)\
                        .then_inc(final_done.sem, 1)


def layout(inputs):
    a = {n: np.asarray(x) for n, x in inputs.items()}
    L0, L1, L2, L3 = ((lambda n, p=p: a[p + n]) for p in ("L0_xattn_", "L1_xattn_", "L2_xattn_", "L3_xattn_"))
    flat = {"ln_s": [L0("ln1_s"), L0("ln2_s"), L0("ln3_s")], "ln_b": [L0("ln1_b"), L0("ln2_b"), L0("ln3_b")],
            "bq0": [L0("b_qkv")[0:D]], "bk0": [L0("b_qkv")[D:2 * D]], "bcq": [L0("b_q")], "bck": [L0("b_kv")[0:D]],
            "b1": [L0("b1")], "bo": [L1("bo")], "rwb": [L1("r_w_bias").reshape(-1)], "bq2": [L2("bq")],
            "bk2": [L2("bk")], "theta_b": [L3("theta_b")], "w_b": [L3("w_b")], "gamma": [L3("bn_gamma")],
            "beta": [L3("bn_beta")], "bn_mean": [L3("bn_mean")], "bn_var": [L3("bn_var")]}
    cols = np.zeros((P, NCOLS), np.float32)
    for name, (at, n) in COLS.items():
        vec = np.concatenate(flat[name])
        if vec.size < P:
            vec = np.concatenate([vec, np.zeros(P - vec.size, np.float32)])
        cols[:, at:at + n] = vec.reshape(n, P).T
    rows = np.concatenate([L0("b_qkv")[2 * D:], L0("b_ao"), L0("b_kv")[D:], L0("b_co"), L0("b2"),
                           L2("bv"), L3("phi_b"), L3("g_b")])
    arrays = {
        "x": a["x"], "ctx_in": a["ctx_2048"], "ctxT": a["ctx_2048"].reshape(B * P, D).T,
        "smask": a["mask_1x1xSxS2_fc1"].reshape(P, P), "cmask": a["mask_Bx1xSxS2_ff1"].reshape(B, P, P),
        "cols_in": cols, "rows_in": rows,
        "wqkv_in": L0("w_qkv"), "wao_in": L0("w_ao"), "wq_in": L0("w_q"), "wkv_in": L0("w_kv"),
        "wco_in": L0("w_co"), "w1_in": L0("w1"), "w2_in": L0("w2"),
        "wz_in": np.concatenate([L1("Wqkv0").T, L1("Wqkv1").T]),
        "wi_in": np.concatenate([L1("Winj0").T, L1("Winj1").T]),
        "wo_in": L1("Wo").T,
        "wqk2_in": np.concatenate([L2("Wq").T, L2("Wk").T], axis=1),
        "wvpg_in": np.concatenate([L2("Wv").T, L3("phi_w").T, L3("g_w").T], axis=1),
        "theta_in": L3("theta_w").T, "ww_in": L3("w_w").T,
    }
    return {n: np.ascontiguousarray(x) for n, x in arrays.items()}


def kernel(**inputs):
    import concourse.bacc as bacc
    from concourse.bass_utils import run_bass_kernel_spmd

    arrays = layout(inputs)
    nc = bacc.Bacc("TRN2", target_bir_lowering=False, num_devices=1)
    args = [nc.dram_tensor(n, x.shape, mybir.dt.from_np(x.dtype), kind="ExternalInput").ap()
            for n, x in arrays.items()]
    out = nc.dram_tensor("out", (B, P, D), F32, kind="ExternalOutput").ap()
    program(nc, *args, out)
    result = run_bass_kernel_spmd(nc, [arrays], core_ids=[0])
    return result.results[0]["out"]
```

```python
from contextlib import ExitStack

import numpy as np
import concourse.bass as bass
from concourse import mybir

F32 = mybir.dt.float32
F32R = mybir.dt.float32r
ALU = mybir.AluOpType
ACT = mybir.ActivationFunctionType
AX = mybir.AxisListType

P = 128
B = 16
D = 256
G = 4
ROUNDS = B // G
TOK = G * P
EPS = 1e-5
H0, HD0 = 16, 16
QUAD = 4
F0 = 1024
H1, HD1 = 16, 64
PAIRS = H1 // 2
BANK = 512
LAG_T, LAG_V = 2, 3


class Event:

    def __init__(self, ctx, nc, name, per, unit=1):
        self.sem = ctx.enter_context(nc.semaphore(name))
        self.per, self.unit = per * unit, unit

    def at(self, i, k=0):
        return self.sem, (i + 1) * self.per + (k + 1) * self.unit


class Banks:

    def __init__(self, ctx, nc, tag, names, banks):
        n = len(banks)
        assert len(names) % n == 0
        self.place = {name: (k % n, k // n) for k, name in enumerate(names)}
        self.banks = banks
        self.full_ev = [Event(ctx, nc, f"{tag}_bank{j}_full", len(names) // n) for j in range(n)]
        self.out_ev = [Event(ctx, nc, f"{tag}_bank{j}_read_out", len(names) // n) for j in range(n)]

    def psum(self, name):
        return self.banks[self.place[name][0]]

    def free(self, name, i):
        j, k = self.place[name]
        return self.out_ev[j].at(i, k - 1)

    def full(self, name, i):
        j, k = self.place[name]
        return self.full_ev[j].at(i, k)

    def out(self, name, i):
        j, k = self.place[name]
        return self.out_ev[j].at(i, k)

    def fills(self, name):
        return self.full_ev[self.place[name][0]].sem

    def reads(self, name):
        return self.out_ev[self.place[name][0]].sem


COLS = {}
for _name, _n in (("ln_s", 6), ("ln_b", 6), ("bq0", 2), ("bk0", 2), ("bcq", 2), ("bck", 2), ("b1", 8),
                  ("bo", 1), ("rwb", 8), ("bq2", 1), ("bk2", 1), ("theta_b", 1), ("w_b", 1), ("gamma", 1),
                  ("beta", 1), ("bn_mean", 1), ("bn_var", 1)):
    _at = sum(n for _, n in COLS.values())
    COLS[_name] = (_at, _n)
NCOLS = sum(n for _, n in COLS.values())
ROWS = {n: k * D for k, n in enumerate(("bv0", "bao", "bcv", "bco", "b2", "bvpg"))}


def program(nc, x, ctx_in, ctxT, smask, cmask, cols_in, rows_in, wqkv_in, wao_in, wq_in, wkv_in, wco_in,
            w1_in, w2_in, wz_in, wi_in, wo_in, wqk2_in, wvpg_in, theta_in, ww_in, out, dbg=None, phases="ABC"):
    with ExitStack() as ctx:
        def sb(name, shape, c=ctx):
            return c.enter_context(nc.sbuf_tensor(name, shape, F32))

        psum = ctx.enter_context(nc.psum_tensor("psum", [P, 8, BANK], F32))

        xs = sb("xs", [P, B, D])
        ident = sb("ident", [P, P])
        mean_w = sb("mean_w", [P, P])
        cols = sb("cols", [P, NCOLS])
        half_neg = sb("half_neg", [P, 4])

        def col(name, k=0, n=1, p=P):
            at = COLS[name][0] + k
            return cols[0:p, at:at + n]

        if "A" in phases:
            layer0(nc, locals())
        if "B" in phases:
            layer1(nc, locals())
        if "C" in phases:
            layers23(nc, locals())
        if dbg is not None:
            s_dbg = ctx.enter_context(nc.semaphore("s_dbg"))
            block = nc.Block()
            with block:
                @block.sync
                def _(sp):
                    sp.dma_start(dbg.rearrange("b p d -> p b d"), xs[:, :, :]).then_inc(s_dbg, 16)
                    sp.wait_ge(s_dbg, 16)


def layer0(nc, v):
    (psum, xs, ident, mean_w, cols, half_neg, col) = (v[n] for n in (
        "psum", "xs", "ident", "mean_w", "cols", "half_neg", "col"))
    U = G * H0 // QUAD
    RE, RT, RK = 4, 2, 4
    L_E, L_T, L_P, L_V, LEAD_K = 1, 3, 4, 5, 2
    STEPS = U + L_V
    VSTEP = P + HD0
    with ExitStack() as ctx:
        def sb(name, shape):
            return ctx.enter_context(nc.sbuf_tensor(name, shape, F32))

        def sem(name):
            return ctx.enter_context(nc.semaphore(name))

        events = []

        def event(name, per, unit=1):
            e = Event(ctx, nc, name, per, unit)
            events.append(e)
            return e

        rows = sb("rows", [P, len(ROWS) * D])
        wqkv = sb("wqkv", [P, 2, 3 * D])
        wao = sb("wao", [P, 2, D])
        wq = sb("wq", [P, 2, D])
        wkv = sb("wkv", [P, 2, 2 * D])
        wco = sb("wco", [P, 2, D])
        w1 = sb("w1", [P, 2, F0])
        w2 = sb("w2", [P, F0 // P, D])
        xg = sb("xg", [P, G, D])
        xr = sb("xr", [P, G, D])
        xm = sb("xm", [P, G, D])
        ln = sb("ln", [P, G, D])
        lnT1 = sb("lnT1", [P, 2, TOK])
        lnT = sb("lnT", [P, 2, TOK])
        qT, kT, oT, cT, cqT, ckT = (sb(n, [P, 2, TOK]) for n in ("qT", "kT", "oT", "cT", "cqT", "ckT"))
        hid = sb("hid", [P, F0 // P, TOK])
        km = sb("km", [P, RK, BANK])
        vm = sb("vm", [P, 2, 2, 8 * VSTEP])
        ring_e = sb("ring_e", [P, RE, BANK])
        ring_t = sb("ring_t", [P, RT, BANK])
        ring_h = sb("ring_h", [P, 2, BANK])
        ring_g = sb("ring_g", [P, 2, BANK])
        neg_max = sb("neg_max", [P, RE, QUAD])
        z_sum = sb("z_sum", [P, RE, QUAD])
        z_inv = sb("z_inv", [P, RE, QUAD])
        self_mul = sb("self_mul", [P, P])
        self_add = sb("self_add", [P, P])
        cross_mul = sb("cross_mul", [P, G, P])
        cross_add = sb("cross_add", [P, G, P])
        stats = sb("stats", [P, G, 6])
        mean_var = sb("mean_var", [P, G, 2])
        var_eps = sb("var_eps", [P, G])
        eps = sb("eps", [P, G])
        first_stat = sb("first_stat", [P, 1])
        rstd = sb("rstd", [P, G])
        head_rows = sb("head_rows", [P, 8])
        bq_scaled = sb("bq_scaled", [P, 4])

        def row(name):
            return rows[:, ROWS[name]:ROWS[name] + D]

        score_bank = [psum[:, j, :] for j in range(2)]
        turn_bank = psum[:, 2, :]
        pv_bank = psum[:, 3, :]

        entry = Banks(ctx, nc, "entry", ["T0h0", "T0h1", "q0", "q1", "k0", "k1", "v0", "v1", "v2", "v3"],
                      [psum[:, 4, :]])
        middle = Banks(ctx, nc, "middle", ["ck0", "ck1", "o0", "o1", "cv0", "T1h0", "T1h1", "cq0", "cq1", "cv1",
                                           "cv2", "cv3", "co0", "co1"], [psum[:, 5 + j, :] for j in range(2)])
        mlp = Banks(ctx, nc, "mlp", ["T2h0", "T2h1"] + [f"f{f}" for f in range(8)] + [f"y{b}" for b in range(G)],
                    [psum[:, 7, :]])
        for banks in (entry, middle, mlp):
            events += banks.full_ev + banks.out_ev
        input_in = event("input_in", 1, 16)
        cross_mask_in = event("cross_mask_in", 1, 16)
        ctxT_in = event("ctxT_in", 1, 16)
        stats_done = [event(f"stats{k}_done", 1) for k in range(3)]
        mean_var_done = [event(f"mean_var{k}_done", 1) for k in range(3)]
        var_eps_done = [event(f"var_eps{k}_done", 1) for k in range(3)]
        rstd_done = [event(f"rstd{k}_done", 1) for k in range(3)]
        ln_done = [event(f"ln{k}_done", 1) for k in range(3)]
        residual_biased = [event(f"residual{k}_biased", 1) for k in range(3)]
        keys_masked = event("keys_masked", 2 * U)
        scores_done = event("scores_done", 2 * U)
        scores_mul = event("scores_mul", 2 * U)
        scores_add = event("scores_add", 2 * U)
        max_done = event("max_done", 2 * U)
        exp_done = event("exp_done", 2 * U)
        z_inv_done = event("z_inv_done", 2 * U)
        probs_done = event("probs_done", 2 * U)
        turned = event("turned", 2 * U)
        probsT_done = event("probsT_done", 2 * U)
        pv_done = event("pv_done", 2 * U)
        heads_out = event("heads_out", U)
        cross_add_made = event("cross_add_made", 1)
        h_lin = event("h_lin", 8)
        h_poly = event("h_poly", 8)
        h_arg = event("h_arg", 8)
        h_tanh = event("h_tanh", 8)
        h_gate = event("h_gate", 8)

        (w_consts, w_qkv, w_ao, w_kv, w_q, w_co, w_1, w_2, w_mask) = (
            sem(f"weights_in_{n}") for n in ("consts", "qkv", "ao", "kv", "q", "co", "1", "2", "mask"))
        consts_made = sem("consts_made")
        head_rows_made = sem("head_rows_made")
        dve_consts = sem("dve_consts")
        ident_step = sem("ident_step")

        BESIDE = [{1: "T2h0", 2: "T2h1", 3: "f0", 4: "f1", 5: "v1", 6: "f2", 7: "f3", 8: "f4", 9: "v2", 10: "f5",
                   11: "f6", 12: "f7", 13: "v3", 15: "y0", 16: "y1", 17: "y2", 18: "y3", 19: "ck0", 20: "ck1"},
                  {5: "cv1", 7: "T0h0", 8: "T0h1", 9: "cv2", 13: "cv3", 14: "q0", 15: "q1", 16: "k0",
                   17: "k1", 18: "v0"}]
        NORM_AT = (3, 6)

        def beside(i, a, t, first, last):
            name = BESIDE[a].get(t)
            if name is None or (a == 0 and name in mlp.place and first) or (a == 1 and name in entry.place and last):
                return None, 0
            return name, i - 1 if name in mlp.place else i + 1 if a == 1 and name in entry.place else i

        def banks_of(name):
            return entry if name in entry.place else middle if name in middle.place else mlp

        def bodies(eng, prologue, body, epilogue):
            prologue()
            body(0, first=True, last=False)
            with eng.Fori(1, ROUNDS - 1) as i:
                body(i, first=False, last=False)
            body(ROUNDS - 1, first=False, last=True)
            epilogue(ROUNDS)

        block = ctx.enter_context(nc.Block())

        @block.sync
        def _(sp):
            for e in events:
                sp.nop().then_inc(e.sem, e.per)

            def load_round(i):
                sp.dma_start(xg[:, :, :], v["x"].rearrange("b s d -> s b d")[:, bass.ds(i * G, G), :])\
                    .then_inc(input_in.sem, 16)

            def load_cross(i):
                sp.dma_start(cT[:, :, :], v["ctxT"].rearrange("(c p) t -> p c t", c=2)[:, :, bass.ds(i * TOK, TOK)])\
                    .then_inc(ctxT_in.sem, 16)
                sp.dma_start(cross_mul[:, :, :], v["cmask"].rearrange("b q k -> q b k")[:, bass.ds(i * G, G), :])\
                    .then_inc(cross_mask_in.sem, 16)

            load_round(0)
            sp.dma_start(cols[:, :], v["cols_in"]).then_inc(w_consts, 16)
            sp.dma_start(rows[:, :], v["rows_in"].partition_broadcast(P)).then_inc(w_consts, 16)
            sp.dma_start(wqkv[:, :, :], v["wqkv_in"].rearrange("(c p) n -> p c n", p=P)).then_inc(w_qkv, 16)
            sp.dma_start(self_mul[:, :], v["smask"]).then_inc(w_mask, 16)
            load_cross(0)
            for w, src, s in ((wkv, "wkv_in", w_kv), (wao, "wao_in", w_ao), (wq, "wq_in", w_q),
                              (wco, "wco_in", w_co), (w1, "w1_in", w_1), (w2, "w2_in", w_2)):
                sp.dma_start(w[:, :, :], v[src].rearrange("(c p) n -> p c n", p=P)).then_inc(s, 16)
            with sp.Fori(1, ROUNDS) as i:
                sp.wait_ge(*ln_done[0].at(i - 1))
                sp.wait_ge(*residual_biased[0].at(i - 1))
                load_round(i)
                sp.wait_ge(*middle.full("cv3", i - 1))
                sp.wait_ge(*scores_mul.at(i - 1, 2 * U - 1))
                load_cross(i)
            sp.wait_ge(w_mask, 16)

        @block.gpsimd
        def _(pool):
            pool.memset(ident[:, :], 0.0).then_inc(ident_step, 1)
            pool.memset(head_rows[:, :], 1.0).then_inc(ident_step, 1)
            pool.wait_ge(ident_step, 2)
            pool.affine_select(out=ident[:, :], in_=ident[:, :], compare_op=ALU.not_equal, fill=1.0, base=0,
                               pattern=[[-1, P]], channel_multiplier=1).then_inc(consts_made, 1)
            pool.affine_select(out=head_rows[:, :], in_=head_rows[:, :], compare_op=ALU.is_ge, fill=0.0, base=0,
                               pattern=[[-HD0, 8]], channel_multiplier=1).then_inc(ident_step, 1)
            pool.wait_ge(ident_step, 3)
            pool.affine_select(out=head_rows[:, :], in_=head_rows[:, :], compare_op=ALU.is_ge, fill=0.0,
                               base=HD0 - 1, pattern=[[HD0, 8]], channel_multiplier=-1).then_inc(head_rows_made, 1)
            pool.memset(half_neg[:, :], -0.5).then_inc(head_rows_made, 1)
            pool.memset(mean_w[:, :], 1.0 / P)
            pool.memset(eps[:, :], EPS).then_inc(head_rows_made, 1)
            pool.wait_ge(head_rows_made, 3)
            pool.wait_ge(w_consts, 32)

            def inverse_std(i, k):
                pool.wait_ge(*mean_var_done[k].at(i))
                pool.tensor_tensor(var_eps[:, :], mean_var[:, :, 1], eps[:, :], ALU.add)\
                    .then_inc(var_eps_done[k].sem, 1)
                pool.wait_ge(*var_eps_done[k].at(i))
                pool.tensor_tensor(rstd[:, :], var_eps[:, :], half_neg[:, 0:G], ALU.pow)\
                    .then_inc(rstd_done[k].sem, 1)

            def add_bias(i, k, dst, src, bias):
                pool.wait_ge(*ln_done[k].at(i))
                pool.tensor_tensor(dst[:, :, :], src[:, :, :], row(bias).unsqueeze(1).broadcast_to([P, G, D]),
                                   ALU.add).then_inc(residual_biased[k].sem, 1)

            def mask_keys(i, a, u):
                b, quad = divmod(u, QUAD)
                half, q = divmod(quad, 2)
                n = a * U + u
                if u == 0:
                    pool.wait_ge(*(entry.out("k1", i) if a == 0 else middle.out("ck1", i)))
                    if a == 1:
                        pool.wait_ge(*middle.out("ck0", i))
                pool.wait_ge(*scores_done.at(i, n - RK))
                pool.tensor_tensor(
                    km[:, n % RK, :].rearrange("p (h k) -> p h k", h=QUAD),
                    (kT, ckT)[a][:, half, b * P:(b + 1) * P].unsqueeze(1).broadcast_to([P, QUAD, P]),
                    head_rows[:, QUAD * q:QUAD * q + QUAD].unsqueeze(2).broadcast_to([P, QUAD, P]),
                    ALU.mult).then_inc(keys_masked.sem, 1)

            def norm(i, n):
                pool.wait_ge(*z_inv_done.at(i, n))
                p = ring_e[:, n % RE, :].rearrange("p (h k) -> p h k", h=QUAD)
                pool.tensor_tensor(p, p, z_inv[:, n % RE, :].unsqueeze(2).broadcast_to([P, QUAD, P]), ALU.mult)\
                    .then_inc(probs_done.sem, 1)

            def attend(i, a, last):
                for u in range(LEAD_K):
                    mask_keys(i, a, u)
                for t in range(STEPS):
                    if t + LEAD_K < U:
                        mask_keys(i, a, t + LEAD_K)
                    if 0 <= t - L_E < U:
                        norm(i, a * U + t - L_E)
                    if a == 1 and t == NORM_AT[0] and not last:
                        inverse_std(i + 1, 0)
                    if a == 0 and t == 1:
                        add_bias(i, 0, xr, xg, "bao")

            def body(i, first, last):
                attend(i, 0, last)
                inverse_std(i, 1)
                add_bias(i, 1, xr, xr, "bco")
                attend(i, 1, last)
                inverse_std(i, 2)
                if not first:
                    pool.wait_ge(*mlp.out("y3", i - 1))
                add_bias(i, 2, xm, xr, "b2")

            bodies(pool, lambda: inverse_std(0, 0), body, lambda i: None)

        @block.tensor
        def _(pe):
            def bank(name, i):
                banks = banks_of(name)
                pe.wait_ge(*banks.free(name, i))
                return banks.psum(name)

            def full(name, ins):
                ins.then_inc(banks_of(name).fills(name), 1)

            def norm_turn(i, k, c):
                name = f"T{k}h{c}"
                pe.wait_ge(*ln_done[k].at(i))
                ps = bank(name, i)
                for b in range(G):
                    last = nc.tensor.transpose(ps[:, b * P:(b + 1) * P], ln[:, b, c * P:(c + 1) * P], ident[:, :])
                full(name, last)

            def features_out(i, name, w, at, src):
                ps = bank(name, i)
                for c in range(2):
                    last = nc.tensor.matmul(ps, w[:, c, at:at + P], src[:, c, :], start=c == 0, stop=c == 1)
                full(name, last)

            def tokens_out(i, name, w, at, src, chunks, batches):
                ps = bank(name, i)
                for n, b in enumerate(batches):
                    for c in range(chunks):
                        last = nc.tensor.matmul(ps[:, n * D:(n + 1) * D], src[:, c, b * P:(b + 1) * P],
                                                w[:, c, at:at + D], start=c == 0, stop=c == chunks - 1)
                full(name, last)

            def work(name, i):
                m = int(name[-1])
                if name[0] == "T":
                    norm_turn(i, int(name[1]), m)
                elif name[0] == "q":
                    if m == 0:
                        pe.wait_ge(*entry.out("T0h1", i))
                    features_out(i, name, wqkv, m * P, lnT1)
                elif name[0] == "k":
                    features_out(i, name, wqkv, D + m * P, lnT1)
                elif name[0] == "v":
                    tokens_out(i, name, wqkv, 2 * D, lnT1, 2, [m])
                elif name[0:2] == "cq":
                    features_out(i, name, wq, m * P, lnT)
                elif name[0:2] == "ck":
                    if m == 0:
                        pe.wait_ge(*ctxT_in.at(i))
                    features_out(i, name, wkv, m * P, cT)
                elif name[0:2] == "cv":
                    tokens_out(i, name, wkv, D, cT, 2, [m])
                elif name[0] == "o":
                    tokens_out(i, name, wao, 0, oT, 2, [2 * m, 2 * m + 1])
                elif name[0:2] == "co":
                    tokens_out(i, name, wco, 0, oT, 2, [2 * m, 2 * m + 1])
                elif name[0] == "f":
                    if m == 0:
                        pe.wait_ge(*mlp.out("T2h1", i))
                    features_out(i, name, w1, m * P, lnT)
                else:
                    if m == 0:
                        pe.wait_ge(*h_gate.at(i, 7))
                    tokens_out(i, name, w2, 0, hid, F0 // P, [m])

            def scores(i, a, u):
                b, quad = divmod(u, QUAD)
                n = a * U + u
                pe.wait_ge(*keys_masked.at(i, n))
                pe.wait_ge(*scores_mul.at(i, n - 2))
                nc.tensor.matmul(score_bank[n % 2], (qT, cqT)[a][:, quad // 2, b * P:(b + 1) * P],
                                 km[:, n % RK, :], start=True, stop=True).then_inc(scores_done.sem, 1)

            def turn(i, n):
                pe.wait_ge(*probs_done.at(i, n))
                pe.wait_ge(*probsT_done.at(i, n - 1))
                for h in range(QUAD):
                    last = nc.tensor.transpose(turn_bank[:, h * P:(h + 1) * P],
                                               ring_e[:, n % RE, h * P:(h + 1) * P], ident[:, :])
                last.then_inc(turned.sem, 1)

            def times_v(i, a, u):
                b, quad = divmod(u, QUAD)
                half, q = divmod(quad, 2)
                n = a * U + u
                pe.wait_ge(*probsT_done.at(i, n))
                if q == 0:
                    if quad == 0:
                        pe.wait_ge(*(entry.out(f"v{b}", i) if a == 0 else middle.out(f"cv{b}", i)))
                    pe.wait_ge(*heads_out.at(i, n // 2 - 1))
                for h in range(QUAD):
                    j = QUAD * q + h
                    last = nc.tensor.matmul(pv_bank[:, 0:P], vm[:, b % 2, half, j * P:(j + 1) * P],
                                            ring_t[:, n % RT, h * P:(h + 1) * P], start=j == 0, stop=j == 7)
                last.then_inc(pv_done.sem, 1)

            def attend(i, a, first, last):
                for t in range(STEPS):
                    if t < U:
                        scores(i, a, t)
                    name, r = beside(i, a, t, first, last)
                    if name:
                        work(name, r)
                    if t >= L_V:
                        times_v(i, a, t - L_V)
                    if 0 <= t - L_T < U:
                        turn(i, a * U + t - L_T)

            def prologue():
                work("T0h0", 0)
                work("T0h1", 0)
                for name in ("q0", "q1", "k0", "k1", "v0"):
                    work(name, 0)
                pe.wait_ge(*entry.out("k1", 0))

            def body(i, first, last):
                pe.wait_ge(*entry.out("k1", i))
                attend(i, 0, first, last)
                pe.wait_ge(*heads_out.at(i, U // 2 - 1))
                for name in ("o0", "o1", "cv0", "T1h0", "T1h1"):
                    work(name, i)
                pe.wait_ge(*middle.out("T1h0", i))
                pe.wait_ge(*middle.out("T1h1", i))
                work("cq0", i)
                work("cq1", i)
                pe.wait_ge(*middle.out("cq0", i))
                pe.wait_ge(*middle.out("cq1", i))
                attend(i, 1, first, last)
                pe.wait_ge(*heads_out.at(i, U - 1))
                work("co0", i)
                work("co1", i)

            def epilogue(i):
                for name in mlp.place:
                    work(name, i - 1)

            pe.wait_ge(consts_made, 1)
            for s in (w_qkv, w_ao, w_kv, w_q, w_co, w_1, w_2):
                pe.wait_ge(s, 16)
            bodies(pe, prologue, body, epilogue)

        @block.scalar
        def _(act):
            def affine(i, name, dst, bias, scale):
                banks = banks_of(name)
                act.wait_ge(*banks.full(name, i))
                nc.scalar.activation(dst, banks.psum(name), ACT.Identity, bias=bias, scale=scale)\
                    .then_inc(banks.reads(name), 1)

            def hidden(i, f):
                act.wait_ge(*mlp.full(f"f{f}", i))
                act.wait_ge(*h_gate.at(i, f - 2))
                nc.scalar.activation(ring_h[:, f % 2, :], mlp.psum(f"f{f}"), ACT.Identity, bias=col("b1", f))\
                    .then_inc(h_lin.sem, 1)
                nc.scalar.activation(ring_g[:, f % 2, :], mlp.psum(f"f{f}"), ACT.Square, bias=col("b1", f))\
                    .then_inc(mlp.reads(f"f{f}"), 1)

            def gate(i, f):
                act.wait_ge(*h_arg.at(i, f))
                t = ring_g[:, f % 2, :]
                nc.scalar.activation(t, t, ACT.Tanh, scale=0.7978845608028654).then_inc(h_tanh.sem, 1)

            def work(name, i):
                m = int(name[-1])
                scale = HD0 ** -0.5
                if name[0] == "T":
                    k = int(name[1])
                    affine(i, name, (lnT1 if k == 0 else lnT)[:, m, :], col("ln_b", 2 * k + m),
                           col("ln_s", 2 * k + m))
                elif name[0] == "q":
                    affine(i, name, qT[:, m, :], bq_scaled[:, m:m + 1], scale)
                elif name[0] == "k":
                    affine(i, name, kT[:, m, :], col("bk0", m), 1.0)
                elif name[0:2] == "cq":
                    affine(i, name, cqT[:, m, :], bq_scaled[:, 2 + m:3 + m], scale)
                elif name[0:2] == "ck":
                    affine(i, name, ckT[:, m, :], col("bck", m), 1.0)
                elif name[0] == "f":
                    hidden(i, m)
                    if m >= 1:
                        gate(i, m - 1)

            def exponentials(i, n):
                act.wait_ge(*max_done.at(i, n))
                for h in range(QUAD):
                    e = ring_e[:, n % RE, h * P:(h + 1) * P]
                    last = nc.scalar.activation(e, e, ACT.Exp, bias=neg_max[:, n % RE, h:h + 1],
                                                accum_out=z_sum[:, n % RE, h:h + 1])
                last.then_inc(exp_done.sem, 1)

            def copy_turned(i, n):
                act.wait_ge(*turned.at(i, n))
                act.wait_ge(*pv_done.at(i, n - RT))
                nc.scalar.copy(ring_t[:, n % RT, :], turn_bank).then_inc(probsT_done.sem, 1)

            def copy_heads(i, a, u):
                b, quad = divmod(u, QUAD)
                act.wait_ge(*pv_done.at(i, a * U + u))
                nc.scalar.copy(oT[:, quad // 2, b * P:(b + 1) * P], pv_bank[:, 0:P]).then_inc(heads_out.sem, 1)

            def attend(i, a, first, last):
                for t in range(STEPS):
                    if 0 <= t - L_E < U:
                        exponentials(i, a * U + t - L_E)
                    if 0 <= t - L_P < U:
                        copy_turned(i, a * U + t - L_P)
                    name, r = beside(i, a, t, first, last)
                    if name:
                        work(name, r)
                        if name == "f7":
                            gate(r, 7)
                    if t >= L_V and (t - L_V) % 2 == 1:
                        copy_heads(i, a, t - L_V)

            def prologue():
                for name in ("T0h0", "T0h1", "q0", "q1", "k0", "k1"):
                    work(name, 0)

            def body(i, first, last):
                attend(i, 0, first, last)
                for name in ("T1h0", "T1h1", "cq0", "cq1"):
                    work(name, i)
                attend(i, 1, first, last)

            def epilogue(i):
                for name in ["T2h0", "T2h1"] + [f"f{f}" for f in range(8)]:
                    work(name, i - 1)
                gate(i - 1, 7)

            act.wait_ge(w_consts, 32)
            act.wait_ge(dve_consts, 1)
            bodies(act, prologue, body, epilogue)

        @block.vector
        def _(dve):
            def statistics(i, k, src):
                for b in range(G):
                    last = nc.vector.bn_stats(stats[:, b, :], src[:, b, :])
                last.then_inc(stats_done[k].sem, 1)
                dve.wait_ge(*stats_done[k].at(i))
                nc.vector.tensor_copy(first_stat[:, :], stats[:, 0, 0:1])
                for b in range(G):
                    last = nc.vector.bn_aggr(mean_var[:, b, :], stats[:, b, :])
                last.then_inc(mean_var_done[k].sem, 1)

            def normalise(i, k, src):
                dve.wait_ge(*rstd_done[k].at(i))
                for b in range(G):
                    last = nc.vector.tensor_scalar(ln[:, b, :], src[:, b, :], mean_var[:, b, 0:1], rstd[:, b:b + 1],
                                                   ALU.subtract, ALU.mult)
                last.then_inc(ln_done[k].sem, 1)

            def spread_values(i, name, bias):
                banks = banks_of(name)
                b = int(name[-1])
                dve.wait_ge(*banks.full(name, i))
                dst = vm[:, b % 2, :, :].rearrange("p c (j w) -> p c j w", w=VSTEP)[:, :, :, 0:HD0]
                nc.vector.tensor_tensor(
                    dst, banks.psum(name)[:, 0:D].rearrange("p (c j w) -> p c j w", c=2, w=HD0),
                    row(bias).rearrange("p (c j w) -> p c j w", c=2, w=HD0), ALU.add).then_inc(banks.reads(name), 1)

            def add_product(i, name):
                b = 2 * int(name[-1])
                dve.wait_ge(*middle.full(name, i))
                x = xr[:, b:b + 2, :].rearrange("p b d -> p (b d)")
                nc.vector.tensor_tensor(x, middle.psum(name), x, ALU.add).then_inc(middle.reads(name), 1)

            def polynomial(i, f):
                t, h = ring_g[:, f % 2, :], ring_h[:, f % 2, :]
                dve.wait_ge(*mlp.out(f"f{f}", i))
                nc.vector.tensor_scalar(t, t, 0.044715, 1.0, ALU.mult, ALU.add).then_inc(h_poly.sem, 1)
                dve.wait_ge(*h_poly.at(i, f))
                nc.vector.tensor_tensor(t, t, h, ALU.mult).then_inc(h_arg.sem, 1)

            def gated(i, f):
                dve.wait_ge(*h_tanh.at(i, f))
                nc.vector.scalar_tensor_tensor(out=hid[:, f, :], in0=ring_g[:, f % 2, :], scalar=1.0,
                                               in1=ring_h[:, f % 2, :], op0=ALU.add, op1=ALU.mult)\
                    .then_inc(h_gate.sem, 1)

            def output(i, b):
                name = f"y{b}"
                dve.wait_ge(*mlp.full(name, i))
                if b == 0:
                    dve.wait_ge(*residual_biased[2].at(i))
                nc.vector.scalar_tensor_tensor(out=xs[:, bass.ds(i * G + b, 1), :].rearrange("p a d -> p (a d)"),
                                               in0=mlp.psum(name)[:, 0:D], scalar=0.5, in1=xm[:, b, :],
                                               op0=ALU.mult, op1=ALU.add).then_inc(mlp.reads(name), 1)

            def work(name, i):
                m = int(name[-1])
                if name[0] == "v":
                    spread_values(i, name, "bv0")
                elif name[0:2] == "cv":
                    spread_values(i, name, "bcv")
                elif name[0] == "f":
                    polynomial(i, m)
                    if m >= 1:
                        gated(i, m - 1)
                elif name[0] == "y":
                    if m == 0:
                        gated(i, 7)
                    output(i, m)

            def attend(i, a, first, last):
                def mask(t, u):
                    if a == 0:
                        return t[0][:, :].unsqueeze(1).broadcast_to([P, QUAD, P])
                    return t[1][:, u // QUAD, :].unsqueeze(1).broadcast_to([P, QUAD, P])

                for t in range(STEPS):
                    n = a * U + t
                    if t < U:
                        e = ring_e[:, n % RE, :].rearrange("p (h k) -> p h k", h=QUAD)
                        dve.wait_ge(*scores_done.at(i, n))
                        dve.wait_ge(*turned.at(i, n - RE))
                        nc.vector.tensor_tensor(e, score_bank[n % 2].rearrange("p (h k) -> p h k", h=QUAD),
                                                mask((self_mul, cross_mul), t), ALU.mult).then_inc(scores_mul.sem, 1)
                    if 0 <= t - L_E < U:
                        m = n - L_E
                        dve.wait_ge(*exp_done.at(i, m))
                        nc.vector.reciprocal(z_inv[:, m % RE, :], z_sum[:, m % RE, :]).then_inc(z_inv_done.sem, 1)
                    if t < U:
                        dve.wait_ge(*scores_mul.at(i, n))
                        nc.vector.tensor_tensor(e, e, mask((self_add, cross_add), t), ALU.add)\
                            .then_inc(scores_add.sem, 1)
                        dve.wait_ge(*scores_add.at(i, n))
                        nc.vector.tensor_reduce(neg_max[:, n % RE, :], e, AX.X, ALU.max, negate=True)\
                            .then_inc(max_done.sem, 1)
                    name, r = beside(i, a, t, first, last)
                    if name:
                        work(name, r)
                    if a == 1 and not last:
                        if t == NORM_AT[0]:
                            dve.wait_ge(*input_in.at(i + 1))
                            statistics(i + 1, 0, xg)
                        if t == NORM_AT[1]:
                            normalise(i + 1, 0, xg)

            def prologue():
                dve.wait_ge(*input_in.at(0))
                statistics(0, 0, xg)
                normalise(0, 0, xg)
                work("v0", 0)

            def body(i, first, last):
                attend(i, 0, first, last)
                dve.wait_ge(*residual_biased[0].at(i))
                add_product(i, "o0")
                add_product(i, "o1")
                dve.wait_ge(*middle.out("o0", i))
                dve.wait_ge(*middle.out("o1", i))
                statistics(i, 1, xr)
                dve.wait_ge(*cross_mask_in.at(i))
                nc.vector.tensor_scalar(cross_add[:, :, :], cross_mul[:, :, :], -1.0, 10000.0, ALU.add, ALU.mult)\
                    .then_inc(cross_add_made.sem, 1)
                normalise(i, 1, xr)
                work("cv0", i)
                dve.wait_ge(*cross_add_made.at(i))
                attend(i, 1, first, last)
                dve.wait_ge(*residual_biased[1].at(i))
                add_product(i, "co0")
                add_product(i, "co1")
                dve.wait_ge(*middle.out("co0", i))
                dve.wait_ge(*middle.out("co1", i))
                statistics(i, 2, xr)
                normalise(i, 2, xr)

            def epilogue(i):
                for name in [f"f{f}" for f in range(8)] + [f"y{b}" for b in range(G)]:
                    work(name, i - 1)

            dve.memset(vm[:, :, :, :], 0.0)
            dve.wait_ge(w_mask, 16)
            nc.vector.tensor_scalar(self_add[:, :], self_mul[:, :], -1.0, 10000.0, ALU.add, ALU.mult)
            dve.wait_ge(w_consts, 32)
            nc.vector.tensor_scalar(bq_scaled[:, 0:2], col("bq0", 0, 2), HD0 ** -0.5, None, ALU.mult)
            nc.vector.tensor_scalar(bq_scaled[:, 2:4], col("bcq", 0, 2), HD0 ** -0.5, None, ALU.mult)\
                .then_inc(dve_consts, 1)
            dve.wait_ge(dve_consts, 1)
            bodies(dve, prologue, body, epilogue)


def layer1(nc, v):
    (sb_, psum, xs, ident, mean_w, half_neg, col) = (v[n] for n in (
        "sb", "psum", "xs", "ident", "mean_w", "half_neg", "col"))
    NB = 2
    R1 = B // NB
    UNITS = H1 * NB
    NQ = H1 * HD1
    RE, RT = 4, 2
    L_E, L_T, L_P, L_V, L_O, L_W = 1, 2, 3, 4, 5, 1
    SCALE = HD1 ** -0.5
    with ExitStack() as ctx:
        def sb(name, shape, dt=F32):
            return ctx.enter_context(nc.sbuf_tensor(name, shape, dt))

        def sem(name):
            return ctx.enter_context(nc.semaphore(name))

        events = []

        def event(name, per, unit=1):
            e = Event(ctx, nc, "l1_" + name, per, unit)
            events.append(e)
            return e

        wz = [sb(f"wz{p}", [P, 2, 3 * NQ], F32R) for p in ("h", "l")]
        wi = [sb(f"wi{p}", [P, 2, 3 * NQ], F32R) for p in ("h", "l")]
        wo = [sb(f"wo{p}", [P, H1, P], F32R) for p in ("h", "l")]
        zu = [sb(f"zu{p}", [P, 2, 2, NB, P], F32R) for p in ("h", "l")]
        q = [sb(f"q{p}", [P, 2, 2, 2, NB, P], F32R) for p in ("h", "l")]
        k = [sb(f"k{p}", [P, 2, 2, NB, P], F32R) for p in ("h", "l")]
        vs = sb("vs", [P, 2, NB, 2, 4, 2, HD1], F32R)
        STAGE = 3 * NQ // 2
        plain = sb("plain", [P, RE * BANK + 3 * NB * D])
        stage = plain[:, 0:2 * STAGE].rearrange("p (s n) -> p s n", s=2)
        prob = plain[:, 0:RE * BANK].rearrange("p (s n) -> p s n", s=RE)
        ub, y, ysq = (plain[:, RE * BANK + j * NB * D:RE * BANK + (j + 1) * NB * D].rearrange(
            "p (b d) -> p b d", b=NB) for j in range(3))
        pT = [sb(f"pT{p}", [P, RT, BANK], F32R) for p in ("h", "l")]
        aT = [sb(f"aT{p}", [P, RT, D], F32R) for p in ("h", "l")]
        neg_max = sb("l1_neg_max", [P, RE, 2])
        z_sum = sb("l1_z_sum", [P, RE, 2])
        z_inv = sb("l1_z_inv", [P, RE, 2])
        var_eps = sb("l1_var_eps", [P, 4])
        rstd = sb("l1_rstd", [P, 4])
        diag = ysq.rearrange("p b (h c) -> p (b h) c", h=2)

        score_bank = [psum[:, j, :] for j in range(2)]
        turn_bank = [psum[:, 2 + j, :] for j in range(2)]
        pv_bank = psum[:, 4, :]
        wo_bank = [psum[:, 7, b * D:(b + 1) * D] for b in range(NB)]

        with ExitStack() as c2:
            staged = c2.enter_context(nc.semaphore("weights_staged"))
            staged1 = c2.enter_context(nc.semaphore("weights_staged_odd"))
            hi_made = c2.enter_context(nc.semaphore("weights_hi_made"))
            lo_made = c2.enter_context(nc.semaphore("weights_lo_made"))
            chunks = [(src, pair, c, h) for src, pair in (("wz_in", wz), ("wi_in", wi)) for c in range(2)
                      for h in range(2)]
            landed = [staged, staged1]

            def views(n):
                src, pair, c, h = chunks[n]
                return [w[:, c, h * STAGE:(h + 1) * STAGE] for w in pair]

            block = c2.enter_context(nc.Block())

            @block.sync
            def _(sp):
                for n, (src, pair, c, h) in enumerate(chunks):
                    if n >= 2:
                        sp.wait_ge(lo_made, n - 1)
                    sp.dma_start(stage[:, n % 2, :], v[src].rearrange("(c p) n -> p c n", p=P)[
                        :, c, h * STAGE:(h + 1) * STAGE]).then_inc(landed[n % 2], 16)
                for g in range(2):
                    n = len(chunks) + g
                    sp.wait_ge(lo_made, n - 1)
                    src = v["wo_in"].rearrange("(h r) o -> r h o", r=HD1)[:, g * 8:(g + 1) * 8, :]
                    for half in range(2):
                        sp.dma_start(stage[half * HD1:(half + 1) * HD1, n % 2, 0:8 * P].rearrange(
                            "p (h o) -> p h o", h=8), src).then_inc(landed[n % 2], 16)

            def arrived(n):
                done = n // 2 + 1
                return landed[n % 2], 16 * (done if n < len(chunks) else done + 1)

            def parts(n):
                if n < len(chunks):
                    return stage[:, n % 2, :], *views(n)
                g = n - len(chunks)
                return (stage[:, n % 2, 0:8 * P], *(w[:, g * 8:(g + 1) * 8, :].rearrange("p h o -> p (h o)")
                                                    for w in wo))

            @block.scalar
            def _(act):
                for n in range(len(chunks) + 2):
                    src, hi, lo = parts(n)
                    act.wait_ge(*arrived(n))
                    nc.scalar.copy(hi, src).then_inc(hi_made, 1)

            @block.vector
            def _(dve):
                for n in range(len(chunks) + 2):
                    src, hi, lo = parts(n)
                    dve.wait_ge(hi_made, n + 1)
                    nc.vector.tensor_tensor(lo, src, hi.bitcast(F32), ALU.subtract).then_inc(lo_made, 1)

        names = ["q0", "k0", "v0b0", "v0b1", "q1", "k1", "q2", "k2", "v1b0", "v1b1", "q3", "k3", "mean", "var",
                 "q4", "k4", "v2b0", "v2b1", "q5", "k5", "inv0", "inv1", "q6", "k6", "v3b0", "v3b1",
                 "q7", "k7"]
        made = [n for n in names if n[0] in "qkv" and n != "var"]
        work = Banks(ctx, nc, "l1_work", names, [psum[:, 5 + j, :] for j in range(2)])
        events += work.full_ev + work.out_ev
        work_hi = event("work_hi", len(made))
        u_in = event("u_in", 1, 16)
        zu_hi = event("zu_hi", 2)
        zu_lo = event("zu_lo", 2)
        scores_done = event("scores_done", UNITS)
        max_done = event("max_done", UNITS)
        exp_done = event("exp_done", UNITS)
        z_inv_done = event("z_inv_done", UNITS)
        probs_done = event("probs_done", UNITS)
        turned = event("turned", UNITS)
        pT_hi = event("pT_hi", UNITS)
        pT_lo = event("pT_lo", UNITS)
        pv_done = event("pv_done", UNITS)
        aT_hi = event("aT_hi", UNITS)
        aT_lo = event("aT_lo", UNITS)
        wo_done = event("wo_done", UNITS)
        y_done = event("y_done", 1)
        centred = event("centred", 1)
        squared = event("squared", 1)
        rstd_done = event("rstd_done", 1)
        diagonal = event("diagonal", 1)
        zeroed = sem("l1_zeroed")

        def unit(n):
            n %= UNITS
            return n // 4, n % 4 // 2, n % 2

        def work_at(t):
            s, r = divmod(t, 4)
            nxt = (s + 1) % 8
            if r < 2:
                return "qk"[r] + str(nxt), int(s == 7)
            return (f"v{nxt // 2}b{r - 2}", int(s == 7)) if s % 2 == 1 else (None, 0)

        T_Y, T_MEAN, T_VAR, T_INV, T_ZU = L_O, 10, 11, 18, 26

        def work_to_round(i, t, last):
            n = t - L_W
            name, ahead = work_at(n % UNITS)
            ahead += -1 if n < 0 else 0
            return (name, i + ahead) if name and not (last and ahead == 1) else (None, 0)

        def tile_of(name):
            slot = int(name[1]) % 2
            if name[0] == "q":
                return [[(w[h * HD1:(h + 1) * HD1, slot, h, :, :, :].rearrange("p c b l -> p (c b l)"))
                         for w in q] for h in range(2)]
            if name[0] == "k":
                return [w[:, slot, :, :, :].rearrange("p c b l -> p (c b l)") for w in k]
            d = vs[:, slot, int(name[3]), :, :, :, :].rearrange("p c h s f -> p (c h) s f")
            return [d[:, :, s, :] for s in range(2)]

        def work_psum(name):
            ps = work.psum(name)
            return ps if name[0] != "v" else ps.rearrange("p (c f) -> p c f", f=HD1)

        def rounds(eng, body, tail):
            body(0, first=True, last=False)
            with eng.Fori(1, R1 - 1) as i:
                body(i, first=False, last=False)
            body(R1 - 1, first=False, last=True)
            tail(R1)

        block = ctx.enter_context(nc.Block())

        @block.sync
        def _(sp):
            for e in events:
                sp.nop().then_inc(e.sem, e.per)

            def load_u(i):
                sp.dma_start(ub[:, :, :], v["ctx_in"].rearrange("b p d -> p b d")[:, bass.ds(i * NB, NB), :])\
                    .then_inc(u_in.sem, 16)

            load_u(0)
            with sp.Fori(1, R1) as i:
                sp.wait_ge(*zu_lo.at(i - 1, 1))
                load_u(i)

        @block.gpsimd
        def _(pool):
            def norm(i, n):
                pool.wait_ge(*z_inv_done.at(i, n))
                e = prob[:, n % RE, :].rearrange("p (t c) -> p t c", t=2)
                pool.tensor_tensor(e, e, z_inv[:, n % RE, :].unsqueeze(2).broadcast_to([P, 2, D]), ALU.mult)\
                    .then_inc(probs_done.sem, 1)

            def inverse_std(i, name):
                pool.wait_ge(*work.out(name, i))
                pool.tensor_tensor(rstd[:, :], var_eps[:, :], half_neg[:, 0:4], ALU.pow).then_inc(rstd_done.sem, 1)

            def body(i, first, last):
                for t in range(UNITS):
                    if t >= L_E or not first:
                        norm(i, t - L_E)
                    if t == T_VAR + 1:
                        inverse_std(i, "var")

            def tail(i):
                for t in range(L_E):
                    norm(i, t - L_E)
                inverse_std(i, "k0")

            pool.memset(q[0][:, :, :, :, :, :].bitcast(F32), 0.0).then_inc(zeroed, 1)
            pool.memset(q[1][:, :, :, :, :, :].bitcast(F32), 0.0).then_inc(zeroed, 1)
            rounds(pool, body, tail)

        @block.tensor
        def _(pe):
            mm = nc.tensor.matmul

            def project(i, name):
                ps = work.psum(name)
                pe.wait_ge(*work.free(name, i))
                pe.wait_ge(*zu_lo.at(i, 1))
                for c in range(2):
                    o = ps[:, c * D:(c + 1) * D]
                    for s, w in enumerate((wz, wi)):
                        for wp, xp in ((0, 0), (0, 1), (1, 0)):
                            flags = {"start": (s, wp, xp) == (0, 0, 0), "stop": (s, wp, xp) == (1, 1, 0)}
                            if name[0] in "qk":
                                at = "qk".index(name[0]) * NQ + int(name[1]) * P
                                last = mm(o, w[wp][:, c, at:at + P],
                                          zu[xp][:, s, c, :, :].rearrange("p b l -> p (b l)"), **flags)
                            else:
                                at = 2 * NQ + int(name[1]) * D
                                last = mm(o, zu[xp][:, s, c, int(name[3]), :], w[wp][:, c, at:at + D], **flags)
                last.then_inc(work.fills(name), 1)

            def scores(i, n):
                pair, h, b = unit(n)
                if n % 4 == 0:
                    pe.wait_ge(*work.out(f"q{pair}", i))
                    pe.wait_ge(*work.out(f"k{pair}", i))
                pe.wait_ge(*exp_done.at(i, n - 2))
                for qt in range(2):
                    for qp, kp in ((0, 0), (0, 1), (1, 0)):
                        last = mm(score_bank[n % 2][:, qt * D:(qt + 1) * D], q[qp][:, pair % 2, h, qt, b, :],
                                  k[kp][:, pair % 2, :, b, :], start=(qp, kp) == (0, 0), stop=(qp, kp) == (1, 0))
                last.then_inc(scores_done.sem, 1)

            def turn(i, n):
                pe.wait_ge(*probs_done.at(i, n))
                pe.wait_ge(*pT_lo.at(i, n - 2))
                for qt in range(2):
                    for kt in range(2):
                        last = nc.tensor.transpose(turn_bank[n % 2][:, kt * D + qt * P:kt * D + (qt + 1) * P],
                                                   prob[:, n % RE, qt * D + kt * P:qt * D + (kt + 1) * P],
                                                   ident[:, :])
                last.then_inc(turned.sem, 1)

            def times_v(i, n):
                pair, h, b = unit(n)
                if n % 8 == 0:
                    pe.wait_ge(*work.out(f"v{pair // 2}b0", i))
                    pe.wait_ge(*work.out(f"v{pair // 2}b1", i))
                pe.wait_ge(*pT_lo.at(i, n))
                pe.wait_ge(*aT_lo.at(i, n - 1))
                for kt in range(2):
                    w = vs[:, pair // 2 % 2, b, kt, 2 * (pair % 2) + h, :, :].rearrange("p s f -> p (s f)")
                    for pp in range(2):
                        last = mm(pv_bank[:, 0:D], w, pT[pp][:, n % RT, kt * D:(kt + 1) * D],
                                  start=(kt, pp) == (0, 0), stop=(kt, pp) == (1, 1))
                last.then_inc(pv_done.sem, 1)

            def times_wo(i, n):
                pair, h, b = unit(n)
                head = 2 * pair + h
                pe.wait_ge(*aT_lo.at(i, n))
                if head == 0:
                    pe.wait_ge(*y_done.at(i))
                for wp, ap in ((0, 0), (0, 1), (1, 0)):
                    last = mm(wo_bank[b], wo[wp][:, head, :], aT[ap][:, n % RT, :],
                              start=(head, b, wp, ap) == (0, 0, 0, 0),
                              stop=head == H1 - 1 and (wp, ap) == (1, 0), skip_group_check=True)
                last.then_inc(wo_done.sem, 1)

            def mean(i, name):
                pe.wait_ge(*work.free(name, i))
                pe.wait_ge(*y_done.at(i))
                mm(work.psum(name), mean_w[:, :], y[:, :, :].rearrange("p b d -> p (b d)"),
                   start=True, stop=True).then_inc(work.fills(name), 1)

            def variance(i, name):
                pe.wait_ge(*work.free(name, i))
                pe.wait_ge(*squared.at(i))
                for j in range(4):
                    last = mm(work.psum(name)[:, j:j + 1], ysq[:, j // 2, j % 2 * P:(j % 2 + 1) * P],
                              mean_w[:, 0:1], start=True, stop=True)
                last.then_inc(work.fills(name), 1)

            def spread(i, name, b):
                pe.wait_ge(*work.free(name, i))
                pe.wait_ge(*diagonal.at(i))
                for j in range(2):
                    last = mm(work.psum(name)[:, j * P:(j + 1) * P], mean_w[:, :],
                              diag[:, 2 * b + j, :], start=True, stop=True)
                last.then_inc(work.fills(name), 1)

            def body(i, first, last):
                for t in range(UNITS):
                    scores(i, t)
                    if t >= L_V or not first:
                        times_v(i, t - L_V)
                    if t >= L_O or not first:
                        times_wo(i, t - L_O)
                    name, ahead = work_at(t)
                    if name and not (last and ahead):
                        project(i + ahead, name)
                    if t == T_MEAN:
                        mean(i, "mean")
                    if t == T_VAR:
                        variance(i, "var")
                    if t in (T_INV, T_INV + 1):
                        spread(i, f"inv{t - T_INV}", t - T_INV)
                    if t >= L_T or not first:
                        turn(i, t - L_T)

            def tail(i):
                for t in range(L_O):
                    if t < L_V:
                        times_v(i, t - L_V)
                    times_wo(i, t - L_O)
                    if t < L_T:
                        turn(i, t - L_T)
                mean(i, "q0")
                variance(i, "k0")
                spread(i, "v0b0", 0)
                spread(i, "v0b1", 1)

            pe.wait_ge(zeroed, 2)
            for name in names[:4]:
                project(0, name)
            rounds(pe, body, tail)

        @block.scalar
        def _(act):
            def exponentials(i, n):
                act.wait_ge(*max_done.at(i, n))
                act.wait_ge(*turned.at(i, n - RE))
                for qt in range(2):
                    last = nc.scalar.activation(prob[:, n % RE, qt * D:(qt + 1) * D],
                                                score_bank[n % 2][:, qt * D:(qt + 1) * D], ACT.Exp,
                                                bias=neg_max[:, n % RE, qt:qt + 1],
                                                accum_out=z_sum[:, n % RE, qt:qt + 1])
                last.then_inc(exp_done.sem, 1)

            def round_probs(i, n):
                act.wait_ge(*turned.at(i, n))
                act.wait_ge(*pv_done.at(i, n - RT))
                nc.scalar.copy(pT[0][:, n % RT, :], turn_bank[n % 2]).then_inc(pT_hi.sem, 1)

            def round_heads(i, n):
                act.wait_ge(*pv_done.at(i, n))
                act.wait_ge(*wo_done.at(i, n - RT))
                nc.scalar.copy(aT[0][:, n % RT, :], pv_bank[:, 0:D]).then_inc(aT_hi.sem, 1)

            def round_work(i, name):
                act.wait_ge(*work.full(name, i))
                tile, ps = tile_of(name), work_psum(name)
                if name[0] == "q":
                    for h in range(2):
                        at = slice(h * HD1, (h + 1) * HD1)
                        last = nc.scalar.activation(tile[h][0], ps[at, :], ACT.Identity,
                                                    bias=col("rwb", int(name[1]))[at, :])
                elif name[0] == "k":
                    last = nc.scalar.activation(tile[0], ps, ACT.Identity, scale=SCALE)
                else:
                    last = nc.scalar.copy(tile[0], ps)
                last.then_inc(work_hi.sem, 1)

            def round_inputs(i):
                if not isinstance(i, int) or i > 0:
                    act.wait_ge(*work.full("k7", i - 1))
                nc.scalar.copy(zu[0][:, 0, :, :, :], xs[:, bass.ds(i * NB, NB), :].rearrange(
                    "p b (c l) -> p c b l", c=2)).then_inc(zu_hi.sem, 1)
                act.wait_ge(*u_in.at(i))
                nc.scalar.copy(zu[0][:, 1, :, :, :], ub[:, :, :].rearrange("p b (c l) -> p c b l", c=2))\
                    .then_inc(zu_hi.sem, 1)

            def body(i, first, last):
                for t in range(UNITS):
                    if t >= L_E or not first:
                        exponentials(i, t - L_E)
                    if t >= L_P or not first:
                        round_probs(i, t - L_P)
                    name, r = work_to_round(i, t, last)
                    if name and (t >= L_W or not first):
                        round_work(r, name)
                    if t >= L_V or not first:
                        round_heads(i, t - L_V)
                    if t == T_ZU and not last:
                        round_inputs(i + 1)

            def tail(i):
                for t in range(L_V):
                    if t < L_E:
                        exponentials(i, t - L_E)
                    if t < L_P:
                        round_probs(i, t - L_P)
                    round_heads(i, t - L_V)

            round_inputs(0)
            act.wait_ge(zeroed, 2)
            for name in names[:4]:
                round_work(0, name)
            rounds(act, body, tail)

        @block.vector
        def _(dve):
            def maxima(i, n):
                dve.wait_ge(*scores_done.at(i, n))
                dve.wait_ge(*exp_done.at(i, n - RE))
                nc.vector.tensor_reduce(neg_max[:, n % RE, :], score_bank[n % 2].rearrange("p (t c) -> p t c", t=2),
                                        AX.X, ALU.max, negate=True).then_inc(max_done.sem, 1)

            def inverse_sums(i, n):
                dve.wait_ge(*exp_done.at(i, n))
                dve.wait_ge(*probs_done.at(i, n - RE))
                nc.vector.reciprocal(z_inv[:, n % RE, :], z_sum[:, n % RE, :]).then_inc(z_inv_done.sem, 1)

            def rest_probs(i, n):
                dve.wait_ge(*pT_hi.at(i, n))
                nc.vector.tensor_tensor(pT[1][:, n % RT, :], turn_bank[n % 2], pT[0][:, n % RT, :].bitcast(F32),
                                        ALU.subtract).then_inc(pT_lo.sem, 1)

            def rest_heads(i, n):
                dve.wait_ge(*aT_hi.at(i, n))
                nc.vector.tensor_tensor(aT[1][:, n % RT, :], pv_bank[:, 0:D], aT[0][:, n % RT, :].bitcast(F32),
                                        ALU.subtract).then_inc(aT_lo.sem, 1)

            def rest_work(i, name):
                dve.wait_ge(*work_hi.at(i, made.index(name)))
                tile, ps = tile_of(name), work_psum(name)
                if name[0] == "q":
                    for h in range(2):
                        at = slice(h * HD1, (h + 1) * HD1)
                        hi, lo = tile[h]
                        last = nc.vector.scalar_tensor_tensor(
                            out=lo, in0=ps[at, :], scalar=col("rwb", int(name[1]))[at, :], in1=hi.bitcast(F32),
                            op0=ALU.add, op1=ALU.subtract)
                elif name[0] == "k":
                    last = nc.vector.scalar_tensor_tensor(out=tile[1], in0=ps, scalar=SCALE,
                                                          in1=tile[0].bitcast(F32), op0=ALU.mult, op1=ALU.subtract)
                else:
                    last = nc.vector.tensor_tensor(tile[1], ps, tile[0].bitcast(F32), ALU.subtract)
                last.then_inc(work.reads(name), 1)

            def rest_inputs(i):
                dve.wait_ge(*zu_hi.at(i, 0))
                z = xs[:, bass.ds(i * NB, NB), :].rearrange("p b (c l) -> p c b l", c=2)
                nc.vector.tensor_tensor(zu[1][:, 0, :, :, :], z, zu[0][:, 0, :, :, :].bitcast(F32), ALU.subtract)\
                    .then_inc(zu_lo.sem, 1)
                dve.wait_ge(*zu_hi.at(i, 1))
                nc.vector.tensor_tensor(zu[1][:, 1, :, :, :], ub[:, :, :].rearrange("p b (c l) -> p c b l", c=2),
                                        zu[0][:, 1, :, :, :].bitcast(F32), ALU.subtract).then_inc(zu_lo.sem, 1)

            def residual(i):
                dve.wait_ge(*wo_done.at(i, -1))
                for b in range(NB):
                    last = nc.vector.scalar_tensor_tensor(
                        out=y[:, b, :], in0=wo_bank[b], scalar=col("bo"),
                        in1=xs[:, bass.ds((i - 1) * NB + b, 1), :].rearrange("p a d -> p (a d)"),
                        op0=ALU.add, op1=ALU.add)
                last.then_inc(y_done.sem, 1)

            def centre(i, name):
                dve.wait_ge(*work.full(name, i))
                yy = y[:, :, :].rearrange("p b d -> p (b d)")
                nc.vector.tensor_tensor(yy, yy, work.psum(name), ALU.subtract)\
                    .then_inc(work.reads(name), 1)
                dve.wait_ge(*work.out(name, i))
                nc.vector.tensor_tensor(ysq[:, :, :], y[:, :, :], y[:, :, :], ALU.mult).then_inc(squared.sem, 1)

            def read_variance(i, name):
                dve.wait_ge(*work.full(name, i))
                nc.vector.tensor_scalar(var_eps[:, :], work.psum(name)[:, 0:4], EPS, None, ALU.add)\
                    .then_inc(work.reads(name), 1)

            def make_diagonal(i):
                dve.wait_ge(*rstd_done.at(i))
                for j in range(4):
                    last = nc.vector.tensor_scalar(diag[:, j, :], ident[:, :], rstd[:, j:j + 1], float(P),
                                                   ALU.mult, ALU.mult)
                last.then_inc(diagonal.sem, 1)

            def output(i, name, b, first=False):
                dve.wait_ge(*work.full(name, i))
                ps = work.psum(name)[:, 0:D]
                to = y[:, b, :] if first else xs[:, bass.ds((i - 1) * NB + b, 1), :].rearrange("p a d -> p (a d)")
                nc.vector.tensor_tensor(to, y[:, b, :], ps, ALU.mult).then_inc(work.reads(name), 1)

            def body(i, first, last):
                for t in range(UNITS):
                    maxima(i, t)
                    if t >= L_E or not first:
                        inverse_sums(i, t - L_E)
                    if t >= L_P or not first:
                        rest_probs(i, t - L_P)
                    name, r = work_to_round(i, t, last)
                    if name and (t >= L_W or not first):
                        rest_work(r, name)
                    if t == T_Y:
                        if first:
                            nc.vector.memset(y[:, :, :], 0.0).then_inc(y_done.sem, 1)
                        else:
                            residual(i)
                    if t >= L_V or not first:
                        rest_heads(i, t - L_V)
                    if t == T_MEAN:
                        centre(i, "mean")
                    if t == T_VAR:
                        read_variance(i, "var")
                    if t == T_VAR + 2:
                        make_diagonal(i)
                    if t in (T_INV, T_INV + 1):
                        output(i, f"inv{t - T_INV}", t - T_INV, first)
                    if t == T_ZU and not last:
                        rest_inputs(i + 1)

            def tail(i):
                for t in range(L_V):
                    if t < L_E:
                        inverse_sums(i, t - L_E)
                    if t < L_P:
                        rest_probs(i, t - L_P)
                    rest_heads(i, t - L_V)
                residual(i)
                centre(i, "q0")
                read_variance(i, "k0")
                make_diagonal(i)
                output(i, "v0b0", 0)
                output(i, "v0b1", 1)

            rest_inputs(0)
            dve.wait_ge(zeroed, 2)
            for name in names[:4]:
                rest_work(0, name)
            rounds(dve, body, tail)


def layers23(nc, v):
    (psum, xs, ident, half_neg, col) = (v[n] for n in ("psum", "xs", "ident", "half_neg", "col"))
    DK = 16
    CI = 64
    RE, RT = 4, 2
    with ExitStack() as ctx:
        def sb(name, shape, dt=F32):
            return ctx.enter_context(nc.sbuf_tensor(name, shape, dt))

        def sem(name):
            return ctx.enter_context(nc.semaphore(name))

        events = []

        def event(name, per, unit=1):
            e = Event(ctx, nc, "l2_" + name, per, unit)
            events.append(e)
            return e

        wqk = sb("wqk2", [P, 2 * DK])
        wvpg = sb("wvpg", [P, D])
        wtheta = sb("wtheta", [P, CI])
        ww = sb("ww", [CI, P])
        bvpg = sb("bvpg", [P, D])
        bn = sb("bn", [P, 4])
        cg = sb("cg", [P, G, D])
        xg = sb("l2_xg", [P, G, D])
        q2 = sb("q2", [P, G, D])
        k2 = sb("k2", [P, G, D])
        vpg = sb("vpg", [P, G, 2, D])
        gT = sb("gT", [CI, G, P])
        hw = sb("hw", [CI, G, P])
        theta = sb("theta", [CI, G, D])
        prob = sb("l2_prob", [P, RE, BANK])
        pT = sb("l2_pT", [P, RT, BANK])
        x2 = sb("x2", [P, G, D])
        fin = sb("fin", [P, G, D])
        neg_max = sb("l2_neg_max", [P, RE, 2])
        z_sum = sb("l2_z_sum", [P, RE, 2])
        z_inv = sb("l2_z_inv", [P, RE, 2])

        score_bank = [psum[:, j, :] for j in range(2)]
        turn_bank = [psum[:, 2 + j, :] for j in range(2)]
        pv_bank = [psum[:, 4 + j, 0:D] for j in range(2)]

        names = ["q0", "q1", "k0", "k1"] + [f"w{b}" for b in range(G)] + ["g", "h", "t0", "t1", "y0", "y1"]
        work = Banks(ctx, nc, "l2_work", names, [psum[:, 6 + j, :] for j in range(2)])
        events += work.full_ev + work.out_ev
        ctx_in = event("ctx_in", 1, 16)
        x_copied = event("x_copied", 1)
        scores_done = event("scores_done", G)
        max_done = event("max_done", G)
        exp_done = event("exp_done", G)
        z_inv_done = event("z_inv_done", G)
        probs_done = event("probs_done", G)
        turned = event("turned", G)
        probsT_done = event("probsT_done", G)
        pv_done = event("pv_done", G)
        x2_done = event("x2_done", G)
        final_done = event("final_done", 2)
        out_written = event("out_written", 1, 16)
        weights_in = sem("l2_weights_in")
        zeroed = sem("l2_zeroed")
        bn_step = sem("bn_step")

        def two(t, m):
            return t[:, 2 * m:2 * m + 2, :].rearrange("p b d -> p (b d)")

        block = ctx.enter_context(nc.Block())

        @block.sync
        def _(sp):
            for e in events:
                sp.nop().then_inc(e.sem, e.per)
            sp.dma_start(wqk[:, :], v["wqk2_in"]).then_inc(weights_in, 16)
            sp.dma_start(wvpg[:, :], v["wvpg_in"]).then_inc(weights_in, 16)
            sp.dma_start(wtheta[:, :], v["theta_in"]).then_inc(weights_in, 16)
            sp.dma_start(ww[:, :], v["ww_in"]).then_inc(weights_in, 16)
            sp.dma_start(bvpg[:, :], v["rows_in"][ROWS["bvpg"]:ROWS["bvpg"] + D].partition_broadcast(P))\
                .then_inc(weights_in, 16)

            def load(i):
                sp.dma_start(cg[:, :, :], v["ctx_in"].rearrange("b p d -> p b d")[:, bass.ds(i * G, G), :])\
                    .then_inc(ctx_in.sem, 16)

            def store(i):
                sp.wait_ge(*final_done.at(i, 1))
                sp.dma_start(v["out"].rearrange("b p d -> p b d")[:, bass.ds(i * G, G), :], fin[:, :, :])\
                    .then_inc(out_written.sem, 16)

            load(0)
            with sp.Fori(1, ROUNDS) as i:
                sp.wait_ge(*work.full("w3", i - 1))
                load(i)
                store(i - 1)
            store(ROUNDS - 1)
            sp.wait_ge(*out_written.at(ROUNDS - 1))

        @block.gpsimd
        def _(pool):
            pool.memset(q2[:, :, :], 0.0).then_inc(zeroed, 1)
            pool.memset(k2[:, :, :], 0.0).then_inc(zeroed, 1)
            pool.memset(gT[:, :, :], 0.0).then_inc(zeroed, 1)
            pool.tensor_scalar(bn[:, 0:1], col("bn_var"), EPS, None, ALU.add).then_inc(bn_step, 1)
            pool.tensor_tensor(bn[:, 3:4], col("w_b"), col("bn_mean"), ALU.subtract).then_inc(bn_step, 1)
            pool.wait_ge(bn_step, 2)
            pool.tensor_tensor(bn[:, 1:2], bn[:, 0:1], half_neg[:, 0:1], ALU.pow).then_inc(bn_step, 1)
            pool.wait_ge(bn_step, 3)
            pool.tensor_tensor(bn[:, 2:3], bn[:, 1:2], col("gamma"), ALU.mult).then_inc(bn_step, 1)
            pool.wait_ge(bn_step, 4)
            pool.tensor_tensor(bn[:, 3:4], bn[:, 3:4], bn[:, 2:3], ALU.mult).then_inc(bn_step, 1)
            pool.wait_ge(bn_step, 5)
            pool.tensor_tensor(bn[:, 3:4], bn[:, 3:4], col("beta"), ALU.add).then_inc(bn_step, 1)

        @block.tensor
        def _(pe):
            mm = nc.tensor.matmul

            def bank(name, i):
                pe.wait_ge(*work.free(name, i))
                return work.psum(name)

            pe.wait_ge(weights_in, 80)
            pe.wait_ge(zeroed, 3)
            with pe.Fori(0, ROUNDS) as i:
                pe.wait_ge(*x_copied.at(i))
                for m in range(2):
                    mm(bank(f"q{m}", i)[0:DK, :], wqk[:, 0:DK], two(xg, m), start=True, stop=True)\
                        .then_inc(work.fills(f"q{m}"), 1)
                pe.wait_ge(*ctx_in.at(i))
                for m in range(2):
                    mm(bank(f"k{m}", i)[0:DK, :], wqk[:, DK:2 * DK], two(cg, m), start=True, stop=True)\
                        .then_inc(work.fills(f"k{m}"), 1)
                for b in range(G):
                    ps = bank(f"w{b}", i)
                    for j in range(2):
                        last = mm(ps[:, j * D:(j + 1) * D], cg[:, b, j * P:(j + 1) * P], wvpg[:, :],
                                  start=True, stop=True)
                    last.then_inc(work.fills(f"w{b}"), 1)
                pe.wait_ge(*work.out("k0", i))
                pe.wait_ge(*work.out("k1", i))

                def scores(b):
                    pe.wait_ge(*exp_done.at(i, b - 2))
                    for qt in range(2):
                        last = mm(score_bank[b % 2][:, qt * D:(qt + 1) * D], q2[:, b, qt * P:(qt + 1) * P],
                                  k2[:, b, :], start=True, stop=True)
                    last.then_inc(scores_done.sem, 1)

                def turn(b):
                    pe.wait_ge(*probs_done.at(i, b))
                    pe.wait_ge(*probsT_done.at(i, b - 2))
                    for qt in range(2):
                        for kt in range(2):
                            last = nc.tensor.transpose(turn_bank[b % 2][:, kt * D + qt * P:kt * D + (qt + 1) * P],
                                                       prob[:, b % RE, qt * D + kt * P:qt * D + (kt + 1) * P],
                                                       ident[:, :])
                    last.then_inc(turned.sem, 1)

                def times_v(b):
                    pe.wait_ge(*probsT_done.at(i, b))
                    pe.wait_ge(*x2_done.at(i, b - 2))
                    for kt in range(2):
                        last = mm(pv_bank[b % 2], vpg[:, b, kt, 0:P], pT[:, b % RT, kt * D:(kt + 1) * D],
                                  start=kt == 0, stop=kt == 1)
                    last.then_inc(pv_done.sem, 1)

                for b in range(3):
                    scores(b)
                pe.wait_ge(*work.out("w2", i))
                pe.wait_ge(*work.out("w3", i))
                ps = bank("g", i)
                for b in range(G):
                    for j in range(2):
                        last = mm(ps[0:CI, b * CI:(b + 1) * CI], vpg[:, b, j, P + CI:D], vpg[:, b, j, P:P + CI],
                                  start=j == 0, stop=j == 1)
                last.then_inc(work.fills("g"), 1)
                turn(0)
                scores(3)
                turn(1)
                times_v(0)
                pe.wait_ge(*work.out("g", i))
                ps = bank("h", i)
                for b in range(G):
                    last = mm(ps[:, b * P:(b + 1) * P], gT[:, b, :], ww[:, :], start=True, stop=True)
                last.then_inc(work.fills("h"), 1)
                turn(2)
                times_v(1)
                turn(3)
                times_v(2)
                pe.wait_ge(*x2_done.at(i, 1))
                mm(bank("t0", i)[0:CI, :], wtheta[:, :], two(x2, 0), start=True, stop=True)\
                    .then_inc(work.fills("t0"), 1)
                times_v(3)
                pe.wait_ge(*x2_done.at(i, 3))
                mm(bank("t1", i)[0:CI, :], wtheta[:, :], two(x2, 1), start=True, stop=True)\
                    .then_inc(work.fills("t1"), 1)
                pe.wait_ge(*work.out("h", i))
                for m in range(2):
                    pe.wait_ge(*work.out(f"t{m}", i))
                    ps = bank(f"y{m}", i)
                    for b in (2 * m, 2 * m + 1):
                        last = mm(ps[:, b % 2 * D:(b % 2 + 1) * D], hw[:, b, :], theta[:, b, :],
                                  start=True, stop=True)
                    last.then_inc(work.fills(f"y{m}"), 1)

        @block.scalar
        def _(act):
            act.wait_ge(zeroed, 3)
            with act.Fori(0, ROUNDS) as i:
                act.wait_ge(*x2_done.at(i - 1, G - 1))
                nc.scalar.copy(xg[:, :, :], xs[:, bass.ds(i * G, G), :]).then_inc(x_copied.sem, 1)
                for name, t, bias in (("q", q2, "bq2"), ("k", k2, "bk2")):
                    for m in range(2):
                        act.wait_ge(*work.full(f"{name}{m}", i))
                        nc.scalar.activation(two(t, m)[0:DK, :], work.psum(f"{name}{m}")[0:DK, :],
                                             ACT.Identity, bias=col(bias, p=DK)).then_inc(work.reads(f"{name}{m}"), 1)

                def exponentials(b):
                    act.wait_ge(*max_done.at(i, b))
                    act.wait_ge(*turned.at(i, b - RE))
                    for qt in range(2):
                        last = nc.scalar.activation(prob[:, b % RE, qt * D:(qt + 1) * D],
                                                    score_bank[b % 2][:, qt * D:(qt + 1) * D], ACT.Exp,
                                                    bias=neg_max[:, b % RE, qt:qt + 1],
                                                    accum_out=z_sum[:, b % RE, qt:qt + 1])
                    last.then_inc(exp_done.sem, 1)

                def turned_out(b):
                    act.wait_ge(*turned.at(i, b))
                    act.wait_ge(*pv_done.at(i, b - RT))
                    nc.scalar.copy(pT[:, b % RT, :], turn_bank[b % 2]).then_inc(probsT_done.sem, 1)

                exponentials(0)
                exponentials(1)
                exponentials(2)
                act.wait_ge(*work.full("g", i))
                nc.scalar.activation(gT[:, :, 0:CI], work.psum("g")[0:CI, 0:G * CI].rearrange(
                    "p (b c) -> p b c", b=G), ACT.Identity, scale=1.0 / D).then_inc(work.reads("g"), 1)
                turned_out(0)
                exponentials(3)
                turned_out(1)
                act.wait_ge(*work.full("h", i))
                nc.scalar.copy(hw[:, :, :].rearrange("p b c -> p (b c)"), work.psum("h")[0:CI, :])\
                    .then_inc(work.reads("h"), 1)
                turned_out(2)
                turned_out(3)
                for m in range(2):
                    act.wait_ge(*work.full(f"t{m}", i))
                    nc.scalar.activation(two(theta, m), work.psum(f"t{m}")[0:CI, :], ACT.Identity,
                                         bias=col("theta_b", p=CI)).then_inc(work.reads(f"t{m}"), 1)

        @block.vector
        def _(dve):
            dve.wait_ge(weights_in, 80)
            dve.wait_ge(bn_step, 6)
            with dve.Fori(0, ROUNDS) as i:
                def maxima(b):
                    dve.wait_ge(*scores_done.at(i, b))
                    dve.wait_ge(*exp_done.at(i, b - RE))
                    nc.vector.tensor_reduce(neg_max[:, b % RE, :], score_bank[b % 2].rearrange(
                        "p (t c) -> p t c", t=2), AX.X, ALU.max, negate=True).then_inc(max_done.sem, 1)

                def values(b):
                    dve.wait_ge(*work.full(f"w{b}", i))
                    nc.vector.tensor_tensor(vpg[:, b, :, :], work.psum(f"w{b}").rearrange(
                        "p (j n) -> p j n", j=2), bvpg[:, :].unsqueeze(1).broadcast_to([P, 2, D]), ALU.add)\
                        .then_inc(work.reads(f"w{b}"), 1)

                def norm(b):
                    dve.wait_ge(*exp_done.at(i, b))
                    nc.vector.reciprocal(z_inv[:, b % RE, :], z_sum[:, b % RE, :]).then_inc(z_inv_done.sem, 1)
                    dve.wait_ge(*z_inv_done.at(i, b))
                    e = prob[:, b % RE, :].rearrange("p (t c) -> p t c", t=2)
                    nc.vector.tensor_tensor(e, e, z_inv[:, b % RE, :].unsqueeze(2).broadcast_to([P, 2, D]),
                                            ALU.mult).then_inc(probs_done.sem, 1)

                def add_x(b):
                    dve.wait_ge(*pv_done.at(i, b))
                    nc.vector.tensor_tensor(x2[:, b, :], pv_bank[b % 2], xg[:, b, :], ALU.add)\
                        .then_inc(x2_done.sem, 1)

                for b in range(G):
                    values(b)
                maxima(0)
                maxima(1)
                norm(0)
                maxima(2)
                norm(1)
                norm(2)
                maxima(3)
                norm(3)
                for b in range(G):
                    add_x(b)
                for m in range(2):
                    dve.wait_ge(*work.full(f"y{m}", i))
                    if m == 0:
                        dve.wait_ge(*out_written.at(i - 1))
                    nc.vector.tensor_scalar(two(fin, m), work.psum(f"y{m}"), bn[:, 2:3], bn[:, 3:4],
                                            ALU.mult, ALU.add).then_inc(work.reads(f"y{m}"), 1)
                    dve.wait_ge(*work.out(f"y{m}", i))
                    nc.vector.tensor_tensor(two(fin, m), two(fin, m), two(x2, m), ALU.add)\
                        .then_inc(final_done.sem, 1)


def layout(inputs):
    a = {n: np.asarray(x) for n, x in inputs.items()}
    L0, L1, L2, L3 = ((lambda n, p=p: a[p + n]) for p in ("L0_xattn_", "L1_xattn_", "L2_xattn_", "L3_xattn_"))
    flat = {"ln_s": [L0("ln1_s"), L0("ln2_s"), L0("ln3_s")], "ln_b": [L0("ln1_b"), L0("ln2_b"), L0("ln3_b")],
            "bq0": [L0("b_qkv")[0:D]], "bk0": [L0("b_qkv")[D:2 * D]], "bcq": [L0("b_q")], "bck": [L0("b_kv")[0:D]],
            "b1": [L0("b1")], "bo": [L1("bo")], "rwb": [L1("r_w_bias").reshape(-1)], "bq2": [L2("bq")],
            "bk2": [L2("bk")], "theta_b": [L3("theta_b")], "w_b": [L3("w_b")], "gamma": [L3("bn_gamma")],
            "beta": [L3("bn_beta")], "bn_mean": [L3("bn_mean")], "bn_var": [L3("bn_var")]}
    cols = np.zeros((P, NCOLS), np.float32)
    for name, (at, n) in COLS.items():
        vec = np.concatenate(flat[name])
        if vec.size < P:
            vec = np.concatenate([vec, np.zeros(P - vec.size, np.float32)])
        cols[:, at:at + n] = vec.reshape(n, P).T
    rows = np.concatenate([L0("b_qkv")[2 * D:], L0("b_ao"), L0("b_kv")[D:], L0("b_co"), L0("b2"),
                           L2("bv"), L3("phi_b"), L3("g_b")])
    arrays = {
        "x": a["x"], "ctx_in": a["ctx_2048"], "ctxT": a["ctx_2048"].reshape(B * P, D).T,
        "smask": a["mask_1x1xSxS2_fc1"].reshape(P, P), "cmask": a["mask_Bx1xSxS2_ff1"].reshape(B, P, P),
        "cols_in": cols, "rows_in": rows,
        "wqkv_in": L0("w_qkv"), "wao_in": L0("w_ao"), "wq_in": L0("w_q"), "wkv_in": L0("w_kv"),
        "wco_in": L0("w_co"), "w1_in": L0("w1"), "w2_in": L0("w2"),
        "wz_in": np.concatenate([L1("Wqkv0").T, L1("Wqkv1").T]),
        "wi_in": np.concatenate([L1("Winj0").T, L1("Winj1").T]),
        "wo_in": L1("Wo").T,
        "wqk2_in": np.concatenate([L2("Wq").T, L2("Wk").T], axis=1),
        "wvpg_in": np.concatenate([L2("Wv").T, L3("phi_w").T, L3("g_w").T], axis=1),
        "theta_in": L3("theta_w").T, "ww_in": L3("w_w").T,
    }
    return {n: np.ascontiguousarray(x) for n, x in arrays.items()}


def kernel(**inputs):
    import concourse.bacc as bacc
    from concourse.bass_utils import run_bass_kernel_spmd

    arrays = layout(inputs)
    nc = bacc.Bacc("TRN2", target_bir_lowering=False, num_devices=1)
    args = [nc.dram_tensor(n, x.shape, mybir.dt.from_np(x.dtype), kind="ExternalInput").ap()
            for n, x in arrays.items()]
    out = nc.dram_tensor("out", (B, P, D), F32, kind="ExternalOutput").ap()
    program(nc, *args, out)
    result = run_bass_kernel_spmd(nc, [arrays], core_ids=[0])
    return result.results[0]["out"]
```

```python
from contextlib import ExitStack

import numpy as np
import concourse.bass as bass
from concourse import mybir

F32 = mybir.dt.float32
F32R = mybir.dt.float32r
ALU = mybir.AluOpType
ACT = mybir.ActivationFunctionType
AX = mybir.AxisListType

P = 128
B = 16
D = 256
G = 4
ROUNDS = B // G
EPS = 1e-5
H0, HD0 = 16, 16
QUAD = 4
F0 = 1024
H1, HD1 = 16, 64
NQ = H1 * HD1
BANK = 512


class Event:

    def __init__(self, ctx, nc, name, per, unit=1, credit=1):
        self.sem = ctx.enter_context(nc.semaphore(name))
        self.per, self.unit, self.credit = per * unit, unit, credit

    def at(self, i, k=0):
        return self.sem, (i + 1) * self.per + (k + 1) * self.unit


class Banks:

    def __init__(self, ctx, nc, tag, names, banks):
        n = len(banks)
        assert len(names) % n == 0
        self.place = {name: (k % n, k // n) for k, name in enumerate(names)}
        self.banks = banks
        self.full_ev = [Event(ctx, nc, f"{tag}_bank{j}_full", len(names) // n) for j in range(n)]
        self.out_ev = [Event(ctx, nc, f"{tag}_bank{j}_read_out", len(names) // n) for j in range(n)]

    def psum(self, name):
        return self.banks[self.place[name][0]]

    def free(self, name, i):
        j, k = self.place[name]
        return self.out_ev[j].at(i, k - 1)

    def full(self, name, i):
        j, k = self.place[name]
        return self.full_ev[j].at(i, k)

    def out(self, name, i):
        j, k = self.place[name]
        return self.out_ev[j].at(i, k)

    def fills(self, name):
        return self.full_ev[self.place[name][0]].sem

    def reads(self, name):
        return self.out_ev[self.place[name][0]].sem


COLS = {}
for _name, _n in (("ln_s", 6), ("ln_b", 6), ("bq0", 2), ("bk0", 2), ("bcq", 2), ("bck", 2), ("b1", 8),
                  ("bo", 1), ("rwb", 8), ("bq2", 1), ("bk2", 1), ("theta_b", 1), ("w_b", 1), ("gamma", 1),
                  ("beta", 1), ("bn_mean", 1), ("bn_var", 1)):
    _at = sum(n for _, n in COLS.values())
    COLS[_name] = (_at, _n)
NCOLS = sum(n for _, n in COLS.values())
ROWS = {n: k * D for k, n in enumerate(("bv0", "bao", "bcv", "bco", "b2", "bvpg"))}


def program(nc, x, ctx_in, ctxT, smask, cmask, cols_in, rows_in, wqkv_in, wao_in, wq_in, wkv_in, wco_in,
            w1_in, w2_in, wz_in, wi_in, wo_in, wqk2_in, wvpg_in, theta_in, ww_in, out, dbg=None, phases="ABC"):
    with ExitStack() as ctx:
        def sb(name, shape, c=ctx):
            return c.enter_context(nc.sbuf_tensor(name, shape, F32))

        psum = ctx.enter_context(nc.psum_tensor("psum", [P, 8, BANK], F32))

        xs = sb("xs", [P, B, D])
        ident = sb("ident", [P, P])
        mean_w = sb("mean_w", [P, P])
        cols = sb("cols", [P, NCOLS])
        half_neg = sb("half_neg", [P, 4])
        raw_place = ExitStack()
        wz0_raw, wz1_raw, wi0_raw = (raw_place.enter_context(nc.sbuf_tensor(n, [P, 3 * NQ], F32)) for n in (
            "wz0_raw", "wz1_raw", "wi0_raw"))
        l1_weights_in = ctx.enter_context(nc.semaphore("l1_weights_in"))

        def col(name, k=0, n=1, p=P):
            at = COLS[name][0] + k
            return cols[0:p, at:at + n]

        if "A" in phases:
            layer0(nc, locals())
        raw_place.close()
        wzl0, wzl1, wil0 = (ctx.enter_context(nc.sbuf_tensor(n, [P, 3 * NQ], F32R)) for n in (
            "wzl0", "wzl1", "wil0"))
        if "B" in phases:
            layer1(nc, locals())
        if "C" in phases:
            layers23(nc, locals())
        if dbg is not None:
            s_dbg = ctx.enter_context(nc.semaphore("s_dbg"))
            block = nc.Block()
            with block:
                @block.sync
                def _(sp):
                    sp.dma_start(dbg.rearrange("b p d -> p b d"), xs[:, :, :]).then_inc(s_dbg, 16)
                    sp.wait_ge(s_dbg, 16)


def layer0(nc, v):
    (psum, xs, ident, mean_w, cols, half_neg, col) = (v[n] for n in (
        "psum", "xs", "ident", "mean_w", "cols", "half_neg", "col"))
    (l1_weights_in, wz0_raw, wz1_raw, wi0_raw) = (v[n] for n in ("l1_weights_in", "wz0_raw", "wz1_raw", "wi0_raw"))
    NB = 2
    TOK = NB * P
    R0 = B // NB
    U = NB * H0 // QUAD
    STEPS = 2 * U
    RE, RT, RK = 4, 2, 4
    L_E, L_T, L_P, L_V, LEAD_K = 1, 3, 4, 5, 2
    VSTEP = P + HD0
    with ExitStack() as ctx:
        def sb(name, shape):
            return ctx.enter_context(nc.sbuf_tensor(name, shape, F32))

        def sem(name):
            return ctx.enter_context(nc.semaphore(name))

        events = []

        def event(name, per, unit=1, credit=1):
            e = Event(ctx, nc, name, per, unit, credit)
            events.append(e)
            return e

        rows = sb("rows", [P, len(ROWS) * D])
        wqkv = sb("wqkv", [P, 2, 3 * D])
        wao = sb("wao", [P, 2, D])
        wq = sb("wq", [P, 2, D])
        wkv = sb("wkv", [P, 2, 2 * D])
        wco = sb("wco", [P, 2, D])
        w1 = sb("w1", [P, 2, F0])
        w2 = sb("w2", [P, F0 // P, D])
        x_in, x_ao, x_1, x_co, x_2, x_mlp = (sb(n, [P, NB, D]) for n in (
            "x_in", "x_ao", "x_1", "x_co", "x_2", "x_mlp"))
        ln = [sb(f"ln{k}", [P, NB, D]) for k in range(3)]
        lnT = [sb(f"lnT{k}", [P, 2, TOK]) for k in range(3)]
        cT = sb("cT", [P, 2, TOK])
        qT = [sb(n, [P, 2, TOK]) for n in ("qT", "cqT")]
        kT = [sb(n, [P, 2, TOK]) for n in ("kT", "ckT")]
        oT = [sb(n, [P, 2, TOK]) for n in ("oT", "coT")]
        vm = [sb(n, [P, NB, 2, 8 * VSTEP]) for n in ("vm", "cvm")]
        hid = sb("hid", [P, F0 // P, TOK])
        km = sb("km", [P, RK, BANK])
        ring_e = sb("ring_e", [P, RE, BANK])
        ring_t = sb("ring_t", [P, RT, BANK])
        ring_h = sb("ring_h", [P, 2, BANK])
        ring_g = sb("ring_g", [P, 2, BANK])
        neg_max = sb("neg_max", [P, RE, QUAD])
        z_sum = sb("z_sum", [P, RE, QUAD])
        z_inv = sb("z_inv", [P, RE, QUAD])
        self_mul = sb("self_mul", [P, P])
        self_add = sb("self_add", [P, P])
        cross_mul = sb("cross_mul", [P, NB, P])
        cross_add = sb("cross_add", [P, NB, P])
        stats = sb("stats", [P, 3, NB, 6])
        mean_var = sb("mean_var", [P, 3, NB, 2])
        var_eps = sb("var_eps", [P, 3, NB])
        rstd = sb("rstd", [P, 3, NB])
        eps = sb("eps", [P, NB])
        first_stat = sb("first_stat", [P, 1])
        head_rows = sb("head_rows", [P, 8])
        bq_scaled = sb("bq_scaled", [P, 4])

        def row(name):
            return rows[:, ROWS[name]:ROWS[name] + D]

        score_bank = [psum[:, j, :] for j in range(2)]
        turn_bank = psum[:, 2, :]
        pv_bank = psum[:, 3, :]

        entry = Banks(ctx, nc, "entry", ["T0", "q", "k", "v"], [psum[:, 4, :]])
        middle = Banks(ctx, nc, "middle", ["o", "T1", "ck", "cq", "cv"], [psum[:, 5, :]])
        post = Banks(ctx, nc, "post", ["co", "T2", "f0", "f1", "f2", "f3", "y0", "y1"],
                     [psum[:, 6 + j, :] for j in range(2)])
        for banks in (entry, middle, post):
            events += banks.full_ev + banks.out_ev
        input_in = event("input_in", 1, 16)
        cross_mask_in = event("cross_mask_in", 1, 16)
        ctxT_in = event("ctxT_in", 1, 16)
        stats_done = [event(f"stats{k}_done", 1) for k in range(3)]
        mean_var_done = [event(f"mean_var{k}_done", 1) for k in range(3)]
        var_eps_done = [event(f"var_eps{k}_done", 1) for k in range(3)]
        rstd_done = [event(f"rstd{k}_done", 1) for k in range(3)]
        ln_done = [event(f"ln{k}_done", 1) for k in range(3)]
        residual_biased = [event(f"residual{k}_biased", 1) for k in range(3)]
        cross_add_made = event("cross_add_made", 1)
        h_lin, h_poly, h_arg, h_tanh, h_gate = (event(n, 4) for n in (
            "h_lin", "h_poly", "h_arg", "h_tanh", "h_gate"))
        (keys_masked, scores_done, scores_mul, scores_add, max_done, exp_done, z_inv_done, probs_done, turned,
         probsT_done, pv_done) = (event(n, STEPS, credit=2) for n in (
             "keys_masked", "scores_done", "scores_mul", "scores_add", "max_done", "exp_done", "z_inv_done",
             "probs_done", "turned", "probsT_done", "pv_done"))
        heads_out = event("heads_out", U, credit=2)

        (w_cols, w_rows, w_qkv, w_ao, w_kv, w_q, w_co, w_1, w_2, w_mask) = (
            sem(f"weights_in_{n}") for n in ("cols", "rows", "qkv", "ao", "kv", "q", "co", "1", "2", "mask"))
        consts_made = sem("consts_made")
        head_rows_made = sem("head_rows_made")
        dve_consts = sem("dve_consts")
        vm_zeroed = sem("vm_zeroed")
        ident_step = sem("ident_step")

        BESIDE = {0: [("T2", -3)], 1: [("f0", -3)], 2: [("T0", 0), ("f1", -3)], 3: [("q", 0)], 4: [("k", 0)],
                  5: [("f2", -3)], 6: [("o", -1)], 7: [("f3", -3)], 8: [("v", 0)], 9: [("y0", -3)],
                  10: [("T1", -1)], 11: [("y1", -3)], 12: [("ck", -1)], 13: [("co", -2)], 14: [("cq", -1)],
                  15: [("cv", -1)]}
        BODIES = R0 + 3

        LIKE = 5

        def bodies(eng, body):
            for g in range(3):
                body(g, g)
            with eng.Fori(3, R0) as j:
                body(j, LIKE)
            for g in range(R0, BODIES):
                body(g, g)

        def pair(j, g, off):
            return j + off if 0 <= g + off < R0 else None

        def unit(j, g, s):
            shift = s // STEPS
            j, g, s = j + shift, g + shift, s % STEPS
            a = int(s < U)
            i = pair(j, g, -2 if a else 0)
            if i is None:
                return None
            at = (1, U * g + s - U) if g <= 1 else (R0, U + s) if g == R0 + 1 else (j, s)
            return a, i, s % U, at[0], at[1]

        def beside(j, g, s):
            return [(name, pair(j, g, off)) for name, off in BESIDE.get(s, []) if pair(j, g, off) is not None]

        def at(event, j, g, s):
            w = unit(j, g, s)
            return event.at(w[3], w[4]) if w else None

        def wait_unit(eng, event, j, g, s):
            if unit(j, g, s):
                eng.wait_ge(*at(event, j, g, s))

        def banks_of(name):
            return entry if name in entry.place else middle if name in middle.place else post

        block = ctx.enter_context(nc.Block())

        @block.sync
        def _(sp):
            for e in events:
                sp.nop().then_inc(e.sem, e.credit * e.per)

            def load_x(i):
                sp.dma_start(x_in[:, :, :], v["x"].rearrange("b s d -> s b d")[:, bass.ds(i * NB, NB), :])\
                    .then_inc(input_in.sem, 16)

            def load_ctx(i):
                sp.dma_start(cT[:, :, :], v["ctxT"].rearrange("(c p) t -> p c t", c=2)[:, :, bass.ds(i * TOK, TOK)])\
                    .then_inc(ctxT_in.sem, 16)

            def load_mask(i):
                sp.dma_start(cross_mul[:, :, :], v["cmask"].rearrange("b q k -> q b k")[:, bass.ds(i * NB, NB), :])\
                    .then_inc(cross_mask_in.sem, 16)

            def next_x(i):
                sp.wait_ge(*ln_done[0].at(i - 1))
                sp.wait_ge(*residual_biased[0].at(i - 1))
                load_x(i)

            def next_ctx(i):
                sp.wait_ge(*middle.full("cv", i - 1))
                load_ctx(i)

            def next_mask(i):
                sp.wait_ge(*scores_mul.at(i + 1, U - 1))
                load_mask(i)

            load_x(0)
            sp.dma_start(cols[:, :], v["cols_in"]).then_inc(w_cols, 16)
            sp.dma_start(wqkv[:, :, :], v["wqkv_in"].rearrange("(c p) n -> p c n", p=P)).then_inc(w_qkv, 16)
            sp.dma_start(rows[:, :], v["rows_in"].partition_broadcast(P)).then_inc(w_rows, 16)
            sp.dma_start(self_mul[:, :], v["smask"]).then_inc(w_mask, 16)
            load_ctx(0)
            load_mask(0)
            for w, src, s in ((wkv, "wkv_in", w_kv), (wao, "wao_in", w_ao), (wq, "wq_in", w_q),
                              (wco, "wco_in", w_co), (w1, "w1_in", w_1), (w2, "w2_in", w_2)):
                sp.dma_start(w[:, :, :], v[src].rearrange("(c p) n -> p c n", p=P)).then_inc(s, 16)
            next_x(1)
            next_x(2)
            next_ctx(1)
            for w, src, c in ((wz0_raw, "wz_in", 0), (wz1_raw, "wz_in", 1), (wi0_raw, "wi_in", 0)):
                sp.dma_start(w[:, :], v[src][c * P:(c + 1) * P, :]).then_inc(l1_weights_in, 16)
            with sp.Fori(2, R0 - 1) as j:
                next_mask(j - 1)
                next_x(j + 1)
                next_ctx(j)
            next_mask(R0 - 2)
            next_ctx(R0 - 1)
            next_mask(R0 - 1)
            sp.wait_ge(w_mask, 16)
            sp.wait_ge(l1_weights_in, 48)

        @block.gpsimd
        def _(pool):
            pool.memset(ident[:, :], 0.0).then_inc(ident_step, 1)
            pool.memset(head_rows[:, :], 1.0).then_inc(ident_step, 1)
            pool.memset(half_neg[:, :], -0.5).then_inc(head_rows_made, 1)
            pool.memset(eps[:, :], EPS).then_inc(head_rows_made, 1)
            pool.wait_ge(ident_step, 2)
            pool.affine_select(out=ident[:, :], in_=ident[:, :], compare_op=ALU.not_equal, fill=1.0, base=0,
                               pattern=[[-1, P]], channel_multiplier=1).then_inc(consts_made, 1)
            pool.affine_select(out=head_rows[:, :], in_=head_rows[:, :], compare_op=ALU.is_ge, fill=0.0, base=0,
                               pattern=[[-HD0, 8]], channel_multiplier=1).then_inc(ident_step, 1)
            pool.wait_ge(ident_step, 3)
            pool.affine_select(out=head_rows[:, :], in_=head_rows[:, :], compare_op=ALU.is_ge, fill=0.0,
                               base=HD0 - 1, pattern=[[HD0, 8]], channel_multiplier=-1).then_inc(head_rows_made, 1)
            pool.memset(mean_w[:, :], 1.0 / P)
            pool.wait_ge(head_rows_made, 3)

            def inverse_std(i, k):
                pool.wait_ge(*mean_var_done[k].at(i))
                pool.tensor_tensor(var_eps[:, k, :], mean_var[:, k, :, 1], eps[:, :], ALU.add)\
                    .then_inc(var_eps_done[k].sem, 1)
                pool.wait_ge(*var_eps_done[k].at(i))
                pool.tensor_tensor(rstd[:, k, :], var_eps[:, k, :], half_neg[:, 0:NB], ALU.pow)\
                    .then_inc(rstd_done[k].sem, 1)

            def add_bias(i, k, dst, src, bias, used):
                pool.wait_ge(*ln_done[k].at(i))
                pool.wait_ge(*used)
                pool.tensor_tensor(dst[:, :, :], src[:, :, :], row(bias).unsqueeze(1).broadcast_to([P, NB, D]),
                                   ALU.add).then_inc(residual_biased[k].sem, 1)

            def mask_keys(a, i, u, ri, n):
                b, quad = divmod(u, QUAD)
                half, q = divmod(quad, 2)
                if u == 0:
                    pool.wait_ge(*(middle.out("ck", i) if a else entry.out("k", i)))
                pool.wait_ge(*scores_done.at(ri, n - RK))
                pool.tensor_tensor(
                    km[:, n % RK, :].rearrange("p (h k) -> p h k", h=QUAD),
                    kT[a][:, half, b * P:(b + 1) * P].unsqueeze(1).broadcast_to([P, QUAD, P]),
                    head_rows[:, QUAD * q:QUAD * q + QUAD].unsqueeze(2).broadcast_to([P, QUAD, P]),
                    ALU.mult).then_inc(keys_masked.sem, 1)

            def norm(ri, n):
                pool.wait_ge(*z_inv_done.at(ri, n))
                p = ring_e[:, n % RE, :].rearrange("p (h k) -> p h k", h=QUAD)
                pool.tensor_tensor(p, p, z_inv[:, n % RE, :].unsqueeze(2).broadcast_to([P, QUAD, P]), ALU.mult)\
                    .then_inc(probs_done.sem, 1)

            def body(j, g):
                i0, i1, i2, i3 = (pair(j, g, -k) for k in range(4))
                for s in range(STEPS):
                    if unit(j, g, s + LEAD_K):
                        mask_keys(*unit(j, g, s + LEAD_K))
                    if unit(j, g, s - L_E):
                        norm(*unit(j, g, s - L_E)[3:])
                    if s == 0 and i0 is not None:
                        inverse_std(i0, 0)
                    if s == 0 and g == 0:
                        pool.wait_ge(w_rows, 16)
                    if s == 1 and i3 is not None:
                        add_bias(i3, 2, x_mlp, x_2, "b2", post.out("y1", i3 - 1))
                    if s == 6 and i1 is not None:
                        inverse_std(i1, 1)
                    if s == 9 and i0 is not None:
                        add_bias(i0, 0, x_ao, x_in, "bao", middle.out("o", i0 - 1))
                    if s == 13 and i2 is not None:
                        inverse_std(i2, 2)
                    if s == 14 and i1 is not None:
                        add_bias(i1, 1, x_co, x_1, "bco", post.out("co", i1 - 1))

            bodies(pool, body)

        @block.tensor
        def _(pe):
            def bank(name, i):
                banks = banks_of(name)
                pe.wait_ge(*banks.free(name, i))
                return banks.psum(name)

            def full(name, ins):
                ins.then_inc(banks_of(name).fills(name), 1)

            def norm_turn(i, k):
                name = f"T{k}"
                pe.wait_ge(*ln_done[k].at(i))
                ps = bank(name, i)
                for c in range(2):
                    for b in range(NB):
                        last = nc.tensor.transpose(ps[:, c * TOK + b * P:c * TOK + (b + 1) * P],
                                                   ln[k][:, b, c * P:(c + 1) * P], ident[:, :])
                full(name, last)

            def features_out(i, name, w, at, src):
                ps = bank(name, i)
                for m in range(2):
                    for c in range(2):
                        last = nc.tensor.matmul(ps[:, m * TOK:(m + 1) * TOK], w[:, c, at + m * P:at + (m + 1) * P],
                                                src[:, c, :], start=c == 0, stop=c == 1)
                full(name, last)

            def tokens_out(i, name, w, at, src, chunks, batches):
                ps = bank(name, i)
                for n, b in enumerate(batches):
                    for c in range(chunks):
                        last = nc.tensor.matmul(ps[:, n * D:(n + 1) * D], src[:, c, b * P:(b + 1) * P],
                                                w[:, c, at:at + D], start=c == 0, stop=c == chunks - 1)
                full(name, last)

            def work(name, i):
                both = list(range(NB))
                if name[0] == "T":
                    norm_turn(i, int(name[1]))
                elif name == "q":
                    pe.wait_ge(*entry.out("T0", i))
                    features_out(i, name, wqkv, 0, lnT[0])
                elif name == "k":
                    features_out(i, name, wqkv, D, lnT[0])
                elif name == "v":
                    tokens_out(i, name, wqkv, 2 * D, lnT[0], 2, both)
                elif name == "o":
                    tokens_out(i, name, wao, 0, oT[0], 2, both)
                elif name == "cq":
                    pe.wait_ge(*middle.out("T1", i))
                    features_out(i, name, wq, 0, lnT[1])
                elif name == "ck":
                    pe.wait_ge(*ctxT_in.at(i))
                    features_out(i, name, wkv, 0, cT)
                elif name == "cv":
                    tokens_out(i, name, wkv, D, cT, 2, both)
                elif name == "co":
                    tokens_out(i, name, wco, 0, oT[1], 2, both)
                elif name[0] == "f":
                    m = int(name[1])
                    if m == 0:
                        pe.wait_ge(*post.out("T2", i))
                    features_out(i, name, w1, m * 2 * P, lnT[2])
                else:
                    if name == "y0":
                        pe.wait_ge(*h_gate.at(i, 3))
                    tokens_out(i, name, w2, 0, hid, F0 // P, [int(name[1])])

            def scores(a, i, u, ri, n):
                b, quad = divmod(u, QUAD)
                if u == 0:
                    pe.wait_ge(*(middle.out("cq", i) if a else entry.out("q", i)))
                pe.wait_ge(*keys_masked.at(ri, n))
                pe.wait_ge(*scores_mul.at(ri, n - 2))
                nc.tensor.matmul(score_bank[n % 2], qT[a][:, quad // 2, b * P:(b + 1) * P],
                                 km[:, n % RK, :], start=True, stop=True).then_inc(scores_done.sem, 1)

            def turn(ri, n):
                pe.wait_ge(*probs_done.at(ri, n))
                pe.wait_ge(*probsT_done.at(ri, n - 1))
                for h in range(QUAD):
                    last = nc.tensor.transpose(turn_bank[:, h * P:(h + 1) * P],
                                               ring_e[:, n % RE, h * P:(h + 1) * P], ident[:, :])
                last.then_inc(turned.sem, 1)

            def times_v(a, i, u, ri, n):
                b, quad = divmod(u, QUAD)
                half, q = divmod(quad, 2)
                pe.wait_ge(*probsT_done.at(ri, n))
                if u == 0:
                    pe.wait_ge(*(middle.out("cv", i) if a else entry.out("v", i)))
                if q == 0:
                    pe.wait_ge(*heads_out.at(ri, n // 2 - 1))
                for h in range(QUAD):
                    j = QUAD * q + h
                    last = nc.tensor.matmul(pv_bank[:, 0:P], vm[a][:, b, half, j * P:(j + 1) * P],
                                            ring_t[:, n % RT, h * P:(h + 1) * P], start=j == 0, stop=j == 7)
                last.then_inc(pv_done.sem, 1)

            def body(j, g):
                for s in range(STEPS):
                    if unit(j, g, s):
                        scores(*unit(j, g, s))
                    for name, i in beside(j, g, s):
                        if g == 0 and name == "q":
                            pe.wait_ge(w_qkv, 16)
                        if g <= 2 and name == "o":
                            for w in (w_ao, w_kv, w_q):
                                pe.wait_ge(w, 16)
                        if name in ("o", "co"):
                            w = unit(j, g, -1 if name == "o" else U - 1)
                            pe.wait_ge(*heads_out.at(w[3], w[4] // 2))
                        if g == 2 and name == "co":
                            for w in (w_co, w_1, w_2):
                                pe.wait_ge(w, 16)
                        work(name, i)
                    if unit(j, g, s - L_V):
                        times_v(*unit(j, g, s - L_V))
                    if unit(j, g, s - L_T):
                        turn(*unit(j, g, s - L_T)[3:])

            pe.wait_ge(consts_made, 1)
            bodies(pe, body)

        @block.scalar
        def _(act):
            def affine(i, name, dst, bias, scale):
                banks = banks_of(name)
                act.wait_ge(*banks.full(name, i))
                for m in range(2):
                    last = nc.scalar.activation(dst[:, m, :], banks.psum(name)[:, m * TOK:(m + 1) * TOK],
                                                ACT.Identity, bias=bias[:, m:m + 1],
                                                scale=scale if isinstance(scale, float) else scale[:, m:m + 1])
                last.then_inc(banks.reads(name), 1)

            def hidden(i, f):
                act.wait_ge(*post.full(f"f{f}", i))
                act.wait_ge(*h_gate.at(i, f - 2))
                for dst, func, m in ((ring_h, ACT.Identity, 0), (ring_h, ACT.Identity, 1),
                                     (ring_g, ACT.Square, 0), (ring_g, ACT.Square, 1)):
                    last = nc.scalar.activation(dst[:, f % 2, m * TOK:(m + 1) * TOK],
                                                post.psum(f"f{f}")[:, m * TOK:(m + 1) * TOK], func,
                                                bias=col("b1", 2 * f + m))
                last.then_inc(post.reads(f"f{f}"), 1)

            def gate(i, f):
                act.wait_ge(*h_arg.at(i, f))
                t = ring_g[:, f % 2, :]
                nc.scalar.activation(t, t, ACT.Tanh, scale=0.7978845608028654).then_inc(h_tanh.sem, 1)

            def work(name, i, j, g):
                scale = HD0 ** -0.5
                if name[0] == "T":
                    k = int(name[1])
                    act.wait_ge(*(entry.full("v", i - 1), middle.full("cq", i - 1), post.full("f3", i - 1))[k])
                    affine(i, name, lnT[k], col("ln_b", 2 * k, 2), col("ln_s", 2 * k, 2))
                elif name in ("q", "cq"):
                    wait_unit(act, scores_done, j, g, -1 if name == "q" else U - 1)
                    a = int(name == "cq")
                    affine(i, name, qT[a], bq_scaled[:, 2 * a:2 * a + 2], scale)
                elif name in ("k", "ck"):
                    wait_unit(act, keys_masked, j, g, -1 if name == "k" else U - 1)
                    a = int(name == "ck")
                    affine(i, name, kT[a], col(("bk0", "bck")[a], 0, 2), 1.0)
                elif name[0] == "f":
                    hidden(i, int(name[1]))

            def exponentials(ri, n):
                act.wait_ge(*max_done.at(ri, n))
                for h in range(QUAD):
                    e = ring_e[:, n % RE, h * P:(h + 1) * P]
                    last = nc.scalar.activation(e, e, ACT.Exp, bias=neg_max[:, n % RE, h:h + 1],
                                                accum_out=z_sum[:, n % RE, h:h + 1])
                last.then_inc(exp_done.sem, 1)

            def copy_turned(ri, n):
                act.wait_ge(*turned.at(ri, n))
                act.wait_ge(*pv_done.at(ri, n - RT))
                nc.scalar.copy(ring_t[:, n % RT, :], turn_bank).then_inc(probsT_done.sem, 1)

            def copy_heads(a, i, u, ri, n):
                b, quad = divmod(u, QUAD)
                if u == 1:
                    act.wait_ge(*(post.full("co", i - 1) if a else middle.full("o", i - 1)))
                act.wait_ge(*pv_done.at(ri, n))
                nc.scalar.copy(oT[a][:, quad // 2, b * P:(b + 1) * P], pv_bank[:, 0:P]).then_inc(heads_out.sem, 1)

            def body(j, g):
                for s in range(STEPS):
                    if unit(j, g, s - L_E):
                        exponentials(*unit(j, g, s - L_E)[3:])
                    if unit(j, g, s - L_P):
                        copy_turned(*unit(j, g, s - L_P)[3:])
                    for name, i in beside(j, g, s):
                        if g == 0 and name == "q":
                            act.wait_ge(dve_consts, 2)
                        work(name, i, j, g)
                    for name, i in beside(j, g, s - 1):
                        if name[0] == "f":
                            gate(i, int(name[1]))
                    w = unit(j, g, s - L_V)
                    if w and w[2] % 2 == 1:
                        copy_heads(*w)

            act.wait_ge(w_cols, 16)
            bodies(act, body)

        @block.vector
        def _(dve):
            def statistics(i, k, src):
                for b in range(NB):
                    last = nc.vector.bn_stats(stats[:, k, b, :], src[:, b, :])
                last.then_inc(stats_done[k].sem, 1)
                dve.wait_ge(*stats_done[k].at(i))
                nc.vector.tensor_copy(first_stat[:, :], stats[:, k, 0, 0:1])
                for b in range(NB):
                    last = nc.vector.bn_aggr(mean_var[:, k, b, :], stats[:, k, b, :])
                last.then_inc(mean_var_done[k].sem, 1)

            def normalise(i, k, src, turned_before):
                dve.wait_ge(*rstd_done[k].at(i))
                dve.wait_ge(*turned_before)
                for b in range(NB):
                    last = nc.vector.tensor_scalar(ln[k][:, b, :], src[:, b, :], mean_var[:, k, b, 0:1],
                                                   rstd[:, k, b:b + 1], ALU.subtract, ALU.mult)
                last.then_inc(ln_done[k].sem, 1)

            def spread_values(i, name, a, bias, j, g):
                banks = banks_of(name)
                dve.wait_ge(*banks.full(name, i))
                wait_unit(dve, pv_done, j, g, U - 1 if a else -1)
                for b in range(NB):
                    dst = vm[a][:, b, :, :].rearrange("p c (j w) -> p c j w", w=VSTEP)[:, :, :, 0:HD0]
                    last = nc.vector.tensor_tensor(
                        dst, banks.psum(name)[:, b * D:(b + 1) * D].rearrange("p (c j w) -> p c j w", c=2, w=HD0),
                        row(bias).rearrange("p (c j w) -> p c j w", c=2, w=HD0), ALU.add)
                last.then_inc(banks.reads(name), 1)

            def add_product(i, name, dst, src, k):
                banks = banks_of(name)
                dve.wait_ge(*banks.full(name, i))
                dve.wait_ge(*residual_biased[k].at(i))
                dve.wait_ge(*residual_biased[k + 1].at(i - 1))
                nc.vector.tensor_tensor(dst[:, :, :].rearrange("p b d -> p (b d)"), banks.psum(name),
                                        src[:, :, :].rearrange("p b d -> p (b d)"), ALU.add)\
                    .then_inc(banks.reads(name), 1)
                dve.wait_ge(*banks.out(name, i))
                statistics(i, k + 1, dst)

            def polynomial(i, f):
                t, h = ring_g[:, f % 2, :], ring_h[:, f % 2, :]
                dve.wait_ge(*post.out(f"f{f}", i))
                nc.vector.tensor_scalar(t, t, 0.044715, 1.0, ALU.mult, ALU.add).then_inc(h_poly.sem, 1)
                dve.wait_ge(*h_poly.at(i, f))
                nc.vector.tensor_tensor(t, t, h, ALU.mult).then_inc(h_arg.sem, 1)

            def gated(i, f):
                if f == 0:
                    dve.wait_ge(*post.full("y1", i - 1))
                dve.wait_ge(*h_tanh.at(i, f))
                nc.vector.scalar_tensor_tensor(
                    out=hid[:, 2 * f:2 * f + 2, :].rearrange("p m t -> p (m t)"), in0=ring_g[:, f % 2, :],
                    scalar=1.0, in1=ring_h[:, f % 2, :], op0=ALU.add, op1=ALU.mult).then_inc(h_gate.sem, 1)

            def output(i, b):
                name = f"y{b}"
                dve.wait_ge(*post.full(name, i))
                if b == 0:
                    dve.wait_ge(*residual_biased[2].at(i))
                nc.vector.scalar_tensor_tensor(out=xs[:, bass.ds(i * NB + b, 1), :].rearrange("p a d -> p (a d)"),
                                               in0=post.psum(name)[:, 0:D], scalar=0.5, in1=x_mlp[:, b, :],
                                               op0=ALU.mult, op1=ALU.add).then_inc(post.reads(name), 1)

            def work(name, i, j, g):
                if name == "v":
                    spread_values(i, name, 0, "bv0", j, g)
                elif name == "cv":
                    spread_values(i, name, 1, "bcv", j, g)
                elif name == "o":
                    add_product(i, name, x_1, x_ao, 0)
                elif name == "co":
                    add_product(i, name, x_2, x_co, 1)
                elif name[0] == "f":
                    polynomial(i, int(name[1]))
                elif name[0] == "y":
                    output(i, int(name[1]))

            def softmax_step(j, g, s):
                now, before = unit(j, g, s), unit(j, g, s - L_E)
                if now:
                    a, _, u, ri, n = now
                    e = ring_e[:, n % RE, :].rearrange("p (h k) -> p h k", h=QUAD)
                    mul, add = ((m[:, u // QUAD, :] if a else m[:, :]).unsqueeze(1).broadcast_to([P, QUAD, P])
                                for m in ((cross_mul, cross_add) if a else (self_mul, self_add)))
                    if u == 0 and a == 1:
                        dve.wait_ge(*cross_add_made.at(now[1]))
                    dve.wait_ge(*scores_done.at(ri, n))
                    dve.wait_ge(*turned.at(ri, n - RE))
                    nc.vector.tensor_tensor(e, score_bank[n % 2].rearrange("p (h k) -> p h k", h=QUAD), mul,
                                            ALU.mult).then_inc(scores_mul.sem, 1)
                if before:
                    m = before[4]
                    dve.wait_ge(*exp_done.at(before[3], m))
                    nc.vector.reciprocal(z_inv[:, m % RE, :], z_sum[:, m % RE, :]).then_inc(z_inv_done.sem, 1)
                if now:
                    dve.wait_ge(*scores_mul.at(ri, n))
                    nc.vector.tensor_tensor(e, e, add, ALU.add).then_inc(scores_add.sem, 1)
                    dve.wait_ge(*scores_add.at(ri, n))
                    nc.vector.tensor_reduce(neg_max[:, n % RE, :], e, AX.X, ALU.max, negate=True)\
                        .then_inc(max_done.sem, 1)

            def body(j, g):
                i0, i1, i2 = (pair(j, g, -k) for k in range(3))
                for s in range(STEPS):
                    softmax_step(j, g, s)
                    for name, i in beside(j, g, s):
                        if g <= 2 and name in ("v", "cv"):
                            dve.wait_ge(vm_zeroed, 1 if name == "v" else 2)
                        work(name, i, j, g)
                    for name, i in beside(j, g, s - 1):
                        if name[0] == "f":
                            gated(i, int(name[1]))
                    if s == 0 and i0 is not None:
                        dve.wait_ge(*input_in.at(i0))
                        statistics(i0, 0, x_in)
                    if s == 1 and i0 is not None:
                        normalise(i0, 0, x_in, entry.full("T0", i0 - 1))
                    if s == 2 and g == 0:
                        dve.wait_ge(w_cols, 16)
                        nc.vector.tensor_scalar(bq_scaled[:, 0:2], col("bq0", 0, 2), HD0 ** -0.5, None, ALU.mult)\
                            .then_inc(dve_consts, 1)
                        nc.vector.tensor_scalar(bq_scaled[:, 2:4], col("bcq", 0, 2), HD0 ** -0.5, None, ALU.mult)\
                            .then_inc(dve_consts, 1)
                        dve.wait_ge(w_mask, 16)
                        nc.vector.tensor_scalar(self_add[:, :], self_mul[:, :], -1.0, 10000.0, ALU.add, ALU.mult)\
                            .then_inc(dve_consts, 1)
                        dve.wait_ge(dve_consts, 3)
                        dve.wait_ge(w_rows, 16)
                        for t in vm:
                            dve.memset(t[:, :, :, :], 0.0).then_inc(vm_zeroed, 1)
                    if s == 8 and i1 is not None:
                        normalise(i1, 1, x_1, middle.full("T1", i1 - 1))
                    if s == 10 and i1 is not None:
                        dve.wait_ge(*cross_mask_in.at(i1))
                        nc.vector.tensor_scalar(cross_add[:, :, :], cross_mul[:, :, :], -1.0, 10000.0,
                                                ALU.add, ALU.mult).then_inc(cross_add_made.sem, 1)
                    if s == 15 and i2 is not None:
                        normalise(i2, 2, x_2, post.full("T2", i2 - 1))

            bodies(dve, body)


def layer1(nc, v):
    (sb_, psum, xs, ident, mean_w, half_neg, col) = (v[n] for n in (
        "sb", "psum", "xs", "ident", "mean_w", "half_neg", "col"))
    (l1_weights_in, wz0_raw, wz1_raw, wi0_raw, wzl0, wzl1, wil0) = (v[n] for n in (
        "l1_weights_in", "wz0_raw", "wz1_raw", "wi0_raw", "wzl0", "wzl1", "wil0"))
    NB = 2
    R1 = B // NB
    UNITS = H1 * NB
    RE, RT = 4, 2
    L_E, L_T, L_P, L_V, L_O, L_W = 1, 2, 3, 4, 5, 1
    SCALE = HD1 ** -0.5
    with ExitStack() as ctx:
        def sb(name, shape, dt=F32):
            return ctx.enter_context(nc.sbuf_tensor(name, shape, dt))

        def sem(name):
            return ctx.enter_context(nc.semaphore(name))

        events = []

        def event(name, per, unit=1):
            e = Event(ctx, nc, "l1_" + name, per, unit)
            events.append(e)
            return e

        def place(name, shape):
            with nc.sbuf_tensor(name + "_raw", shape, F32) as raw:
                pass
            return raw, sb(name, shape, F32R)

        wi1_raw, wil1 = place("wil1", [P, 3 * NQ])
        wo_raw, wol = place("wol", [P, H1, P])
        wz = [[sb(f"wzh{c}", [P, 3 * NQ], F32R) for c in range(2)], [wzl0, wzl1]]
        wi = [[sb(f"wih{c}", [P, 3 * NQ], F32R) for c in range(2)], [wil0, wil1]]
        wo = [sb("woh", [P, H1, P], F32R), wol]
        zu = [sb(f"zu{p}", [P, 2, 2, NB, P], F32R) for p in ("h", "l")]
        q = [sb(f"q{p}", [P, 2, 2, 2, NB, P], F32R) for p in ("h", "l")]
        k = [sb(f"k{p}", [P, 2, 2, NB, P], F32R) for p in ("h", "l")]
        vs = sb("vs", [P, 2, NB, 2, 4, 2, HD1], F32R)
        plain = sb("plain", [P, RE * BANK + 3 * NB * D])
        prob = plain[:, 0:RE * BANK].rearrange("p (s n) -> p s n", s=RE)
        ub, y, ysq = (plain[:, RE * BANK + j * NB * D:RE * BANK + (j + 1) * NB * D].rearrange(
            "p (b d) -> p b d", b=NB) for j in range(3))
        pT = [sb(f"pT{p}", [P, RT, BANK], F32R) for p in ("h", "l")]
        aT = [sb(f"aT{p}", [P, RT, D], F32R) for p in ("h", "l")]
        neg_max = sb("l1_neg_max", [P, RE, 2])
        z_sum = sb("l1_z_sum", [P, RE, 2])
        z_inv = sb("l1_z_inv", [P, RE, 2])
        var_eps = sb("l1_var_eps", [P, 4])
        rstd = sb("l1_rstd", [P, 4])
        diag = ysq.rearrange("p b (h c) -> p (b h) c", h=2)

        score_bank = [psum[:, j, :] for j in range(2)]
        turn_bank = [psum[:, 2 + j, :] for j in range(2)]
        pv_bank = psum[:, 4, :]
        wo_bank = [psum[:, 7, b * D:(b + 1) * D] for b in range(NB)]

        HALF = 3 * NQ // 2
        parts = [tuple(w[:, h * HALF:(h + 1) * HALF] for w in (hi, lo, raw)) for h in range(2)
                 for hi, lo, raw in ((wz[0][0], wz[1][0], wz0_raw), (wz[0][1], wz[1][1], wz1_raw),
                                     (wi[0][0], wi[1][0], wi0_raw), (wi[0][1], wi[1][1], wi1_raw))]
        wo_parts = [tuple(w[:, g * 8:(g + 1) * 8, :].rearrange("p h o -> p (h o)") for w in (*wo, wo_raw))
                    for g in range(2)]
        wi_in, wo_in = sem("l1_wi_in"), sem("l1_wo_in")
        hi_made, lo_made, wo_hi_made, wo_lo_made = (sem(n) for n in (
            "weights_hi_made", "weights_lo_made", "wo_hi_made", "wo_lo_made"))

        names = ["q0", "k0", "v0b0", "v0b1", "q1", "k1", "q2", "k2", "v1b0", "v1b1", "q3", "k3", "mean", "var",
                 "q4", "k4", "v2b0", "v2b1", "q5", "k5", "inv0", "inv1", "q6", "k6", "v3b0", "v3b1",
                 "q7", "k7"]
        made = [n for n in names if n[0] in "qkv" and n != "var"]
        work = Banks(ctx, nc, "l1_work", names, [psum[:, 5 + j, :] for j in range(2)])
        events += work.full_ev + work.out_ev
        work_hi = event("work_hi", len(made))
        u_in = event("u_in", 1, 16)
        zu_hi = event("zu_hi", 2)
        zu_lo = event("zu_lo", 2)
        scores_done = event("scores_done", UNITS)
        max_done = event("max_done", UNITS)
        exp_done = event("exp_done", UNITS)
        z_inv_done = event("z_inv_done", UNITS)
        probs_done = event("probs_done", UNITS)
        turned = event("turned", UNITS)
        pT_hi = event("pT_hi", UNITS)
        pT_lo = event("pT_lo", UNITS)
        pv_done = event("pv_done", UNITS)
        aT_hi = event("aT_hi", UNITS)
        aT_lo = event("aT_lo", UNITS)
        wo_done = event("wo_done", UNITS)
        y_done = event("y_done", 1)
        centred = event("centred", 1)
        squared = event("squared", 1)
        rstd_done = event("rstd_done", 1)
        diagonal = event("diagonal", 1)
        zeroed = sem("l1_zeroed")

        def unit(n):
            n %= UNITS
            return n // 4, n % 4 // 2, n % 2

        def work_at(t):
            s, r = divmod(t, 4)
            nxt = (s + 1) % 8
            if r < 2:
                return "qk"[r] + str(nxt), int(s == 7)
            return (f"v{nxt // 2}b{r - 2}", int(s == 7)) if s % 2 == 1 else (None, 0)

        T_Y, T_MEAN, T_VAR, T_INV, T_ZU = L_O, 10, 11, 18, 26

        def work_to_round(i, t, last):
            n = t - L_W
            name, ahead = work_at(n % UNITS)
            ahead += -1 if n < 0 else 0
            return (name, i + ahead) if name and not (last and ahead == 1) else (None, 0)

        def tile_of(name):
            slot = int(name[1]) % 2
            if name[0] == "q":
                return [[(w[h * HD1:(h + 1) * HD1, slot, h, :, :, :].rearrange("p c b l -> p (c b l)"))
                         for w in q] for h in range(2)]
            if name[0] == "k":
                return [w[:, slot, :, :, :].rearrange("p c b l -> p (c b l)") for w in k]
            d = vs[:, slot, int(name[3]), :, :, :, :].rearrange("p c h s f -> p (c h) s f")
            return [d[:, :, s, :] for s in range(2)]

        def work_psum(name):
            ps = work.psum(name)
            return ps if name[0] != "v" else ps.rearrange("p (c f) -> p c f", f=HD1)

        def rounds(eng, body, tail):
            body(0, first=True, last=False)
            with eng.Fori(1, R1 - 1) as i:
                body(i, first=False, last=False)
            body(R1 - 1, first=False, last=True)
            tail(R1)

        block = ctx.enter_context(nc.Block())

        @block.sync
        def _(sp):
            for e in events:
                sp.nop().then_inc(e.sem, e.per)

            def load_u(i):
                sp.dma_start(ub[:, :, :], v["ctx_in"].rearrange("b p d -> p b d")[:, bass.ds(i * NB, NB), :])\
                    .then_inc(u_in.sem, 16)

            load_u(0)
            for h in range(2):
                sp.dma_start(wi1_raw[:, h * HALF:(h + 1) * HALF],
                             v["wi_in"][P:2 * P, h * HALF:(h + 1) * HALF]).then_inc(wi_in, 16)
                sp.wait_ge(wi_in, 16 * (h + 1))
            for half in range(2):
                sp.dma_start(wo_raw[half * HD1:(half + 1) * HD1, :, :], v["wo_in"].rearrange(
                    "(h r) o -> r h o", r=HD1)).then_inc(wo_in, 16)
            with sp.Fori(1, R1) as i:
                sp.wait_ge(*zu_lo.at(i - 1, 1))
                load_u(i)

        @block.gpsimd
        def _(pool):
            def norm(i, n):
                pool.wait_ge(*z_inv_done.at(i, n))
                e = prob[:, n % RE, :].rearrange("p (t c) -> p t c", t=2)
                pool.tensor_tensor(e, e, z_inv[:, n % RE, :].unsqueeze(2).broadcast_to([P, 2, D]), ALU.mult)\
                    .then_inc(probs_done.sem, 1)

            def inverse_std(i, name):
                pool.wait_ge(*work.out(name, i))
                pool.tensor_tensor(rstd[:, :], var_eps[:, :], half_neg[:, 0:4], ALU.pow).then_inc(rstd_done.sem, 1)

            def body(i, first, last):
                for t in range(UNITS):
                    if t >= L_E or not first:
                        norm(i, t - L_E)
                    if t == T_VAR + 1:
                        inverse_std(i, "var")

            def tail(i):
                for t in range(L_E):
                    norm(i, t - L_E)
                inverse_std(i, "k0")

            pool.memset(q[0][:, :, :, :, :, :].bitcast(F32), 0.0).then_inc(zeroed, 1)
            pool.memset(q[1][:, :, :, :, :, :].bitcast(F32), 0.0).then_inc(zeroed, 1)
            for g, (hi, lo, raw) in enumerate(wo_parts):
                pool.wait_ge(wo_hi_made, g + 1)
                pool.tensor_tensor(lo, raw, hi.bitcast(F32), ALU.subtract).then_inc(wo_lo_made, 1)
            rounds(pool, body, tail)

        @block.tensor
        def _(pe):
            mm = nc.tensor.matmul

            def project(i, name):
                ps = work.psum(name)
                pe.wait_ge(*work.free(name, i))
                pe.wait_ge(*zu_lo.at(i, 1))
                for c in range(2):
                    o = ps[:, c * D:(c + 1) * D]
                    for s, w in enumerate((wz, wi)):
                        for wp, xp in ((0, 0), (0, 1), (1, 0)):
                            flags = {"start": (s, wp, xp) == (0, 0, 0), "stop": (s, wp, xp) == (1, 1, 0)}
                            if name[0] in "qk":
                                at = "qk".index(name[0]) * NQ + int(name[1]) * P
                                last = mm(o, w[wp][c][:, at:at + P],
                                          zu[xp][:, s, c, :, :].rearrange("p b l -> p (b l)"), **flags)
                            else:
                                at = 2 * NQ + int(name[1]) * D
                                last = mm(o, zu[xp][:, s, c, int(name[3]), :], w[wp][c][:, at:at + D], **flags)
                last.then_inc(work.fills(name), 1)

            def scores(i, n):
                pair, h, b = unit(n)
                if n % 4 == 0:
                    pe.wait_ge(*work.out(f"q{pair}", i))
                    pe.wait_ge(*work.out(f"k{pair}", i))
                pe.wait_ge(*exp_done.at(i, n - 2))
                for qt in range(2):
                    for qp, kp in ((0, 0), (0, 1), (1, 0)):
                        last = mm(score_bank[n % 2][:, qt * D:(qt + 1) * D], q[qp][:, pair % 2, h, qt, b, :],
                                  k[kp][:, pair % 2, :, b, :], start=(qp, kp) == (0, 0), stop=(qp, kp) == (1, 0))
                last.then_inc(scores_done.sem, 1)

            def turn(i, n):
                pe.wait_ge(*probs_done.at(i, n))
                pe.wait_ge(*pT_lo.at(i, n - 2))
                for qt in range(2):
                    for kt in range(2):
                        last = nc.tensor.transpose(turn_bank[n % 2][:, kt * D + qt * P:kt * D + (qt + 1) * P],
                                                   prob[:, n % RE, qt * D + kt * P:qt * D + (kt + 1) * P],
                                                   ident[:, :])
                last.then_inc(turned.sem, 1)

            def times_v(i, n):
                pair, h, b = unit(n)
                if n % 8 == 0:
                    pe.wait_ge(*work.out(f"v{pair // 2}b0", i))
                    pe.wait_ge(*work.out(f"v{pair // 2}b1", i))
                pe.wait_ge(*pT_lo.at(i, n))
                pe.wait_ge(*aT_lo.at(i, n - 1))
                for kt in range(2):
                    w = vs[:, pair // 2 % 2, b, kt, 2 * (pair % 2) + h, :, :].rearrange("p s f -> p (s f)")
                    for pp in range(2):
                        last = mm(pv_bank[:, 0:D], w, pT[pp][:, n % RT, kt * D:(kt + 1) * D],
                                  start=(kt, pp) == (0, 0), stop=(kt, pp) == (1, 1))
                last.then_inc(pv_done.sem, 1)

            def times_wo(i, n):
                pair, h, b = unit(n)
                head = 2 * pair + h
                pe.wait_ge(*aT_lo.at(i, n))
                if head == 0:
                    pe.wait_ge(*y_done.at(i))
                for wp, ap in ((0, 0), (0, 1), (1, 0)):
                    last = mm(wo_bank[b], wo[wp][:, head, :], aT[ap][:, n % RT, :],
                              start=(head, b, wp, ap) == (0, 0, 0, 0),
                              stop=head == H1 - 1 and (wp, ap) == (1, 0), skip_group_check=True)
                last.then_inc(wo_done.sem, 1)

            def mean(i, name):
                pe.wait_ge(*work.free(name, i))
                pe.wait_ge(*y_done.at(i))
                mm(work.psum(name), mean_w[:, :], y[:, :, :].rearrange("p b d -> p (b d)"),
                   start=True, stop=True).then_inc(work.fills(name), 1)

            def variance(i, name):
                pe.wait_ge(*work.free(name, i))
                pe.wait_ge(*squared.at(i))
                for j in range(4):
                    last = mm(work.psum(name)[:, j:j + 1], ysq[:, j // 2, j % 2 * P:(j % 2 + 1) * P],
                              mean_w[:, 0:1], start=True, stop=True)
                last.then_inc(work.fills(name), 1)

            def spread(i, name, b):
                pe.wait_ge(*work.free(name, i))
                pe.wait_ge(*diagonal.at(i))
                for j in range(2):
                    last = mm(work.psum(name)[:, j * P:(j + 1) * P], mean_w[:, :],
                              diag[:, 2 * b + j, :], start=True, stop=True)
                last.then_inc(work.fills(name), 1)

            def body(i, first, last):
                for t in range(UNITS):
                    scores(i, t)
                    if t >= L_V or not first:
                        times_v(i, t - L_V)
                    if first and t == L_O:
                        pe.wait_ge(wo_lo_made, len(wo_parts))
                    if t >= L_O or not first:
                        times_wo(i, t - L_O)
                    name, ahead = work_at(t)
                    if name and not (last and ahead):
                        project(i + ahead, name)
                    if t == T_MEAN:
                        mean(i, "mean")
                    if t in (T_INV, T_INV + 1):
                        spread(i, f"inv{t - T_INV}", t - T_INV)
                    if t >= L_T or not first:
                        turn(i, t - L_T)
                    if t == T_VAR:
                        variance(i, "var")

            def tail(i):
                for t in range(L_O):
                    if t < L_V:
                        times_v(i, t - L_V)
                    times_wo(i, t - L_O)
                    if t < L_T:
                        turn(i, t - L_T)
                mean(i, "q0")
                variance(i, "k0")
                spread(i, "v0b0", 0)
                spread(i, "v0b1", 1)

            pe.wait_ge(zeroed, 2)
            for name in names[:4]:
                pe.wait_ge(lo_made, len(parts) // 2 if name in ("q0", "k0") else len(parts))
                project(0, name)
            rounds(pe, body, tail)

        @block.scalar
        def _(act):
            def exponentials(i, n):
                act.wait_ge(*max_done.at(i, n))
                act.wait_ge(*turned.at(i, n - RE))
                for qt in range(2):
                    last = nc.scalar.activation(prob[:, n % RE, qt * D:(qt + 1) * D],
                                                score_bank[n % 2][:, qt * D:(qt + 1) * D], ACT.Exp,
                                                bias=neg_max[:, n % RE, qt:qt + 1],
                                                accum_out=z_sum[:, n % RE, qt:qt + 1])
                last.then_inc(exp_done.sem, 1)

            def round_probs(i, n):
                act.wait_ge(*turned.at(i, n))
                act.wait_ge(*pv_done.at(i, n - RT))
                nc.scalar.copy(pT[0][:, n % RT, :], turn_bank[n % 2]).then_inc(pT_hi.sem, 1)

            def round_heads(i, n):
                act.wait_ge(*pv_done.at(i, n))
                act.wait_ge(*wo_done.at(i, n - RT))
                nc.scalar.copy(aT[0][:, n % RT, :], pv_bank[:, 0:D]).then_inc(aT_hi.sem, 1)

            def round_work(i, name):
                act.wait_ge(*work.full(name, i))
                tile, ps = tile_of(name), work_psum(name)
                if name[0] == "q":
                    for h in range(2):
                        at = slice(h * HD1, (h + 1) * HD1)
                        last = nc.scalar.activation(tile[h][0], ps[at, :], ACT.Identity,
                                                    bias=col("rwb", int(name[1]))[at, :])
                elif name[0] == "k":
                    last = nc.scalar.activation(tile[0], ps, ACT.Identity, scale=SCALE)
                else:
                    last = nc.scalar.copy(tile[0], ps)
                last.then_inc(work_hi.sem, 1)

            def round_z(i):
                if not isinstance(i, int) or i > 0:
                    act.wait_ge(*work.full("k7", i - 1))
                nc.scalar.copy(zu[0][:, 0, :, :, :], xs[:, bass.ds(i * NB, NB), :].rearrange(
                    "p b (c l) -> p c b l", c=2)).then_inc(zu_hi.sem, 1)

            def round_u(i):
                act.wait_ge(*u_in.at(i))
                nc.scalar.copy(zu[0][:, 1, :, :, :], ub[:, :, :].rearrange("p b (c l) -> p c b l", c=2))\
                    .then_inc(zu_hi.sem, 1)

            def body(i, first, last):
                for t in range(UNITS):
                    if t >= L_E or not first:
                        exponentials(i, t - L_E)
                    if t >= L_P or not first:
                        round_probs(i, t - L_P)
                    name, r = work_to_round(i, t, last)
                    if name and (t >= L_W or not first):
                        round_work(r, name)
                    if t >= L_V or not first:
                        round_heads(i, t - L_V)
                    if t == T_ZU and not last:
                        round_z(i + 1)
                    if t == T_ZU + 1 and not last:
                        round_u(i + 1)

            def tail(i):
                for t in range(L_V):
                    if t < L_E:
                        exponentials(i, t - L_E)
                    if t < L_P:
                        round_probs(i, t - L_P)
                    round_heads(i, t - L_V)

            round_z(0)
            act.wait_ge(l1_weights_in, 48)
            for n, (hi, lo, raw) in enumerate(parts):
                if n % 4 == 3:
                    act.wait_ge(wi_in, 16 * (n // 4 + 1))
                nc.scalar.copy(hi, raw).then_inc(hi_made, 1)
                if n == 3:
                    round_u(0)
            act.wait_ge(zeroed, 2)
            for name in names[:4]:
                round_work(0, name)
                if name == "k0":
                    act.wait_ge(wo_in, 32)
                    for hi, lo, raw in wo_parts:
                        nc.scalar.copy(hi, raw).then_inc(wo_hi_made, 1)
            rounds(act, body, tail)

        @block.vector
        def _(dve):
            def maxima(i, n):
                dve.wait_ge(*scores_done.at(i, n))
                dve.wait_ge(*exp_done.at(i, n - RE))
                nc.vector.tensor_reduce(neg_max[:, n % RE, :], score_bank[n % 2].rearrange("p (t c) -> p t c", t=2),
                                        AX.X, ALU.max, negate=True).then_inc(max_done.sem, 1)

            def inverse_sums(i, n):
                dve.wait_ge(*exp_done.at(i, n))
                dve.wait_ge(*probs_done.at(i, n - RE))
                nc.vector.reciprocal(z_inv[:, n % RE, :], z_sum[:, n % RE, :]).then_inc(z_inv_done.sem, 1)

            def rest_probs(i, n):
                dve.wait_ge(*pT_hi.at(i, n))
                nc.vector.tensor_tensor(pT[1][:, n % RT, :], turn_bank[n % 2], pT[0][:, n % RT, :].bitcast(F32),
                                        ALU.subtract).then_inc(pT_lo.sem, 1)

            def rest_heads(i, n):
                dve.wait_ge(*aT_hi.at(i, n))
                nc.vector.tensor_tensor(aT[1][:, n % RT, :], pv_bank[:, 0:D], aT[0][:, n % RT, :].bitcast(F32),
                                        ALU.subtract).then_inc(aT_lo.sem, 1)

            def rest_work(i, name):
                dve.wait_ge(*work_hi.at(i, made.index(name)))
                tile, ps = tile_of(name), work_psum(name)
                if name[0] == "q":
                    for h in range(2):
                        at = slice(h * HD1, (h + 1) * HD1)
                        hi, lo = tile[h]
                        last = nc.vector.scalar_tensor_tensor(
                            out=lo, in0=ps[at, :], scalar=col("rwb", int(name[1]))[at, :], in1=hi.bitcast(F32),
                            op0=ALU.add, op1=ALU.subtract)
                elif name[0] == "k":
                    last = nc.vector.scalar_tensor_tensor(out=tile[1], in0=ps, scalar=SCALE,
                                                          in1=tile[0].bitcast(F32), op0=ALU.mult, op1=ALU.subtract)
                else:
                    last = nc.vector.tensor_tensor(tile[1], ps, tile[0].bitcast(F32), ALU.subtract)
                last.then_inc(work.reads(name), 1)

            def rest_z(i):
                dve.wait_ge(*zu_hi.at(i, 0))
                z = xs[:, bass.ds(i * NB, NB), :].rearrange("p b (c l) -> p c b l", c=2)
                nc.vector.tensor_tensor(zu[1][:, 0, :, :, :], z, zu[0][:, 0, :, :, :].bitcast(F32), ALU.subtract)\
                    .then_inc(zu_lo.sem, 1)

            def rest_u(i):
                dve.wait_ge(*zu_hi.at(i, 1))
                nc.vector.tensor_tensor(zu[1][:, 1, :, :, :], ub[:, :, :].rearrange("p b (c l) -> p c b l", c=2),
                                        zu[0][:, 1, :, :, :].bitcast(F32), ALU.subtract).then_inc(zu_lo.sem, 1)

            def residual(i):
                dve.wait_ge(*wo_done.at(i, -1))
                for b in range(NB):
                    last = nc.vector.scalar_tensor_tensor(
                        out=y[:, b, :], in0=wo_bank[b], scalar=col("bo"),
                        in1=xs[:, bass.ds((i - 1) * NB + b, 1), :].rearrange("p a d -> p (a d)"),
                        op0=ALU.add, op1=ALU.add)
                last.then_inc(y_done.sem, 1)

            def centre(i, name):
                dve.wait_ge(*work.full(name, i))
                yy = y[:, :, :].rearrange("p b d -> p (b d)")
                nc.vector.tensor_tensor(yy, yy, work.psum(name), ALU.subtract)\
                    .then_inc(work.reads(name), 1)
                dve.wait_ge(*work.out(name, i))
                nc.vector.tensor_tensor(ysq[:, :, :], y[:, :, :], y[:, :, :], ALU.mult).then_inc(squared.sem, 1)

            def read_variance(i, name):
                dve.wait_ge(*work.full(name, i))
                nc.vector.tensor_scalar(var_eps[:, :], work.psum(name)[:, 0:4], EPS, None, ALU.add)\
                    .then_inc(work.reads(name), 1)

            def make_diagonal(i):
                dve.wait_ge(*rstd_done.at(i))
                for j in range(4):
                    last = nc.vector.tensor_scalar(diag[:, j, :], ident[:, :], rstd[:, j:j + 1], float(P),
                                                   ALU.mult, ALU.mult)
                last.then_inc(diagonal.sem, 1)

            def output(i, name, b, first=False):
                dve.wait_ge(*work.full(name, i))
                ps = work.psum(name)[:, 0:D]
                to = y[:, b, :] if first else xs[:, bass.ds((i - 1) * NB + b, 1), :].rearrange("p a d -> p (a d)")
                nc.vector.tensor_tensor(to, y[:, b, :], ps, ALU.mult).then_inc(work.reads(name), 1)

            def body(i, first, last):
                for t in range(UNITS):
                    if t == T_Y:
                        if first:
                            nc.vector.memset(y[:, :, :], 0.0).then_inc(y_done.sem, 1)
                        else:
                            residual(i)
                    maxima(i, t)
                    if t >= L_E or not first:
                        inverse_sums(i, t - L_E)
                    if t >= L_P or not first:
                        rest_probs(i, t - L_P)
                    name, r = work_to_round(i, t, last)
                    if name and (t >= L_W or not first):
                        rest_work(r, name)
                    if t >= L_V or not first:
                        rest_heads(i, t - L_V)
                    if t == T_MEAN:
                        centre(i, "mean")
                    if t == T_VAR:
                        read_variance(i, "var")
                    if t == T_VAR + 2:
                        make_diagonal(i)
                    if t in (T_INV, T_INV + 1):
                        output(i, f"inv{t - T_INV}", t - T_INV, first)
                    if t == T_ZU and not last:
                        rest_z(i + 1)
                    if t == T_ZU + 1 and not last:
                        rest_u(i + 1)

            def tail(i):
                for t in range(L_V):
                    if t < L_E:
                        inverse_sums(i, t - L_E)
                    if t < L_P:
                        rest_probs(i, t - L_P)
                    rest_heads(i, t - L_V)
                residual(i)
                centre(i, "q0")
                read_variance(i, "k0")
                make_diagonal(i)
                output(i, "v0b0", 0)
                output(i, "v0b1", 1)

            rest_z(0)
            for n, (hi, lo, raw) in enumerate(parts):
                dve.wait_ge(hi_made, n + 1)
                nc.vector.tensor_tensor(lo, raw, hi.bitcast(F32), ALU.subtract).then_inc(lo_made, 1)
                if n == 3:
                    rest_u(0)
            dve.wait_ge(zeroed, 2)
            for name in names[:4]:
                rest_work(0, name)
            rounds(dve, body, tail)


def layers23(nc, v):
    (psum, xs, ident, half_neg, col) = (v[n] for n in ("psum", "xs", "ident", "half_neg", "col"))
    DK = 16
    CI = 64
    RE, RT = 4, 2
    with ExitStack() as ctx:
        def sb(name, shape, dt=F32):
            return ctx.enter_context(nc.sbuf_tensor(name, shape, dt))

        def sem(name):
            return ctx.enter_context(nc.semaphore(name))

        events = []

        def event(name, per, unit=1):
            e = Event(ctx, nc, "l2_" + name, per, unit)
            events.append(e)
            return e

        wqk = sb("wqk2", [P, 2 * DK])
        wvpg = sb("wvpg", [P, D])
        wtheta = sb("wtheta", [P, CI])
        ww = sb("ww", [CI, P])
        bvpg = sb("bvpg", [P, D])
        bn = sb("bn", [P, 4])
        cg = sb("cg", [P, G, D])
        xg = sb("l2_xg", [P, G, D])
        q2 = sb("q2", [P, G, D])
        k2 = sb("k2", [P, G, D])
        vpg = sb("vpg", [P, G, 2, D])
        gT = sb("gT", [CI, G, P])
        hw = sb("hw", [CI, G, P])
        theta = sb("theta", [CI, G, D])
        prob = sb("l2_prob", [P, RE, BANK])
        pT = sb("l2_pT", [P, RT, BANK])
        x2 = sb("x2", [P, G, D])
        fin = sb("fin", [P, G, D])
        neg_max = sb("l2_neg_max", [P, RE, 2])
        z_sum = sb("l2_z_sum", [P, RE, 2])
        z_inv = sb("l2_z_inv", [P, RE, 2])

        score_bank = [psum[:, j, :] for j in range(2)]
        turn_bank = [psum[:, 2 + j, :] for j in range(2)]
        pv_bank = [psum[:, 4 + j, 0:D] for j in range(2)]

        names = ["q0", "q1", "k0", "k1"] + [f"w{b}" for b in range(G)] + ["g", "h", "t0", "t1", "y0", "y1"]
        work = Banks(ctx, nc, "l2_work", names, [psum[:, 6 + j, :] for j in range(2)])
        events += work.full_ev + work.out_ev
        ctx_in = event("ctx_in", 1, 16)
        x_copied = event("x_copied", 1)
        scores_done = event("scores_done", G)
        max_done = event("max_done", G)
        exp_done = event("exp_done", G)
        z_inv_done = event("z_inv_done", G)
        probs_done = event("probs_done", G)
        turned = event("turned", G)
        probsT_done = event("probsT_done", G)
        pv_done = event("pv_done", G)
        x2_done = event("x2_done", G)
        final_done = event("final_done", 2)
        out_written = event("out_written", 1, 16)
        weights_in = sem("l2_weights_in")
        zeroed = sem("l2_zeroed")
        bn_step = sem("bn_step")

        def two(t, m):
            return t[:, 2 * m:2 * m + 2, :].rearrange("p b d -> p (b d)")

        block = ctx.enter_context(nc.Block())

        @block.sync
        def _(sp):
            for e in events:
                sp.nop().then_inc(e.sem, e.per)
            sp.dma_start(wqk[:, :], v["wqk2_in"]).then_inc(weights_in, 16)
            sp.dma_start(wvpg[:, :], v["wvpg_in"]).then_inc(weights_in, 16)
            sp.dma_start(wtheta[:, :], v["theta_in"]).then_inc(weights_in, 16)
            sp.dma_start(ww[:, :], v["ww_in"]).then_inc(weights_in, 16)
            sp.dma_start(bvpg[:, :], v["rows_in"][ROWS["bvpg"]:ROWS["bvpg"] + D].partition_broadcast(P))\
                .then_inc(weights_in, 16)

            def load(i):
                sp.dma_start(cg[:, :, :], v["ctx_in"].rearrange("b p d -> p b d")[:, bass.ds(i * G, G), :])\
                    .then_inc(ctx_in.sem, 16)

            def store(i):
                sp.wait_ge(*final_done.at(i, 1))
                sp.dma_start(v["out"].rearrange("b p d -> p b d")[:, bass.ds(i * G, G), :], fin[:, :, :])\
                    .then_inc(out_written.sem, 16)

            load(0)
            with sp.Fori(1, ROUNDS) as i:
                sp.wait_ge(*work.full("w3", i - 1))
                load(i)
                store(i - 1)
            store(ROUNDS - 1)
            sp.wait_ge(*out_written.at(ROUNDS - 1))

        @block.gpsimd
        def _(pool):
            pool.memset(q2[:, :, :], 0.0).then_inc(zeroed, 1)
            pool.memset(k2[:, :, :], 0.0).then_inc(zeroed, 1)
            pool.memset(gT[:, :, :], 0.0).then_inc(zeroed, 1)
            pool.tensor_scalar(bn[:, 0:1], col("bn_var"), EPS, None, ALU.add).then_inc(bn_step, 1)
            pool.tensor_tensor(bn[:, 3:4], col("w_b"), col("bn_mean"), ALU.subtract).then_inc(bn_step, 1)
            pool.wait_ge(bn_step, 2)
            pool.tensor_tensor(bn[:, 1:2], bn[:, 0:1], half_neg[:, 0:1], ALU.pow).then_inc(bn_step, 1)
            pool.wait_ge(bn_step, 3)
            pool.tensor_tensor(bn[:, 2:3], bn[:, 1:2], col("gamma"), ALU.mult).then_inc(bn_step, 1)
            pool.wait_ge(bn_step, 4)
            pool.tensor_tensor(bn[:, 3:4], bn[:, 3:4], bn[:, 2:3], ALU.mult).then_inc(bn_step, 1)
            pool.wait_ge(bn_step, 5)
            pool.tensor_tensor(bn[:, 3:4], bn[:, 3:4], col("beta"), ALU.add).then_inc(bn_step, 1)

        @block.tensor
        def _(pe):
            mm = nc.tensor.matmul

            def bank(name, i):
                pe.wait_ge(*work.free(name, i))
                return work.psum(name)

            pe.wait_ge(weights_in, 80)
            pe.wait_ge(zeroed, 3)
            with pe.Fori(0, ROUNDS) as i:
                pe.wait_ge(*x_copied.at(i))
                for m in range(2):
                    mm(bank(f"q{m}", i)[0:DK, :], wqk[:, 0:DK], two(xg, m), start=True, stop=True)\
                        .then_inc(work.fills(f"q{m}"), 1)
                pe.wait_ge(*ctx_in.at(i))
                for m in range(2):
                    mm(bank(f"k{m}", i)[0:DK, :], wqk[:, DK:2 * DK], two(cg, m), start=True, stop=True)\
                        .then_inc(work.fills(f"k{m}"), 1)
                for b in range(G):
                    ps = bank(f"w{b}", i)
                    for j in range(2):
                        last = mm(ps[:, j * D:(j + 1) * D], cg[:, b, j * P:(j + 1) * P], wvpg[:, :],
                                  start=True, stop=True)
                    last.then_inc(work.fills(f"w{b}"), 1)
                pe.wait_ge(*work.out("k0", i))
                pe.wait_ge(*work.out("k1", i))

                def scores(b):
                    pe.wait_ge(*exp_done.at(i, b - 2))
                    for qt in range(2):
                        last = mm(score_bank[b % 2][:, qt * D:(qt + 1) * D], q2[:, b, qt * P:(qt + 1) * P],
                                  k2[:, b, :], start=True, stop=True)
                    last.then_inc(scores_done.sem, 1)

                def turn(b):
                    pe.wait_ge(*probs_done.at(i, b))
                    pe.wait_ge(*probsT_done.at(i, b - 2))
                    for qt in range(2):
                        for kt in range(2):
                            last = nc.tensor.transpose(turn_bank[b % 2][:, kt * D + qt * P:kt * D + (qt + 1) * P],
                                                       prob[:, b % RE, qt * D + kt * P:qt * D + (kt + 1) * P],
                                                       ident[:, :])
                    last.then_inc(turned.sem, 1)

                def times_v(b):
                    pe.wait_ge(*probsT_done.at(i, b))
                    pe.wait_ge(*x2_done.at(i, b - 2))
                    for kt in range(2):
                        last = mm(pv_bank[b % 2], vpg[:, b, kt, 0:P], pT[:, b % RT, kt * D:(kt + 1) * D],
                                  start=kt == 0, stop=kt == 1)
                    last.then_inc(pv_done.sem, 1)

                for b in range(3):
                    scores(b)
                pe.wait_ge(*work.out("w2", i))
                pe.wait_ge(*work.out("w3", i))
                ps = bank("g", i)
                for b in range(G):
                    for j in range(2):
                        last = mm(ps[0:CI, b * CI:(b + 1) * CI], vpg[:, b, j, P + CI:D], vpg[:, b, j, P:P + CI],
                                  start=j == 0, stop=j == 1)
                last.then_inc(work.fills("g"), 1)
                turn(0)
                scores(3)
                turn(1)
                times_v(0)
                pe.wait_ge(*work.out("g", i))
                ps = bank("h", i)
                for b in range(G):
                    last = mm(ps[:, b * P:(b + 1) * P], gT[:, b, :], ww[:, :], start=True, stop=True)
                last.then_inc(work.fills("h"), 1)
                turn(2)
                times_v(1)
                turn(3)
                times_v(2)
                pe.wait_ge(*x2_done.at(i, 1))
                mm(bank("t0", i)[0:CI, :], wtheta[:, :], two(x2, 0), start=True, stop=True)\
                    .then_inc(work.fills("t0"), 1)
                times_v(3)
                pe.wait_ge(*x2_done.at(i, 3))
                mm(bank("t1", i)[0:CI, :], wtheta[:, :], two(x2, 1), start=True, stop=True)\
                    .then_inc(work.fills("t1"), 1)
                pe.wait_ge(*work.out("h", i))
                for m in range(2):
                    pe.wait_ge(*work.out(f"t{m}", i))
                    ps = bank(f"y{m}", i)
                    for b in (2 * m, 2 * m + 1):
                        last = mm(ps[:, b % 2 * D:(b % 2 + 1) * D], hw[:, b, :], theta[:, b, :],
                                  start=True, stop=True)
                    last.then_inc(work.fills(f"y{m}"), 1)

        @block.scalar
        def _(act):
            act.wait_ge(zeroed, 3)
            with act.Fori(0, ROUNDS) as i:
                act.wait_ge(*x2_done.at(i - 1, G - 1))
                nc.scalar.copy(xg[:, :, :], xs[:, bass.ds(i * G, G), :]).then_inc(x_copied.sem, 1)
                for name, t, bias in (("q", q2, "bq2"), ("k", k2, "bk2")):
                    for m in range(2):
                        act.wait_ge(*work.full(f"{name}{m}", i))
                        nc.scalar.activation(two(t, m)[0:DK, :], work.psum(f"{name}{m}")[0:DK, :],
                                             ACT.Identity, bias=col(bias, p=DK)).then_inc(work.reads(f"{name}{m}"), 1)

                def exponentials(b):
                    act.wait_ge(*max_done.at(i, b))
                    act.wait_ge(*turned.at(i, b - RE))
                    for qt in range(2):
                        last = nc.scalar.activation(prob[:, b % RE, qt * D:(qt + 1) * D],
                                                    score_bank[b % 2][:, qt * D:(qt + 1) * D], ACT.Exp,
                                                    bias=neg_max[:, b % RE, qt:qt + 1],
                                                    accum_out=z_sum[:, b % RE, qt:qt + 1])
                    last.then_inc(exp_done.sem, 1)

                def turned_out(b):
                    act.wait_ge(*turned.at(i, b))
                    act.wait_ge(*pv_done.at(i, b - RT))
                    nc.scalar.copy(pT[:, b % RT, :], turn_bank[b % 2]).then_inc(probsT_done.sem, 1)

                exponentials(0)
                exponentials(1)
                exponentials(2)
                act.wait_ge(*work.full("g", i))
                nc.scalar.activation(gT[:, :, 0:CI], work.psum("g")[0:CI, 0:G * CI].rearrange(
                    "p (b c) -> p b c", b=G), ACT.Identity, scale=1.0 / D).then_inc(work.reads("g"), 1)
                turned_out(0)
                exponentials(3)
                turned_out(1)
                act.wait_ge(*work.full("h", i))
                nc.scalar.copy(hw[:, :, :].rearrange("p b c -> p (b c)"), work.psum("h")[0:CI, :])\
                    .then_inc(work.reads("h"), 1)
                turned_out(2)
                turned_out(3)
                for m in range(2):
                    act.wait_ge(*work.full(f"t{m}", i))
                    nc.scalar.activation(two(theta, m), work.psum(f"t{m}")[0:CI, :], ACT.Identity,
                                         bias=col("theta_b", p=CI)).then_inc(work.reads(f"t{m}"), 1)

        @block.vector
        def _(dve):
            dve.wait_ge(weights_in, 80)
            dve.wait_ge(bn_step, 6)
            with dve.Fori(0, ROUNDS) as i:
                def maxima(b):
                    dve.wait_ge(*scores_done.at(i, b))
                    dve.wait_ge(*exp_done.at(i, b - RE))
                    nc.vector.tensor_reduce(neg_max[:, b % RE, :], score_bank[b % 2].rearrange(
                        "p (t c) -> p t c", t=2), AX.X, ALU.max, negate=True).then_inc(max_done.sem, 1)

                def values(b):
                    dve.wait_ge(*work.full(f"w{b}", i))
                    nc.vector.tensor_tensor(vpg[:, b, :, :], work.psum(f"w{b}").rearrange(
                        "p (j n) -> p j n", j=2), bvpg[:, :].unsqueeze(1).broadcast_to([P, 2, D]), ALU.add)\
                        .then_inc(work.reads(f"w{b}"), 1)

                def norm(b):
                    dve.wait_ge(*exp_done.at(i, b))
                    nc.vector.reciprocal(z_inv[:, b % RE, :], z_sum[:, b % RE, :]).then_inc(z_inv_done.sem, 1)
                    dve.wait_ge(*z_inv_done.at(i, b))
                    e = prob[:, b % RE, :].rearrange("p (t c) -> p t c", t=2)
                    nc.vector.tensor_tensor(e, e, z_inv[:, b % RE, :].unsqueeze(2).broadcast_to([P, 2, D]),
                                            ALU.mult).then_inc(probs_done.sem, 1)

                def add_x(b):
                    dve.wait_ge(*pv_done.at(i, b))
                    nc.vector.tensor_tensor(x2[:, b, :], pv_bank[b % 2], xg[:, b, :], ALU.add)\
                        .then_inc(x2_done.sem, 1)

                for b in range(G):
                    values(b)
                maxima(0)
                maxima(1)
                norm(0)
                maxima(2)
                norm(1)
                norm(2)
                maxima(3)
                norm(3)
                for b in range(G):
                    add_x(b)
                for m in range(2):
                    dve.wait_ge(*work.full(f"y{m}", i))
                    if m == 0:
                        dve.wait_ge(*out_written.at(i - 1))
                    nc.vector.tensor_scalar(two(fin, m), work.psum(f"y{m}"), bn[:, 2:3], bn[:, 3:4],
                                            ALU.mult, ALU.add).then_inc(work.reads(f"y{m}"), 1)
                    dve.wait_ge(*work.out(f"y{m}", i))
                    nc.vector.tensor_tensor(two(fin, m), two(fin, m), two(x2, m), ALU.add)\
                        .then_inc(final_done.sem, 1)


def layout(inputs):
    a = {n: np.asarray(x) for n, x in inputs.items()}
    L0, L1, L2, L3 = ((lambda n, p=p: a[p + n]) for p in ("L0_xattn_", "L1_xattn_", "L2_xattn_", "L3_xattn_"))
    flat = {"ln_s": [L0("ln1_s"), L0("ln2_s"), L0("ln3_s")], "ln_b": [L0("ln1_b"), L0("ln2_b"), L0("ln3_b")],
            "bq0": [L0("b_qkv")[0:D]], "bk0": [L0("b_qkv")[D:2 * D]], "bcq": [L0("b_q")], "bck": [L0("b_kv")[0:D]],
            "b1": [L0("b1")], "bo": [L1("bo")], "rwb": [L1("r_w_bias").reshape(-1)], "bq2": [L2("bq")],
            "bk2": [L2("bk")], "theta_b": [L3("theta_b")], "w_b": [L3("w_b")], "gamma": [L3("bn_gamma")],
            "beta": [L3("bn_beta")], "bn_mean": [L3("bn_mean")], "bn_var": [L3("bn_var")]}
    cols = np.zeros((P, NCOLS), np.float32)
    for name, (at, n) in COLS.items():
        vec = np.concatenate(flat[name])
        if vec.size < P:
            vec = np.concatenate([vec, np.zeros(P - vec.size, np.float32)])
        cols[:, at:at + n] = vec.reshape(n, P).T
    rows = np.concatenate([L0("b_qkv")[2 * D:], L0("b_ao"), L0("b_kv")[D:], L0("b_co"), L0("b2"),
                           L2("bv"), L3("phi_b"), L3("g_b")])
    arrays = {
        "x": a["x"], "ctx_in": a["ctx_2048"], "ctxT": a["ctx_2048"].reshape(B * P, D).T,
        "smask": a["mask_1x1xSxS2_fc1"].reshape(P, P), "cmask": a["mask_Bx1xSxS2_ff1"].reshape(B, P, P),
        "cols_in": cols, "rows_in": rows,
        "wqkv_in": L0("w_qkv"), "wao_in": L0("w_ao"), "wq_in": L0("w_q"), "wkv_in": L0("w_kv"),
        "wco_in": L0("w_co"), "w1_in": L0("w1"), "w2_in": L0("w2"),
        "wz_in": np.concatenate([L1("Wqkv0").T, L1("Wqkv1").T]),
        "wi_in": np.concatenate([L1("Winj0").T, L1("Winj1").T]),
        "wo_in": L1("Wo").T,
        "wqk2_in": np.concatenate([L2("Wq").T, L2("Wk").T], axis=1),
        "wvpg_in": np.concatenate([L2("Wv").T, L3("phi_w").T, L3("g_w").T], axis=1),
        "theta_in": L3("theta_w").T, "ww_in": L3("w_w").T,
    }
    return {n: np.ascontiguousarray(x) for n, x in arrays.items()}


def kernel(**inputs):
    import concourse.bacc as bacc
    from concourse.bass_utils import run_bass_kernel_spmd

    arrays = layout(inputs)
    nc = bacc.Bacc("TRN2", target_bir_lowering=False, num_devices=1)
    args = [nc.dram_tensor(n, x.shape, mybir.dt.from_np(x.dtype), kind="ExternalInput").ap()
            for n, x in arrays.items()]
    out = nc.dram_tensor("out", (B, P, D), F32, kind="ExternalOutput").ap()
    program(nc, *args, out)
    result = run_bass_kernel_spmd(nc, [arrays], core_ids=[0])
    return result.results[0]["out"]
```
